# Optimizing a Trainium2 kernel written in Bass

```python
import numpy as np
import jax
import jax.numpy as jnp

def _softmax(x, axis=-1):
    return jax.nn.softmax(x, axis=axis)

def _gelu(x):
    return jax.nn.gelu(x, approximate=True)

def _silu(x):
    return jax.nn.silu(x)

def _sigmoid(x):
    return jax.nn.sigmoid(x)

def _layernorm(x, axis=-1, eps=1e-05):
    m = jnp.mean(x, axis=axis, keepdims=True)
    v = jnp.var(x, axis=axis, keepdims=True)
    return (x - m) / jnp.sqrt(v + eps)

def _scatter_add(tgt, idx, src, axis=0):
    return tgt.at[idx].add(src)

def _segment_sum(src, seg, n):
    return jax.ops.segment_sum(src, seg, n)
kernel_name = 'mk_macaron_d2_jaxref_r8_ebfcce'

def setup_inputs(seed: int=0):
    np.random.seed(seed)
    _w = jnp.asarray

    def _L0_attn_setup():
        import jax, jax.numpy as jnp
        import numpy as np
        import math
        NUM_BUCKETS = 32
        MAX_DISTANCE = 128

        def _relative_position_bucket(relative_position):
            rp = jnp.maximum(-relative_position, 0)
            max_exact = NUM_BUCKETS // 2
            is_small = rp < max_exact
            rp_f = jnp.maximum(rp, 1).astype(jnp.float32)
            large = max_exact + (jnp.log(rp_f / max_exact) / math.log(MAX_DISTANCE / max_exact) * (NUM_BUCKETS - max_exact)).astype(jnp.int32)
            large = jnp.minimum(large, NUM_BUCKETS - 1)
            return jnp.where(is_small, rp, large)

        def _t5_rel_bias(bias_table, T):
            ctx = jnp.arange(T, dtype=jnp.int32)[:, None]
            mem = jnp.arange(T, dtype=jnp.int32)[None, :]
            buckets = _relative_position_bucket(mem - ctx)
            values = bias_table[buckets]
            return jnp.transpose(values, (2, 0, 1))[None]
        key = jax.random.key(seed)
        ks = jax.random.split(key, 6)
        B, T, C, H = (2, 256, 128, 16)
        x = jax.random.normal(ks[0], (B, T, C), dtype=jnp.float32)
        W_attn = jax.random.normal(ks[1], (C, 3 * C), dtype=jnp.float32) * 0.02
        b_attn = jnp.zeros((3 * C,), dtype=jnp.float32)
        W_proj = jax.random.normal(ks[2], (C, C), dtype=jnp.float32) * 0.02
        b_proj = jnp.zeros((C,), dtype=jnp.float32)
        bias_table = jax.random.normal(ks[3], (NUM_BUCKETS, H), dtype=jnp.float32) * 0.02
        return {'x': x, 'W_attn': W_attn, 'b_attn': b_attn, 'W_proj': W_proj, 'b_proj': b_proj, 'bias_table': bias_table}
    _L0_attn_in = _L0_attn_setup()

    def _L0_ffn_setup():
        import jax, jax.numpy as jnp
        import numpy as np
        B, S, IN, OUT, E, R = (8, 512, 128, 128, 8, 8)
        LORA_ALPHA = 16
        SCALING = LORA_ALPHA / R
        key = jax.random.key(seed)
        k = jax.random.split(key, 6)
        x = jax.random.normal(k[0], (B, S, IN), dtype=jnp.float32)
        base_w = jax.random.normal(k[1], (OUT, IN), dtype=jnp.float32) * 0.02
        base_b = jnp.zeros((OUT,), dtype=jnp.float32)
        lora_A = jax.random.normal(k[2], (IN, R), dtype=jnp.float32) * 0.02
        lora_B = jax.random.normal(k[3], (E, R, OUT), dtype=jnp.float32) * 0.02
        router_w = jax.random.normal(k[4], (E, IN), dtype=jnp.float32) * 0.02
        router_b = jnp.zeros((E,), dtype=jnp.float32)
        return {'x': x, 'base_w': base_w, 'base_b': base_b, 'lora_A': lora_A, 'lora_B': lora_B, 'router_w': router_w, 'router_b': router_b}
    _L0_ffn_in = _L0_ffn_setup()

    def _L1_attn_setup():
        import jax, jax.numpy as jnp
        import numpy as np
        B, T, HID = (4, 256, 128)
        H, D, V = (8, 64, 128)
        EPS = 1e-05

        def _rotary(x, T, D):
            inv_freq = 1.0 / 10000.0 ** (jnp.arange(0, D, 2, dtype=jnp.float32) / D)
            t = jnp.arange(T, dtype=jnp.float32)
            freqs = t[:, None] * inv_freq[None, :]
            emb = jnp.concatenate([freqs, freqs], axis=-1)
            cos = jnp.cos(emb)[None, None, :, :]
            sin = jnp.sin(emb)[None, None, :, :]
            x1, x2 = jnp.split(x, 2, axis=-1)
            rot = jnp.concatenate([-x2, x1], axis=-1)
            return x * cos + rot * sin
        key = jax.random.key(seed)
        ks = jax.random.split(key, 7)
        sc = 0.02
        return {'x': jax.random.normal(ks[0], (B, T, HID), dtype=jnp.float32), 'Wq': jax.random.normal(ks[1], (H * D, HID), dtype=jnp.float32) * sc, 'Wk': jax.random.normal(ks[2], (H * D, HID), dtype=jnp.float32) * sc, 'Wv': jax.random.normal(ks[3], (H * V, HID), dtype=jnp.float32) * sc, 'Wg': jax.random.normal(ks[4], (H * V, HID), dtype=jnp.float32) * sc, 'Wo': jax.random.normal(ks[5], (HID, H * V), dtype=jnp.float32) * sc, 'gn_weight': jnp.ones((H * V,), dtype=jnp.float32), 'gn_bias': jnp.zeros((H * V,), dtype=jnp.float32)}
    _L1_attn_in = _L1_attn_setup()

    def _L1_ffn_setup():
        import jax, jax.numpy as jnp
        import numpy as np
        B, S, D = (1, 256, 128)
        E, F = (16, 128)
        NG, TKG, K = (4, 2, 4)
        NSH = 2
        SCALE = 2.5
        STD = 0.02
        EPG = E // NG

        def _route(x_flat, router_w, bias):
            logits = x_flat.astype(jnp.float32) @ router_w.T
            scores = jax.nn.sigmoid(logits)
            s = scores + bias[None, :]
            sg = s.reshape(-1, NG, EPG)
            group_score = jax.lax.top_k(sg, 2)[0].sum(-1)
            gidx = jax.lax.top_k(group_score, TKG)[1]
            gmask = jnp.sum(jax.nn.one_hot(gidx, NG, dtype=jnp.float32), axis=1) > 0
            emask = jnp.repeat(gmask, EPG, axis=1)
            masked = jnp.where(emask, s, -1.0)
            topk_idx = jax.lax.top_k(masked, K)[1]
            tw = jnp.take_along_axis(scores, topk_idx, axis=1)
            tw = tw / (tw.sum(-1, keepdims=True) + 1e-20)
            tw = tw * SCALE
            return (topk_idx, tw)
        key = jax.random.key(seed)
        ks = jax.random.split(key, 8)
        return {'hidden_states': jax.random.normal(ks[0], (B, S, D), jnp.float32), 'router_w': jax.random.normal(ks[1], (E, D), jnp.float32) * STD, 'bias': jnp.zeros((E,), jnp.float32), 'gate_w': jax.random.normal(ks[2], (E, D, F), jnp.float32) * STD, 'up_w': jax.random.normal(ks[3], (E, D, F), jnp.float32) * STD, 'down_w': jax.random.normal(ks[4], (E, F, D), jnp.float32) * STD, 'sh_gate_w': jax.random.normal(ks[5], (D, NSH * F), jnp.float32) * STD, 'sh_up_w': jax.random.normal(ks[6], (D, NSH * F), jnp.float32) * STD, 'sh_down_w': jax.random.normal(ks[7], (NSH * F, D), jnp.float32) * STD}
    _L1_ffn_in = _L1_ffn_setup()
    _d = {'L0_attn_x': _L0_attn_in['x'], 'L0_attn_W_attn': _L0_attn_in['W_attn'], 'L0_attn_b_attn': _L0_attn_in['b_attn'], 'L0_attn_W_proj': _L0_attn_in['W_proj'], 'L0_attn_b_proj': _L0_attn_in['b_proj'], 'L0_attn_bias_table': _L0_attn_in['bias_table'], 'L0_ffn_base_w': _L0_ffn_in['base_w'], 'L0_ffn_base_b': _L0_ffn_in['base_b'], 'L0_ffn_lora_A': _L0_ffn_in['lora_A'], 'L0_ffn_lora_B': _L0_ffn_in['lora_B'], 'L0_ffn_router_w': _L0_ffn_in['router_w'], 'L0_ffn_router_b': _L0_ffn_in['router_b'], 'L1_attn_Wq': _L1_attn_in['Wq'], 'L1_attn_Wk': _L1_attn_in['Wk'], 'L1_attn_Wv': _L1_attn_in['Wv'], 'L1_attn_Wg': _L1_attn_in['Wg'], 'L1_attn_Wo': _L1_attn_in['Wo'], 'L1_attn_gn_weight': _L1_attn_in['gn_weight'], 'L1_attn_gn_bias': _L1_attn_in['gn_bias'], 'L1_ffn_router_w': _L1_ffn_in['router_w'], 'L1_ffn_bias': _L1_ffn_in['bias'], 'L1_ffn_gate_w': _L1_ffn_in['gate_w'], 'L1_ffn_up_w': _L1_ffn_in['up_w'], 'L1_ffn_down_w': _L1_ffn_in['down_w'], 'L1_ffn_sh_gate_w': _L1_ffn_in['sh_gate_w'], 'L1_ffn_sh_up_w': _L1_ffn_in['sh_up_w'], 'L1_ffn_sh_down_w': _L1_ffn_in['sh_down_w']}
    _x0 = _d['L0_attn_x']
    _d['L0_attn_x'] = jax.random.normal(jax.random.fold_in(jax.random.key(seed), 1), (16, 256, 128), dtype=_x0.dtype)
    del _x0
    return _d

def reference(L0_attn_x, L0_attn_W_attn, L0_attn_b_attn, L0_attn_W_proj, L0_attn_b_proj, L0_attn_bias_table, L0_ffn_base_w, L0_ffn_base_b, L0_ffn_lora_A, L0_ffn_lora_B, L0_ffn_router_w, L0_ffn_router_b, L1_attn_Wq, L1_attn_Wk, L1_attn_Wv, L1_attn_Wg, L1_attn_Wo, L1_attn_gn_weight, L1_attn_gn_bias, L1_ffn_router_w, L1_ffn_bias, L1_ffn_gate_w, L1_ffn_up_w, L1_ffn_down_w, L1_ffn_sh_gate_w, L1_ffn_sh_up_w, L1_ffn_sh_down_w):

    def _L0_attn_ref(x, W_attn, b_attn, W_proj, b_proj, bias_table):
        import jax, jax.numpy as jnp
        import numpy as np
        import math
        NUM_BUCKETS = 32
        MAX_DISTANCE = 128

        def _relative_position_bucket(relative_position):
            rp = jnp.maximum(-relative_position, 0)
            max_exact = NUM_BUCKETS // 2
            is_small = rp < max_exact
            rp_f = jnp.maximum(rp, 1).astype(jnp.float32)
            large = max_exact + (jnp.log(rp_f / max_exact) / math.log(MAX_DISTANCE / max_exact) * (NUM_BUCKETS - max_exact)).astype(jnp.int32)
            large = jnp.minimum(large, NUM_BUCKETS - 1)
            return jnp.where(is_small, rp, large)

        def _t5_rel_bias(bias_table, T):
            ctx = jnp.arange(T, dtype=jnp.int32)[:, None]
            mem = jnp.arange(T, dtype=jnp.int32)[None, :]
            buckets = _relative_position_bucket(mem - ctx)
            values = bias_table[buckets]
            return jnp.transpose(values, (2, 0, 1))[None]
        B, T, C = x.shape
        H = bias_table.shape[1]
        D = C // H
        qkv = x @ W_attn + b_attn
        q, k, v = jnp.split(qkv, 3, axis=-1)
        q = q.reshape(B, T, H, D).transpose(0, 2, 1, 3)
        k = k.reshape(B, T, H, D).transpose(0, 2, 1, 3)
        v = v.reshape(B, T, H, D).transpose(0, 2, 1, 3)
        rel_bias = _t5_rel_bias(bias_table, T)
        att = jnp.einsum('bhtd,bhsd->bhts', q, k) * (1.0 / math.sqrt(D))
        att = att + rel_bias
        causal = jnp.tril(jnp.ones((T, T), dtype=bool))
        att = jnp.where(causal, att, -jnp.inf)
        att = jax.nn.softmax(att, axis=-1)
        y = jnp.einsum('bhts,bhsd->bhtd', att, v)
        y = y.transpose(0, 2, 1, 3).reshape(B, T, C)
        return y @ W_proj + b_proj

    def _L0_ffn_ref(x, base_w, base_b, lora_A, lora_B, router_w, router_b):
        import jax, jax.numpy as jnp
        import numpy as np
        B, S, IN, OUT, E, R = (8, 512, 128, 128, 8, 8)
        LORA_ALPHA = 16
        SCALING = LORA_ALPHA / R
        result = jnp.einsum('bsd,od->bso', x, base_w) + base_b
        logits = jnp.einsum('bsd,ed->bse', x, router_w) + router_b
        gating = jax.nn.softmax(logits, axis=-1).astype(jnp.bfloat16)
        mid = jnp.einsum('bsd,dr->bsr', x, lora_A)
        lora_out = jnp.einsum('bsr,erd,bse->bsd', mid, lora_B, gating.astype(jnp.float32))
        return result + lora_out * SCALING

    def _L1_attn_ref(x, Wq, Wk, Wv, Wg, Wo, gn_weight, gn_bias):
        import jax, jax.numpy as jnp
        import numpy as np
        B, T, HID = (4, 256, 128)
        H, D, V = (8, 64, 128)
        EPS = 1e-05

        def _rotary(x, T, D):
            inv_freq = 1.0 / 10000.0 ** (jnp.arange(0, D, 2, dtype=jnp.float32) / D)
            t = jnp.arange(T, dtype=jnp.float32)
            freqs = t[:, None] * inv_freq[None, :]
            emb = jnp.concatenate([freqs, freqs], axis=-1)
            cos = jnp.cos(emb)[None, None, :, :]
            sin = jnp.sin(emb)[None, None, :, :]
            x1, x2 = jnp.split(x, 2, axis=-1)
            rot = jnp.concatenate([-x2, x1], axis=-1)
            return x * cos + rot * sin
        Bx, Tx, _ = x.shape
        q = jnp.einsum('bti,oi->bto', x, Wq).reshape(Bx, Tx, H, D).transpose(0, 2, 1, 3)
        k = jnp.einsum('bti,oi->bto', x, Wk).reshape(Bx, Tx, H, D).transpose(0, 2, 1, 3)
        v = jnp.einsum('bti,oi->bto', x, Wv).reshape(Bx, Tx, H, V).transpose(0, 2, 1, 3)
        g = jnp.einsum('bti,oi->bto', x, Wg)
        q = _rotary(q, Tx, D)
        k = _rotary(k, Tx, D)
        gamma = 1.0 - jnp.exp2(-5.0 - jnp.arange(H, dtype=jnp.float32))
        s = jnp.log2(gamma)
        n = jnp.arange(Tx, dtype=jnp.float32)
        rel = n[:, None] - n[None, :]
        causal = rel >= 0
        decay = jnp.where(causal[None, :, :], jnp.exp2(rel[None, :, :] * s[:, None, None]), 0.0)
        scores = jnp.einsum('bhtd,bhsd->bhts', q, k) * D ** (-0.5)
        scores = scores * decay[None]
        o = jnp.einsum('bhts,bhsv->bhtv', scores, v)
        o = o.transpose(0, 2, 1, 3)
        mean = jnp.mean(o, axis=-1, keepdims=True)
        var = jnp.var(o, axis=-1, keepdims=True)
        o = (o - mean) * jax.lax.rsqrt(var + EPS)
        o = o * gn_weight.reshape(H, V) + gn_bias.reshape(H, V)
        o = o.reshape(Bx, Tx, H * V)
        o = o * jax.nn.silu(g)
        return jnp.einsum('btc,oc->bto', o, Wo)

    def _L1_ffn_ref(hidden_states, router_w, bias, gate_w, up_w, down_w, sh_gate_w, sh_up_w, sh_down_w):
        import jax, jax.numpy as jnp
        import numpy as np
        B, S, D = (1, 256, 128)
        E, F = (16, 128)
        NG, TKG, K = (4, 2, 4)
        NSH = 2
        SCALE = 2.5
        STD = 0.02
        EPG = E // NG

        def _route(x_flat, router_w, bias):
            logits = x_flat.astype(jnp.float32) @ router_w.T
            scores = jax.nn.sigmoid(logits)
            s = scores + bias[None, :]
            sg = s.reshape(-1, NG, EPG)
            group_score = jax.lax.top_k(sg, 2)[0].sum(-1)
            gidx = jax.lax.top_k(group_score, TKG)[1]
            gmask = jnp.sum(jax.nn.one_hot(gidx, NG, dtype=jnp.float32), axis=1) > 0
            emask = jnp.repeat(gmask, EPG, axis=1)
            masked = jnp.where(emask, s, -1.0)
            topk_idx = jax.lax.top_k(masked, K)[1]
            tw = jnp.take_along_axis(scores, topk_idx, axis=1)
            tw = tw / (tw.sum(-1, keepdims=True) + 1e-20)
            tw = tw * SCALE
            return (topk_idx, tw)
        x = hidden_states.reshape(-1, D)
        topk_idx, tw = _route(x, router_w, bias)
        combine = (jax.nn.one_hot(topk_idx, E, dtype=tw.dtype) * tw[..., None]).sum(1)
        h = jnp.einsum('td,edf->etf', x, gate_w)
        u = jnp.einsum('td,edf->etf', x, up_w)
        y = jnp.einsum('etf,efd->etd', jax.nn.silu(h) * u, down_w)
        routed = jnp.einsum('etd,te->td', y, combine)
        sh = jax.nn.silu(x @ sh_gate_w) * (x @ sh_up_w) @ sh_down_w
        return (routed + sh).reshape(hidden_states.shape)
    x = L0_attn_x
    x = x + 0.5 * _L0_ffn_ref(_layernorm(x, axis=-1), L0_ffn_base_w, L0_ffn_base_b, L0_ffn_lora_A, L0_ffn_lora_B, L0_ffn_router_w, L0_ffn_router_b)
    x = x + _L0_attn_ref(_layernorm(x, axis=-1), L0_attn_W_attn, L0_attn_b_attn, L0_attn_W_proj, L0_attn_b_proj, L0_attn_bias_table)
    x = x + 0.5 * _L0_ffn_ref(_layernorm(x, axis=-1), L0_ffn_base_w, L0_ffn_base_b, L0_ffn_lora_A, L0_ffn_lora_B, L0_ffn_router_w, L0_ffn_router_b)
    x = x + 0.5 * _L1_ffn_ref(_layernorm(x, axis=-1), L1_ffn_router_w, L1_ffn_bias, L1_ffn_gate_w, L1_ffn_up_w, L1_ffn_down_w, L1_ffn_sh_gate_w, L1_ffn_sh_up_w, L1_ffn_sh_down_w)
    x = x + _L1_attn_ref(_layernorm(x, axis=-1), L1_attn_Wq, L1_attn_Wk, L1_attn_Wv, L1_attn_Wg, L1_attn_Wo, L1_attn_gn_weight, L1_attn_gn_bias)
    x = x + 0.5 * _L1_ffn_ref(_layernorm(x, axis=-1), L1_ffn_router_w, L1_ffn_bias, L1_ffn_gate_w, L1_ffn_up_w, L1_ffn_down_w, L1_ffn_sh_gate_w, L1_ffn_sh_up_w, L1_ffn_sh_down_w)
    return x

_drawn_inputs = setup_inputs


def setup_inputs(seed=0):
    import zlib

    import numpy as np

    out = dict(_drawn_inputs(seed))
    spreads = {'L0_attn_b_attn': (0.0, 0.386),
     'L0_attn_b_proj': (0.0, 0.1),
     'L0_ffn_base_b': (0.0, 0.1),
     'L0_ffn_router_b': (0.0, 0.8),
     'L1_attn_gn_weight': (1.0, 0.6),
     'L1_attn_gn_bias': (0.0, 0.8),
     'L1_ffn_bias': (0.0, 0.8)}
    factors = {'L0_attn_W_attn': 6.855,
     'L0_attn_W_proj': 2.712,
     'L0_attn_bias_table': 8.0,
     'L0_ffn_lora_A': 6.431,
     'L0_ffn_lora_B': 6.2,
     'L0_ffn_router_w': 8.0,
     'L1_ffn_router_w': 8.0,
     'L1_ffn_gate_w': 8.0,
     'L1_ffn_up_w': 8.0,
     'L1_ffn_down_w': 8.0,
     'L1_ffn_sh_gate_w': 7.215,
     'L1_ffn_sh_up_w': 7.124,
     'L1_ffn_sh_down_w': 7.113}
    for name, (base, spread) in spreads.items():
        noise = np.random.default_rng([zlib.crc32(name.encode()), seed]).standard_normal(out[name].shape)
        drawn = base * np.exp(spread * noise) if base else spread * noise
        out[name] = jnp.asarray(drawn.astype(out[name].dtype))
    for name, factor in factors.items():
        out[name] = (out[name] * factor).astype(out[name].dtype)
    return out
```

```python
from contextlib import ExitStack

import concourse.bass as bass
from concourse import mybir

P = 128
F32 = mybir.dt.float32
F32R = mybir.dt.float32r
BF16 = mybir.dt.bfloat16
ALU = mybir.AluOpType
ACT = mybir.ActivationFunctionType
AX = mybir.AxisListType

BATCHES, T, C = 16, 256, 128
TILES = BATCHES * T // P
LN_EPS = 1e-5

GROUP = 4
GROUPS = TILES // GROUP
GT = GROUP * P

LORA_E, LORA_R = 8, 8
LORA_ROWS = LORA_E * LORA_R
LORA_SCALING = 2.0


def software_pipeline(engine, iterations, units, stages):
    most = max(lead for lead, _ in stages)
    assert most <= units
    for step in range(-most, 0):
        for lead, emit in stages:
            if step + lead >= 0:
                emit((step + lead) // units, (step + lead) % units)
    if iterations > 1:
        with engine.Fori(0, iterations - 1) as it:
            for step in range(units):
                for lead, emit in stages:
                    emit(it + (step + lead) // units, (step + lead) % units)
    for step in range(units):
        for lead, emit in stages:
            if step + lead < units:
                emit(iterations - 1, step + lead)


def new_sem(nc, used, name):
    used.append(nc.alloc_semaphore(name=name))
    return used[-1]


def retire(nc, used):
    nc.clear_and_free_semaphores(used)
    nc.all_engine_barrier()
    used.clear()


def bank_taker(banks):
    taken = [0]

    def take(shape):
        size = 1
        for n in shape[1:]:
            size *= n
        first = taken[0]
        taken[0] += -(-size // 512)
        assert taken[0] <= 8
        flat = banks[0:shape[0], first:taken[0], :].rearrange("p b c -> p (b c)")[:, 0:size]
        if len(shape) == 3:
            return flat.rearrange("p (a b) -> p a b", a=shape[1])
        if len(shape) == 4:
            return flat.rearrange("p (a b c) -> p a b c", a=shape[1], b=shape[2])
        return flat

    return take


def ffn_lora_phase(nc, tag, banks, used, x_res, ident, neg_half, w):
    U = 2
    with ExitStack() as ctx:
        def sb(name, shape, dt=F32):
            return ctx.enter_context(nc.sbuf_tensor(f"{tag}_{name}", shape, dt))

        bank = bank_taker(banks)

        def sem(name):
            return new_sem(nc, used, f"{tag}_{name}")

        stats = sb("stats", [P, 2, GROUP, 6])
        mv = sb("mv", [P, 2, GROUP, 2])
        rstd = sb("rstd", [P, 2, GROUP])
        var_eps = sb("var_eps", [P, 2, GROUP])
        xn = sb("xn", [P, 2, GROUP, C])
        xnT = sb("xnT", [P, 2, GT])
        logit = sb("logit", [P, 2, GROUP, LORA_E])
        top = sb("top", [P, 2, GROUP])
        shifted = sb("shifted", [P, 2, GROUP, LORA_E])
        expd = sb("expd", [P, 2, GROUP, LORA_E])
        total = sb("total", [P, 2, GROUP])
        inv = sb("inv", [P, 2, GROUP])
        gate = sb("gate", [P, 2, GROUP, LORA_E], BF16)
        mid = sb("mid", [P, 2, GROUP, LORA_R])
        om = sb("om", [P, 2, GROUP, LORA_ROWS + 1])
        omT = sb("omT", [LORA_ROWS + 1, 2, GT])
        ps_t = bank([P, GT])
        ps_small = bank([P, GROUP, 16])
        ps_o = bank([LORA_ROWS + 1, GT])
        ps_y = bank([P, 2, GT])

        stats_done, aggr_done, rstd_done, xn_ready = sem("stats_done"), sem("aggr_done"), sem("rstd_done"), sem("xn_ready")
        eps_added = sem("eps_added")
        ones_ready, xn_transposed, xnT_ready, small_ready = sem("ones_ready"), sem("xn_transposed"), sem("xnT_ready"), sem("small_ready")
        logit_done, top_done, shifted_ready, exp_ready = sem("logit_done"), sem("top_done"), sem("shifted_ready"), sem("exp_ready")
        total_done, inv_done, gate_done, om_ready = sem("total_done"), sem("inv_done"), sem("gate_done"), sem("om_ready")
        om_transposed, omT_ready, y_ready, x_updated = sem("om_transposed"), sem("omT_ready"), sem("y_ready"), sem("x_updated")

        block = ctx.enter_context(nc.Block())

        def count(it, u, back=0):
            return it * U + (u + 1 - back)

        def x_group(it, u):
            return x_res[:, bass.ds((it * U + u) * GROUP, GROUP), :]

        @block.vector
        def _(dve):
            for p in range(2):
                dve.memset(om[:, p, :, LORA_ROWS:], 1.0).then_inc(ones_ready, 1)

            def layernorm(it, u):
                p = u % 2
                xg = x_group(it, u)
                for j in range(GROUP):
                    last = dve.bn_stats(stats[:, p, j, :], xg[:, j, :])
                last.then_inc(stats_done, 1)
                dve.wait_ge(stats_done, count(it, u))
                dve.nop(nofuse=True)
                for j in range(GROUP):
                    last = dve.bn_aggr(mv[:, p, j, :], stats[:, p, j, :])
                last.then_inc(aggr_done, 1)

            def normalise(it, u):
                p = u % 2
                xg = x_group(it, u)
                dve.wait_ge(rstd_done, count(it, u))
                for j in range(GROUP):
                    last = dve.tensor_scalar(xn[:, p, j, :], xg[:, j, :], mv[:, p, j, 0:1], rstd[:, p, j:j + 1],
                                             ALU.subtract, ALU.mult)
                last.then_inc(xn_ready, 1)

            def router_shift(it, u):
                p = u % 2
                dve.wait_ge(small_ready, count(it, u))
                dve.tensor_tensor(logit[:, p], ps_small[:, :, 0:LORA_E], w["router_b"][:, :, :], ALU.add).then_inc(logit_done, 1)
                dve.tensor_copy(mid[:, p], ps_small[:, :, LORA_E:])
                dve.wait_ge(logit_done, count(it, u))
                dve.tensor_reduce(top[:, p, :], logit[:, p], AX.X, ALU.max).then_inc(top_done, 1)
                dve.wait_ge(top_done, count(it, u))
                dve.tensor_tensor(shifted[:, p], logit[:, p], top[:, p, :].unsqueeze(2).to_broadcast([P, GROUP, LORA_E]),
                                  ALU.subtract).then_inc(shifted_ready, 1)

            def gates(it, u):
                p = u % 2
                dve.wait_ge(exp_ready, count(it, u))
                dve.tensor_reduce(total[:, p, :], expd[:, p], AX.X, ALU.add).then_inc(total_done, 1)
                dve.wait_ge(total_done, count(it, u))
                dve.reciprocal(inv[:, p, :], total[:, p, :]).then_inc(inv_done, 1)
                dve.wait_ge(inv_done, count(it, u))
                dve.tensor_tensor(gate[:, p], expd[:, p], inv[:, p, :].unsqueeze(2).to_broadcast([P, GROUP, LORA_E]),
                                  ALU.mult).then_inc(gate_done, 1)
                dve.wait_ge(gate_done, count(it, u))
                for j in range(GROUP):
                    last = dve.tensor_tensor(
                        om[:, p, j, 0:LORA_ROWS].rearrange("p (e r) -> p e r", e=LORA_E),
                        gate[:, p, j, :].unsqueeze(2).to_broadcast([P, LORA_E, LORA_R]),
                        mid[:, p, j, :].unsqueeze(1).to_broadcast([P, LORA_E, LORA_R]), ALU.mult)
                last.then_inc(om_ready, 1)

            def residual(it, u):
                dve.wait_ge(y_ready, count(it, u))
                xg = x_group(it, u).rearrange("p j c -> p (j c)")
                dve.scalar_tensor_tensor(xg, ps_y[:, u % 2, :], 0.5, xg, ALU.mult, ALU.add).then_inc(x_updated, 1)

            software_pipeline(dve, GROUPS // U, U, [(2, layernorm), (1, router_shift), (0, residual), (1, gates), (2, normalise)])

        @block.gpsimd
        def _(pool):
            def inverse_std(it, u):
                pool.wait_ge(aggr_done, count(it, u))
                pool.nop(nofuse=True)
                pool.tensor_scalar(var_eps[:, u % 2, :], mv[:, u % 2, :, 1], LN_EPS, None, ALU.add).then_inc(eps_added, 1)
                pool.wait_ge(eps_added, count(it, u))
                pool.tensor_tensor(rstd[:, u % 2, :], var_eps[:, u % 2, :], neg_half[:, 0:GROUP], ALU.pow).then_inc(rstd_done, 1)

            software_pipeline(pool, GROUPS // U, U, [(0, inverse_std)])

        @block.tensor
        def _(pe):
            def transpose_x(it, u):
                pe.wait_ge(xn_ready, count(it, u))
                for j in range(GROUP):
                    last = pe.transpose(ps_t[:, j * P:(j + 1) * P], xn[:, u % 2, j, :], ident[:, :])
                last.then_inc(xn_transposed, 1)

            def router_and_mid(it, u):
                pe.wait_ge(xnT_ready, count(it, u))
                for j in range(GROUP):
                    last = pe.matmul(ps_small[:, j, :], xnT[:, u % 2, j * P:(j + 1) * P], w["router_a"], start=True, stop=True)
                last.then_inc(small_ready, 1)

            def transpose_om(it, u):
                pe.wait_ge(om_ready, count(it, u))
                for j in range(GROUP):
                    last = pe.transpose(ps_o[:, j * P:(j + 1) * P], om[:, u % 2, j, :], ident[:, :])
                last.then_inc(om_transposed, 1)

            def project(it, u):
                pe.wait_ge(omT_ready, count(it, u))
                for j in range(GROUP):
                    y = ps_y[:, u % 2, j * P:(j + 1) * P]
                    pe.matmul(y, xnT[:, u % 2, j * P:(j + 1) * P], w["base_T"], start=True, stop=False)
                    last = pe.matmul(y, omT[:, u % 2, j * P:(j + 1) * P], w["lora_rows"], start=False, stop=True)
                last.then_inc(y_ready, 1)

            pe.wait_ge(ones_ready, 2)
            software_pipeline(pe, GROUPS // U, U, [(1, transpose_x), (0, transpose_om), (1, router_and_mid), (0, project)])

        @block.scalar
        def _(act):
            def copy_xT(it, u):
                act.wait_ge(xn_transposed, count(it, u))
                act.copy(xnT[:, u % 2, :], ps_t[:, :]).then_inc(xnT_ready, 1)

            def exponent(it, u):
                act.wait_ge(shifted_ready, count(it, u))
                act.activation(expd[:, u % 2], shifted[:, u % 2], ACT.Exp).then_inc(exp_ready, 1)

            def copy_omT(it, u):
                act.wait_ge(om_transposed, count(it, u))
                act.copy(omT[:, u % 2, :], ps_o[:, :]).then_inc(omT_ready, 1)

            software_pipeline(act, GROUPS // U, U, [(1, copy_xT), (0, copy_omT), (1, exponent)])


MOE_E, MOE_G, MOE_K = 16, 4, 4
MOE_EPG = MOE_E // MOE_G
MOE_F = 128
MOE_SHARED = 2
MOE_UNITS = MOE_E + MOE_SHARED
MOE_SCALE = 2.5
PAD, PICKED, PICKED_BELOW = -3.0e38, -3.3e38, -3.2e38


def moe_phase(nc, tag, banks, used, x_res, ident, ident_bf, neg_half, w):
    GU = 2
    U = GU * MOE_UNITS
    RING = 3
    with ExitStack() as ctx:
        def sb(name, shape, dt=F32):
            return ctx.enter_context(nc.sbuf_tensor(f"{tag}_{name}", shape, dt))

        bank = bank_taker(banks)

        def sem(name):
            return new_sem(nc, used, f"{tag}_{name}")

        stats = sb("stats", [P, GU, GROUP, 6])
        mv = sb("mv", [P, GU, GROUP, 2])
        var_eps = sb("var_eps", [P, GU, GROUP])
        rstd = sb("rstd", [P, GU, GROUP])
        xn = sb("xn", [P, GROUP, C])
        x_hi = sb("x_hi", [P, GU, GT], F32R)
        x_lo = sb("x_lo", [P, GU, GT], F32R)
        silu_l = sb("silu_l", [P, GROUP, MOE_E])
        tanh_l = sb("tanh_l", [P, GROUP, MOE_E])
        inv_l = sb("inv_l", [P, GROUP, MOE_E])
        not_low = sb("not_low", [P, GROUP, MOE_E])
        upper = sb("upper", [P, GROUP, MOE_E])
        score = sb("score", [P, GROUP, MOE_E])
        biased = sb("biased", [P, GROUP, MOE_E])
        pair_max = sb("pair_max", [P, GROUP * MOE_G, 2])
        pair_min = sb("pair_min", [P, GROUP * MOE_G, 2])
        first = sb("first", [P, GROUP * MOE_G])
        low_max = sb("low_max", [P, GROUP * MOE_G])
        high_min = sb("high_min", [P, GROUP * MOE_G])
        second = sb("second", [P, GROUP * MOE_G])
        group_score = sb("group_score", [P, GROUP, MOE_G])
        above = sb("above", [P, GROUP * MOE_G, MOE_G])
        tied = sb("tied", [P, GROUP * MOE_G, MOE_G])
        tied_before = sb("tied_before", [P, GROUP * MOE_G, MOE_G])
        beaten = sb("beaten", [P, GROUP * MOE_G, MOE_G])
        rank = sb("rank", [P, GROUP * MOE_G])
        kept = sb("kept", [P, GROUP * MOE_G])
        kept_minus = sb("kept_minus", [P, GROUP * MOE_G])
        kept_score = sb("kept_score", [P, GROUP, MOE_E])
        masked = sb("masked", [P, GROUP, MOE_E + MOE_K])
        top8 = sb("top8", [P, GROUP, 8])
        wanted = sb("wanted", [P, GROUP, 8])
        replaced = sb("replaced", [P, GROUP, MOE_E + MOE_K])
        picked = sb("picked", [P, GROUP, MOE_E])
        picked_score = sb("picked_score", [P, GROUP, MOE_E])
        total = sb("total", [P, GROUP])
        total_eps = sb("total_eps", [P, GROUP])
        inv = sb("inv", [P, GROUP])
        inv_scaled = sb("inv_scaled", [P, GROUP])
        combine = sb("combine", [P, GROUP, MOE_E])
        rest = sb("rest", [P, GROUP, MOE_E])
        rest2 = sb("rest2", [P, GROUP, MOE_E])
        combine3 = sb("combine3", [P, GROUP, 3, MOE_E], BF16)
        combine3T = sb("combine3T", [3 * MOE_E, GU, GT], BF16)
        gated = sb("gated", [P, RING, GT])
        product = sb("product", [P, 2, GT])
        act_f = sb("act_f", [P, RING, GT])
        act_hi = sb("act_hi", [P, RING, GT], F32R)
        act_lo = sb("act_lo", [P, RING, GT], F32R)
        yT = sb("yT", [P, GT])
        ps_h, ps_u, ps_c = bank([P, GT]), bank([P, 2, GT]), bank([P, 2, GT])
        ps_y, ps_t = bank([P, GT]), bank([P, GT])
        ps_m = bank([P, GT])
        ps_logit = ps_m[:, 0:GROUP * MOE_E].rearrange("p (j e) -> p j e", e=MOE_E)
        ps_cT = ps_m[0:3 * MOE_E, 256:512].bitcast(BF16)

        pads_set = sem("pads_set")
        stats_done, aggr_done, eps_added, rstd_done, xn_ready = (sem(n) for n in ("stats_done", "aggr_done", "eps_added", "rstd_done", "xn_ready"))
        xn_transposed, x_hi_ready, x_split = sem("xn_transposed"), sem("x_hi_ready"), sem("x_split")
        logits_ready, score_ready, topk_step, combine_split = sem("logits_ready"), sem("score_ready"), sem("topk_step"), sem("combine_split")
        combine_step, combine_transposed, combineT_ready = sem("combine_step"), sem("combine_transposed"), sem("combineT_ready")
        h_ready, u_ready, c_ready, gated_ready, product_done = (sem(n) for n in ("h_ready", "u_ready", "c_ready", "gated_ready", "product_done"))
        act_ready, act_hi_ready, act_lo_ready, down_done = sem("act_ready"), sem("act_hi_ready"), sem("act_lo_ready"), sem("down_done")
        yT_ready, y_transposed, x_updated = sem("yT_ready"), sem("y_transposed"), sem("x_updated")

        block = ctx.enter_context(nc.Block())

        def unit(it, k, back=0):
            return it * U + (k + 1 - back)

        def routed(it, k):
            return it * GU * MOE_E + (k // MOE_UNITS * MOE_E + k % MOE_UNITS + 1)

        def group(it, k, back=0):
            return it * GU + (k // MOE_UNITS + 1 - back)

        def wait_free(engine, semaphore, value):
            if not isinstance(value, int) or value > 0:
                engine.wait_ge(semaphore, value)

        def per_group(at, emit):
            def stage(it, k):
                if k % MOE_UNITS == at:
                    emit(it, k)
            return stage

        def x_group(it, k):
            return x_res[:, bass.ds((it * GU + k // MOE_UNITS) * GROUP, GROUP), :]

        TOPK_STEPS = 33

        @block.vector
        def _(dve):
            dve.memset(masked[:, :, MOE_E:], PAD).then_inc(pads_set, 1)
            dve.memset(wanted[:, :, MOE_K:], PAD).then_inc(pads_set, 1)
            dve.wait_ge(pads_set, 2)

            def layernorm(it, k):
                p = k // MOE_UNITS % GU
                xg = x_group(it, k)
                for j in range(GROUP):
                    last = dve.bn_stats(stats[:, p, j, :], xg[:, j, :])
                last.then_inc(stats_done, 1)
                dve.wait_ge(stats_done, group(it, k))
                dve.nop(nofuse=True)
                for j in range(GROUP):
                    last = dve.bn_aggr(mv[:, p, j, :], stats[:, p, j, :])
                last.then_inc(aggr_done, 1)

            def normalise(it, k):
                p = k // MOE_UNITS % GU
                xg = x_group(it, k)
                dve.wait_ge(rstd_done, group(it, k))
                wait_free(dve, xn_transposed, group(it, k, 1))
                for j in range(GROUP):
                    last = dve.tensor_scalar(xn[:, j, :], xg[:, j, :], mv[:, p, j, 0:1], rstd[:, p, j:j + 1],
                                             ALU.subtract, ALU.mult)
                last.then_inc(xn_ready, 1)

            def split_x(it, k):
                p = k // MOE_UNITS % GU
                dve.wait_ge(x_hi_ready, group(it, k))
                dve.tensor_tensor(x_lo[:, p, :], ps_t[:, :], x_hi[:, p, :].bitcast(F32), ALU.subtract).then_inc(x_split, 1)

            def topk_ops(it, k):
                per_token = [P, GROUP * MOE_G, MOE_G]
                s4 = biased[:, :, :].rearrange("p j (g e) -> p (j g) e", e=MOE_EPG)
                gs = group_score[:, :, :]
                gs_of = group_score[:, :, :].rearrange("p j g -> p (j g)").unsqueeze(2).to_broadcast(per_token)

                def others(dst):
                    return dst[:, :, :].rearrange("p (j g) h -> p j g h", g=MOE_G)

                def compare(dst, op):
                    shape = [P, GROUP, MOE_G, MOE_G]
                    return dve.tensor_tensor(others(dst), gs.unsqueeze(2).to_broadcast(shape),
                                             gs.unsqueeze(3).to_broadcast(shape), op)

                k4 = kept_score[:, :, :].rearrange("p j (g e) -> p (j g) e", e=MOE_EPG)
                m4 = masked[:, :, 0:MOE_E].rearrange("p j (g e) -> p j g e", e=MOE_EPG)
                j4 = [P, GROUP, MOE_G, MOE_EPG]
                return [
                    lambda: dve.tensor_scalar(not_low[:, :, :], ps_logit, -1.0, None, ALU.is_ge),
                    lambda: dve.reciprocal(inv_l[:, :, :], ps_logit),
                    lambda: dve.tensor_tensor(score[:, :, :], silu_l[:, :, :], inv_l[:, :, :], ALU.mult),
                    lambda: dve.tensor_scalar(upper[:, :, :], tanh_l[:, :, :], 0.5, 0.5, ALU.mult, ALU.add),
                    lambda: [dve.nop(nofuse=True), dve.copy_predicated(score[:, :, :], not_low[:, :, :].bitcast(mybir.dt.int32), upper[:, :, :])],
                    lambda: dve.tensor_tensor(biased[:, :, :], score[:, :, :], w["bias"][:, :, :], ALU.add),
                    lambda: dve.tensor_tensor(pair_max[:, :, :], s4[:, :, 0:4:2], s4[:, :, 1:4:2], ALU.max),
                    lambda: dve.tensor_tensor(pair_min[:, :, :], s4[:, :, 0:4:2], s4[:, :, 1:4:2], ALU.min),
                    lambda: dve.tensor_tensor(first[:, :], pair_max[:, :, 0], pair_max[:, :, 1], ALU.max),
                    lambda: dve.tensor_tensor(high_min[:, :], pair_max[:, :, 0], pair_max[:, :, 1], ALU.min),
                    lambda: dve.tensor_tensor(low_max[:, :], pair_min[:, :, 0], pair_min[:, :, 1], ALU.max),
                    lambda: dve.tensor_tensor(second[:, :], high_min[:, :], low_max[:, :], ALU.max),
                    lambda: dve.tensor_tensor(gs.rearrange("p j g -> p (j g)"), first[:, :], second[:, :], ALU.add),
                    lambda: compare(above, ALU.is_gt),
                    lambda: compare(tied, ALU.is_equal),
                    lambda: dve.tensor_tensor(tied_before[:, :, :], tied[:, :, :], w["before"][:, :, :], ALU.mult),
                    lambda: dve.tensor_tensor(beaten[:, :, :], above[:, :, :], tied_before[:, :, :], ALU.add),
                    lambda: dve.tensor_reduce(rank[:, :], beaten[:, :, :], AX.X, ALU.add),
                    lambda: dve.tensor_scalar(kept[:, :], rank[:, :], 2.0, None, ALU.is_lt),
                    lambda: dve.tensor_scalar(kept_minus[:, :], kept[:, :], 1.0, None, ALU.subtract),
                    lambda: dve.tensor_tensor(k4, s4, kept[:, :].unsqueeze(2).to_broadcast(per_token), ALU.mult),
                    lambda: dve.tensor_tensor(
                        m4, kept_score[:, :, :].rearrange("p j (g e) -> p j g e", e=MOE_EPG),
                        kept_minus[:, :].rearrange("p (j g) -> p j g", g=MOE_G).unsqueeze(3).to_broadcast(j4), ALU.add),
                    lambda: [dve.nop(nofuse=True)] + [dve.max(top8[:, j, :], masked[:, j, :]) for j in range(GROUP)],
                    lambda: dve.tensor_copy(wanted[:, :, 0:MOE_K], top8[:, :, 0:MOE_K]),
                    lambda: [dve.nop(nofuse=True)] + [dve.match_replace(replaced[:, j, :], wanted[:, j, :], masked[:, j, :], PICKED)
                                                      for j in range(GROUP)],
                    lambda: dve.tensor_scalar(picked[:, :, :], replaced[:, :, 0:MOE_E], PICKED_BELOW, None, ALU.is_lt),
                    lambda: dve.tensor_tensor(picked_score[:, :, :], picked[:, :, :], score[:, :, :], ALU.mult),
                    lambda: dve.tensor_reduce(total[:, :], picked_score[:, :, :], AX.X, ALU.add),
                    lambda: dve.tensor_scalar(total_eps[:, :], total[:, :], 1e-20, None, ALU.add),
                    lambda: dve.reciprocal(inv[:, :], total_eps[:, :]),
                    lambda: dve.tensor_scalar(inv_scaled[:, :], inv[:, :], MOE_SCALE, None, ALU.mult),
                    lambda: dve.tensor_tensor(combine[:, :, :], picked_score[:, :, :],
                                              inv_scaled[:, :].unsqueeze(2).to_broadcast([P, GROUP, MOE_E]), ALU.mult),
                ]

            def topk(lo, hi):
                def stage(it, k):
                    ops = topk_ops(it, k)
                    assert len(ops) == TOPK_STEPS - 1
                    g0 = it * GU + k // MOE_UNITS
                    if lo == 0:
                        dve.wait_ge(score_ready, group(it, k))
                    for i in range(lo, min(hi, len(ops))):
                        if i > 0:
                            dve.wait_ge(topk_step, g0 * (TOPK_STEPS - 1) + i)
                        if i == len(ops) - 1:
                            wait_free(dve, combine_split, group(it, k, 1))
                        last = ops[i]()
                        if isinstance(last, list):
                            last = last[-1]
                        last.then_inc(topk_step, 1)
                return stage

            def multiply(it, k):
                e = k % MOE_UNITS
                dve.wait_ge(gated_ready, unit(it, k))
                dve.wait_ge(u_ready, unit(it, k))
                if e < MOE_E:
                    dve.tensor_tensor(product[:, k % 2, :], ps_u[:, k % 2, :], gated[:, k % RING, :], ALU.mult).then_inc(product_done, 1)
                    dve.wait_ge(product_done, routed(it, k))
                    dve.wait_ge(c_ready, routed(it, k))
                    wait_free(dve, act_lo_ready, unit(it, k, RING))
                    dve.tensor_tensor(act_f[:, k % RING, :], ps_c[:, k % 2, :], product[:, k % 2, :], ALU.mult).then_inc(act_ready, 1)
                else:
                    wait_free(dve, act_lo_ready, unit(it, k, RING))
                    dve.tensor_tensor(act_f[:, k % RING, :], ps_u[:, k % 2, :], gated[:, k % RING, :], ALU.mult).then_inc(act_ready, 1)

            def residual(it, k):
                dve.wait_ge(y_transposed, group(it, k))
                xg = x_group(it, k).rearrange("p j c -> p (j c)")
                dve.scalar_tensor_tensor(xg, ps_t[:, :], 0.5, xg, ALU.mult, ALU.add).then_inc(x_updated, 1)

            software_pipeline(dve, GROUPS // GU, U, [
                (20, per_group(0, layernorm)), (17, per_group(0, split_x)),
                (15, per_group(0, topk(0, 7))), (14, per_group(0, topk(7, 12))), (13, per_group(0, topk(12, 18))),
                (12, per_group(0, topk(18, 23))), (11, per_group(0, topk(23, 33))), (5, multiply), (19, per_group(0, normalise)), (0, per_group(MOE_UNITS - 1, residual))])

        @block.gpsimd
        def _(pool):
            def inverse_std(it, k):
                p = k // MOE_UNITS % GU
                pool.wait_ge(aggr_done, group(it, k))
                pool.nop(nofuse=True)
                pool.tensor_scalar(var_eps[:, p, :], mv[:, p, :, 1], LN_EPS, None, ALU.add).then_inc(eps_added, 1)
                pool.wait_ge(eps_added, group(it, k))
                pool.tensor_tensor(rstd[:, p, :], var_eps[:, p, :], neg_half[:, 0:GROUP], ALU.pow).then_inc(rstd_done, 1)

            def split_combine(it, k):
                steps = 4 * (it * GU + k // MOE_UNITS)
                part = [combine3[:, :, i, :] for i in range(3)]
                pool.wait_ge(topk_step, (it * GU + k // MOE_UNITS + 1) * (TOPK_STEPS - 1))
                wait_free(pool, combine_transposed, group(it, k, 1))
                pool.nop(nofuse=True)
                pool.tensor_copy(part[0], combine[:, :, :]).then_inc(combine_step, 1)
                pool.wait_ge(combine_step, steps + 1)
                pool.tensor_tensor(rest[:, :, :], combine[:, :, :], part[0], ALU.subtract).then_inc(combine_step, 1)
                pool.wait_ge(combine_step, steps + 2)
                pool.nop(nofuse=True)
                pool.tensor_copy(part[1], rest[:, :, :]).then_inc(combine_step, 1)
                pool.wait_ge(combine_step, steps + 3)
                pool.tensor_tensor(rest2[:, :, :], rest[:, :, :], part[1], ALU.subtract).then_inc(combine_step, 1)
                pool.wait_ge(combine_step, steps + 4)
                pool.nop(nofuse=True)
                pool.tensor_copy(part[2], rest2[:, :, :]).then_inc(combine_split, 1)

            def split_lo(it, k):
                pool.wait_ge(act_hi_ready, unit(it, k))
                wait_free(pool, down_done, unit(it, k, RING))
                pool.tensor_tensor(act_lo[:, k % RING, :], act_f[:, k % RING, :], act_hi[:, k % RING, :].bitcast(F32),
                                   ALU.subtract).then_inc(act_lo_ready, 1)

            software_pipeline(pool, GROUPS // GU, U, [
                (20, per_group(0, inverse_std)), (11, per_group(0, split_combine)), (5, split_lo)])

        @block.scalar
        def _(act):
            def copy_x_hi(it, k):
                act.wait_ge(xn_transposed, group(it, k))
                act.copy(x_hi[:, k // MOE_UNITS % GU, :], ps_t[:, :]).then_inc(x_hi_ready, 1)

            def sigmoid(it, k):
                act.wait_ge(logits_ready, group(it, k))
                wait_free(act, topk_step, (it * GU + k // MOE_UNITS) * (TOPK_STEPS - 1))
                act.activation(silu_l[:, :, :], ps_logit, ACT.Silu)
                act.activation(tanh_l[:, :, :], ps_logit, ACT.Tanh, scale=0.5).then_inc(score_ready, 1)

            def copy_combineT(it, k):
                act.wait_ge(combine_transposed, group(it, k))
                act.copy(combine3T[:, k // MOE_UNITS % GU, :], ps_cT).then_inc(combineT_ready, 1)

            def silu(it, k):
                act.wait_ge(h_ready, unit(it, k))
                wait_free(act, act_ready, unit(it, k, RING))
                act.activation(gated[:, k % RING, :], ps_h[:, :], ACT.Silu).then_inc(gated_ready, 1)

            def split_hi(it, k):
                act.wait_ge(act_ready, unit(it, k))
                wait_free(act, down_done, unit(it, k, RING))
                act.copy(act_hi[:, k % RING, :], act_f[:, k % RING, :]).then_inc(act_hi_ready, 1)

            def copy_yT(it, k):
                act.wait_ge(down_done, unit(it, k))
                wait_free(act, y_transposed, group(it, k, 1))
                act.copy(yT[:, :], ps_y[:, :]).then_inc(yT_ready, 1)

            software_pipeline(act, GROUPS // GU, U, [
                (17, per_group(0, copy_x_hi)), (15, per_group(0, sigmoid)), (8, per_group(0, copy_combineT)),
                (5, silu), (4, split_hi), (1, per_group(MOE_UNITS - 1, copy_yT))])

        @block.tensor
        def _(pe):
            def three_pass(out, weights, column, hi, lo, start=True, stop=True):
                w_hi, w_lo = (part[:, column:column + MOE_F] for part in weights)
                pe.matmul(out, w_hi, hi, start=start, stop=False)
                pe.matmul(out, w_hi, lo, start=False, stop=False)
                return pe.matmul(out, w_lo, hi, start=False, stop=stop)

            def transpose_x(it, k):
                pe.wait_ge(xn_ready, group(it, k))
                wait_free(pe, x_updated, group(it, k, 2))
                for j in range(GROUP):
                    last = pe.transpose(ps_t[:, j * P:(j + 1) * P], xn[:, j, :], ident[:, :])
                last.then_inc(xn_transposed, 1)

            def router(it, k):
                p = k // MOE_UNITS % GU
                pe.wait_ge(x_split, group(it, k))
                wait_free(pe, topk_step, (it * GU + k // MOE_UNITS) * (TOPK_STEPS - 1))
                for j in range(GROUP):
                    hi, lo = x_hi[:, p, j * P:(j + 1) * P], x_lo[:, p, j * P:(j + 1) * P]
                    r_hi, r_lo = w["router"]
                    pe.matmul(ps_logit[:, j, :], hi, r_hi, start=True, stop=False)
                    pe.matmul(ps_logit[:, j, :], lo, r_hi, start=False, stop=False)
                    last = pe.matmul(ps_logit[:, j, :], hi, r_lo, start=False, stop=True)
                last.then_inc(logits_ready, 1)

            def transpose_combine(it, k):
                pe.wait_ge(combine_split, group(it, k))
                wait_free(pe, combineT_ready, group(it, k, 1))
                pe.nop(nofuse=True)
                for j in range(GROUP):
                    last = pe.transpose(ps_cT[:, j * P:(j + 1) * P], combine3[:, j, :, :].rearrange("p i e -> p (i e)"), ident_bf[:, :])
                last.then_inc(combine_transposed, 1)

            def up(it, k):
                p, e = k // MOE_UNITS % GU, k % MOE_UNITS
                if e == 0:
                    pe.wait_ge(x_split, group(it, k))
                wait_free(pe, gated_ready, unit(it, k, 1))
                three_pass(ps_h[:, :], w["up_down"], e * MOE_F, x_hi[:, p, :], x_lo[:, p, :]).then_inc(h_ready, 1)
                if (k - 2) % MOE_UNITS < MOE_E:
                    wait_free(pe, product_done, routed(it, k - 2))
                else:
                    wait_free(pe, act_ready, unit(it, k - 2))
                three_pass(ps_u[:, k % 2, :], w["up_down"], (MOE_UNITS + e) * MOE_F, x_hi[:, p, :], x_lo[:, p, :]).then_inc(u_ready, 1)

            def weights_of(it, k):
                p, e = k // MOE_UNITS % GU, k % MOE_UNITS
                if e >= MOE_E:
                    return
                if e == 0:
                    pe.wait_ge(combineT_ready, group(it, k))
                wait_free(pe, act_ready, unit(it, k, 2))
                pe.matmul(ps_c[:, k % 2, :], w["select"][:, e, :], combine3T[:, p, :], start=True, stop=True).then_inc(c_ready, 1)

            def down(it, k):
                e = k % MOE_UNITS
                d_hi, d_lo = (part[:, (2 * MOE_UNITS + e) * MOE_F:(2 * MOE_UNITS + e + 1) * MOE_F] for part in w["up_down"])
                pe.wait_ge(act_hi_ready, unit(it, k))
                if e == 0:
                    wait_free(pe, yT_ready, group(it, k, 1))
                pe.matmul(ps_y[:, :], d_hi, act_hi[:, k % RING, :], start=(e == 0), stop=False)
                pe.matmul(ps_y[:, :], d_lo, act_hi[:, k % RING, :], start=False, stop=False)
                pe.wait_ge(act_lo_ready, unit(it, k))
                pe.matmul(ps_y[:, :], d_hi, act_lo[:, k % RING, :], start=False, stop=(e == MOE_UNITS - 1)).then_inc(down_done, 1)

            def transpose_y(it, k):
                pe.wait_ge(yT_ready, group(it, k))
                seen = group(it, k, -1)
                pe.wait_ge(x_split, min(seen, GROUPS) if isinstance(seen, int) else seen)
                for j in range(GROUP):
                    last = pe.transpose(ps_t[:, j * P:(j + 1) * P], yT[:, j * P:(j + 1) * P], ident[:, :])
                last.then_inc(y_transposed, 1)

            software_pipeline(pe, GROUPS // GU, U, [
                (17, per_group(0, transpose_x)), (15, per_group(0, router)), (8, per_group(0, transpose_combine)),
                (5, up), (5, weights_of), (2, down), (0, per_group(MOE_UNITS - 1, transpose_y))])


HEADS = 16
HEAD_D = C // HEADS
BATCH_TILES = T // P
HEAD_GROUPS = HEADS // 4
SLOTS = 4
WIDTH = 3 * P
NUM_BUCKETS, MAX_DISTANCE = 32, 128
MASKED = -1.0e30


def attention_phase(nc, tag, banks, used, x_res, ident, neg_half, w):
    GU = 2
    U = GU * HEADS
    Z, PR = 4, 8
    SCALE = HEAD_D ** -0.5
    with ExitStack() as ctx:
        def sb(name, shape, dt=F32):
            return ctx.enter_context(nc.sbuf_tensor(f"{tag}_{name}", shape, dt))

        bank = bank_taker(banks)

        def sem(name):
            return new_sem(nc, used, f"{tag}_{name}")

        stats = sb("stats", [P, GU, BATCH_TILES, 6])
        mv = sb("mv", [P, GU, BATCH_TILES, 2])
        var_eps = sb("var_eps", [P, GU, BATCH_TILES])
        rstd = sb("rstd", [P, GU, BATCH_TILES])
        xn = sb("xn", [P, BATCH_TILES, C])
        xnT = sb("xnT", [P, GU, T])
        v_aug = sb("v_aug", [P, GU, BATCH_TILES, HEADS, 32])
        qk_f = sb("qk_f", [P, 2, 2, T])
        qk_hi = sb("qk_hi", [P, 2, 2, T])
        stack = sb("stack", [P, GU, HEAD_GROUPS, 2, T], F32R)
        z = sb("z", [P, Z, WIDTH])
        top = sb("top", [P, Z, BATCH_TILES])
        prob = sb("prob", [P, PR, WIDTH])
        avT = sb("avT", [P, 2, T])
        inv = sb("inv", [P, 2, BATCH_TILES, 4])
        y = sb("y", [P, BATCH_TILES, C])
        yT = sb("yT", [P, T])
        ps_s, ps_p = bank([P, 2, 512]), bank([P, 2, 512])
        ps_qk, ps_av, ps_heads = bank([P, 2, T]), bank([P, 512])[:, 0:T], bank([P, 512])
        ps_heads = ps_heads[:, 0:T].rearrange("p (j i d) -> p j i d", j=BATCH_TILES, d=32)
        ps_f = bank([P, 512])
        ps_x = ps_v = ps_yT = ps_out = ps_f[:, 0:T]

        ones_set = sem("ones_set")
        stats_done, aggr_done, eps_added, rstd_done, xn_ready = (sem(n) for n in ("stats_done", "aggr_done", "eps_added", "rstd_done", "xn_ready"))
        xn_transposed, xnT_ready, v_projected, v_ready = (sem(n) for n in ("xn_transposed", "xnT_ready", "v_projected", "v_ready"))
        qk_projected, qk_copied, qk_hi_done, stack_ready = (sem(n) for n in ("qk_projected", "qk_copied", "qk_hi_done", "stack_ready"))
        scores_ready, biased_done, shifted0, shifted1 = (sem(n) for n in ("scores_ready", "biased_done", "shifted0", "shifted1"))
        z_transposed, prob_ready, av_done, avT_ready, inv_done, y_ready = (sem(n) for n in ("z_transposed", "prob_ready", "av_done", "avT_ready", "inv_done", "y_ready"))
        heads_transposed = sem("heads_transposed")
        y_transposed, yT_ready, out_ready, x_updated = (sem(n) for n in ("y_transposed", "yT_ready", "out_ready", "x_updated"))

        block = ctx.enter_context(nc.Block())

        def unit(it, k, back=0):
            return it * U + (k + 1 - back)

        def seq(it, k, back=0):
            return it * GU + (k // HEADS + 1 - back)

        def wait_free(engine, semaphore, value):
            if not isinstance(value, int) or value > 0:
                engine.wait_ge(semaphore, value)

        def per_seq(at, emit):
            def stage(it, k):
                if k % HEADS == at:
                    emit(it, k)
            return stage

        def x_seq(it, k):
            return x_res[:, bass.ds((it * GU + k // HEADS) * BATCH_TILES, BATCH_TILES), :]

        def head_groups(emit, leads):
            return [(lead, per_seq(0, lambda it, k, hg=hg: emit(it, k, hg))) for hg, lead in enumerate(leads)]

        def per_four(emit):
            def stage(it, k):
                if k % 4 == 3:
                    emit(it, k)
            return stage

        def fours(it, k, back=0):
            return it * (U // 4) + (k // 4 + 1 - back)

        def hg_count(it, k, hg, back=0):
            return (it * GU + k // HEADS) * HEAD_GROUPS + (hg + 1 - back)

        @block.vector
        def _(dve):
            dve.memset(v_aug[:, :, :, :, HEAD_D:HEAD_D + 1], 1.0)
            dve.memset(v_aug[:, :, :, :, HEAD_D + 1:], 0.0)

            def layernorm(it, k):
                p = k // HEADS % GU
                xs = x_seq(it, k)
                for j in range(BATCH_TILES):
                    last = dve.bn_stats(stats[:, p, j, :], xs[:, j, :])
                last.then_inc(stats_done, 1)
                dve.wait_ge(stats_done, seq(it, k))
                dve.nop(nofuse=True)
                for j in range(BATCH_TILES):
                    last = dve.bn_aggr(mv[:, p, j, :], stats[:, p, j, :])
                last.then_inc(aggr_done, 1)

            def normalise(it, k):
                p = k // HEADS % GU
                xs = x_seq(it, k)
                dve.wait_ge(rstd_done, seq(it, k))
                wait_free(dve, xn_transposed, seq(it, k, 1))
                for j in range(BATCH_TILES):
                    last = dve.tensor_scalar(xn[:, j, :], xs[:, j, :], mv[:, p, j, 0:1], rstd[:, p, j:j + 1],
                                             ALU.subtract, ALU.mult)
                last.then_inc(xn_ready, 1)

            def add_v_bias(it, k):
                p = k // HEADS % GU
                dve.wait_ge(v_projected, seq(it, k))
                wait_free(dve, av_done, (it * GU + k // HEADS - 1) * HEAD_GROUPS)
                for j in range(BATCH_TILES):
                    last = dve.tensor_tensor(v_aug[:, p, j, :, 0:HEAD_D],
                                             ps_v[:, j * C:(j + 1) * C].rearrange("p (h d) -> p h d", d=HEAD_D),
                                             w["v_bias"][:, :].rearrange("p (h d) -> p h d", d=HEAD_D), ALU.add)
                last.then_inc(v_ready, 1)

            def mask_hi(it, k, hg):
                r = hg % 2
                dve.wait_ge(qk_copied, hg_count(it, k, hg))
                wait_free(dve, stack_ready, hg_count(it, k, hg, 2))
                for i in range(2):
                    last = dve.tensor_scalar(qk_hi[:, r, i, :].bitcast(F32R), qk_f[:, r, i, :], w["lo_slots"][:, i:i + 1], None, ALU.mult)
                last.then_inc(qk_hi_done, 1)

            def bias_and_max(it, k):
                h = k % HEADS
                dve.wait_ge(scores_ready, unit(it, k))
                wait_free(dve, z_transposed, unit(it, k, Z))
                dve.nop(nofuse=True)
                for j, cols in enumerate((slice(0, P), slice(P, WIDTH))):
                    last = dve.tensor_tensor_reduce(out=z[:, k % Z, cols], in0=ps_s[:, k % 2, cols], in1=w["rel_bias"][:, h, cols],
                                                    scale=1.0, scalar=-3.0e38, op0=ALU.add, op1=ALU.max,
                                                    accum_out=top[:, k % Z, j:j + 1])
                last.then_inc(biased_done, 1)

            def shift_tile0(it, k):
                dve.wait_ge(biased_done, unit(it, k))
                dve.tensor_scalar(z[:, k % Z, 0:P], z[:, k % Z, 0:P], top[:, k % Z, 0:1], None, ALU.subtract).then_inc(shifted0, 1)

            def divide(it, k):
                r, hg = k // 4 % 2, k % HEADS // 4
                dve.wait_ge(heads_transposed, fours(it, k))
                dve.reciprocal(inv[:, r], ps_heads[:, :, :, HEAD_D]).then_inc(inv_done, 1)
                dve.wait_ge(inv_done, fours(it, k))
                if hg == 0:
                    wait_free(dve, y_transposed, seq(it, k, 1))
                dve.tensor_tensor(y[:, :, 4 * hg * HEAD_D:4 * (hg + 1) * HEAD_D].rearrange("p j (i d) -> p j i d", d=HEAD_D),
                                  ps_heads[:, :, :, 0:HEAD_D],
                                  inv[:, r].unsqueeze(3).to_broadcast([P, BATCH_TILES, 4, HEAD_D]), ALU.mult).then_inc(y_ready, 1)

            def residual(it, k):
                dve.wait_ge(out_ready, seq(it, k))
                xs = x_seq(it, k).rearrange("p j c -> p (j c)")
                dve.tensor_tensor(xs, ps_out, xs, ALU.add).then_inc(x_updated, 1)

            software_pipeline(dve, BATCHES // GU, U, [
                (29, per_seq(0, layernorm)), (27, per_seq(0, normalise)), (24, per_seq(0, add_v_bias)),
                *head_groups(mask_hi, (22, 20, 18, 16)), (11, bias_and_max), (10, shift_tile0),
                (4, per_four(divide)), (1, per_seq(HEADS - 1, residual))])

        @block.gpsimd
        def _(pool):
            def inverse_std(it, k):
                p = k // HEADS % GU
                pool.wait_ge(aggr_done, seq(it, k))
                pool.nop(nofuse=True)
                pool.tensor_scalar(var_eps[:, p, :], mv[:, p, :, 1], LN_EPS, None, ALU.add).then_inc(eps_added, 1)
                pool.wait_ge(eps_added, seq(it, k))
                pool.tensor_tensor(rstd[:, p, :], var_eps[:, p, :], neg_half[:, 0:BATCH_TILES], ALU.pow).then_inc(rstd_done, 1)

            def fill_stack(it, k, hg):
                p = k // HEADS % GU
                pool.wait_ge(qk_hi_done, hg_count(it, k, hg))
                wait_free(pool, scores_ready, (it * GU + k // HEADS - 1) * HEADS + 1)
                pool.tensor_tensor(stack[:, p, hg], qk_f[:, hg % 2], qk_hi[:, hg % 2], ALU.subtract).then_inc(stack_ready, 1)

            def shift_tile1(it, k):
                pool.wait_ge(biased_done, unit(it, k))
                pool.tensor_tensor(z[:, k % Z, P:WIDTH], z[:, k % Z, P:WIDTH],
                                   top[:, k % Z, 1:2].to_broadcast([P, WIDTH - P]), ALU.subtract).then_inc(shifted1, 1)

            software_pipeline(pool, BATCHES // GU, U, [
                (29, per_seq(0, inverse_std)), *head_groups(fill_stack, (21, 19, 17, 15)), (11, shift_tile1)])

        @block.scalar
        def _(act):
            def copy_xT(it, k):
                act.wait_ge(xn_transposed, seq(it, k))
                act.copy(xnT[:, k // HEADS % GU, :], ps_x).then_inc(xnT_ready, 1)

            def copy_qk(it, k, hg):
                r = hg % 2
                act.wait_ge(qk_projected, hg_count(it, k, hg))
                wait_free(act, stack_ready, hg_count(it, k, hg, 2))
                act.activation(qk_f[:, r, 0, :], ps_qk[:, 0, :], ACT.Identity, bias=w["q_bias"][:, hg:hg + 1], scale=SCALE)
                act.activation(qk_f[:, r, 1, :], ps_qk[:, 1, :], ACT.Identity, bias=w["k_bias"][:, hg:hg + 1]).then_inc(qk_copied, 1)

            def exponent(it, k):
                act.wait_ge(z_transposed, unit(it, k))
                wait_free(act, av_done, fours(it, k - PR))
                act.activation(prob[:, k % PR, :], ps_p[:, k % 2, 0:WIDTH], ACT.Exp).then_inc(prob_ready, 1)

            def copy_avT(it, k):
                act.wait_ge(av_done, fours(it, k))
                wait_free(act, heads_transposed, fours(it, k, 2))
                act.copy(avT[:, k // 4 % 2, :], ps_av).then_inc(avT_ready, 1)

            def copy_yT(it, k):
                act.wait_ge(y_transposed, seq(it, k))
                wait_free(act, out_ready, seq(it, k, 1))
                act.copy(yT[:, :], ps_yT).then_inc(yT_ready, 1)

            software_pipeline(act, BATCHES // GU, U, [
                (26, per_seq(0, copy_xT)), *head_groups(copy_qk, (23, 21, 19, 17)), (8, exponent), (6, per_four(copy_avT)),
                (2, per_seq(HEADS - 1, copy_yT))])

        @block.tensor
        def _(pe):
            def transpose_x(it, k):
                pe.wait_ge(xn_ready, seq(it, k))
                wait_free(pe, x_updated, seq(it, k, 3))
                for j in range(BATCH_TILES):
                    last = pe.transpose(ps_x[:, j * P:(j + 1) * P], xn[:, j, :], ident[:, :])
                last.then_inc(xn_transposed, 1)

            def project_v(it, k):
                p = k // HEADS % GU
                pe.wait_ge(xnT_ready, seq(it, k))
                for j in range(BATCH_TILES):
                    last = pe.matmul(ps_v[:, j * C:(j + 1) * C], xnT[:, p, j * P:(j + 1) * P], w["v_w"][:, :], start=True, stop=True)
                last.then_inc(v_projected, 1)

            def project_qk(it, k, hg):
                p = k // HEADS % GU
                wait_free(pe, qk_copied, hg_count(it, k, hg, 1))
                pe.matmul(ps_qk[:, 0, :], w["q_w"][:, hg, :], xnT[:, p, :], start=True, stop=True)
                pe.matmul(ps_qk[:, 1, :], w["k_w"][:, hg, :], xnT[:, p, :], start=True, stop=True).then_inc(qk_projected, 1)

            def scores(it, k):
                p, h = k // HEADS % GU, k % HEADS
                hg, rows = h // 4, slice(32 * (h % 4), 32 * (h % 4) + 32)
                if h % 4 == 0:
                    pe.wait_ge(stack_ready, hg_count(it, k, hg))
                wait_free(pe, biased_done, unit(it, k, 2))
                q, kk = stack[rows, p, hg, 0, :], stack[rows, p, hg, 1, :]
                pe.matmul(ps_s[:, k % 2, 0:P], q[:, 0:P], kk[:, 0:P], start=True, stop=True)
                pe.matmul(ps_s[:, k % 2, P:WIDTH], q[:, P:T], kk[:, :], start=True, stop=True).then_inc(scores_ready, 1)

            def transpose_z(it, k):
                pe.wait_ge(shifted0, unit(it, k))
                pe.wait_ge(shifted1, unit(it, k))
                wait_free(pe, prob_ready, unit(it, k, 2))
                for j in range(3):
                    last = pe.transpose(ps_p[:, k % 2, j * P:(j + 1) * P], z[:, k % Z, j * P:(j + 1) * P], ident[:, :])
                last.then_inc(z_transposed, 1)

            def attend(it, k):
                p, hg = k // HEADS % GU, k % HEADS // 4
                pe.wait_ge(prob_ready, unit(it, k))
                if hg == 0:
                    pe.wait_ge(v_ready, seq(it, k))
                wait_free(pe, avT_ready, fours(it, k, 1))
                for i in range(4):
                    pr, rows = prob[:, (k - 3 + i) % PR, :], slice(32 * i, 32 * i + 32)
                    pe.matmul(ps_av[rows, :], v_aug[:, p, 0, 4 * hg + i, :], pr[:, 0:T], start=True, stop=False, skip_group_check=True)
                for i in range(4):
                    pr, rows = prob[:, (k - 3 + i) % PR, :], slice(32 * i, 32 * i + 32)
                    last = pe.matmul(ps_av[rows, P:T], v_aug[:, p, 1, 4 * hg + i, :], pr[:, T:], start=False, stop=True, skip_group_check=True)
                last.then_inc(av_done, 1)

            def transpose_heads(it, k):
                pe.wait_ge(avT_ready, fours(it, k))
                wait_free(pe, y_ready, fours(it, k, 1))
                for j in range(BATCH_TILES):
                    last = pe.transpose(ps_heads[:, j].rearrange("p i d -> p (i d)"), avT[:, k // 4 % 2, j * P:(j + 1) * P], ident[:, :])
                last.then_inc(heads_transposed, 1)

            def transpose_y(it, k):
                pe.wait_ge(y_ready, fours(it, k))
                ahead = seq(it, k, -2)
                pe.wait_ge(v_ready, min(ahead, BATCHES) if isinstance(ahead, int) else ahead)
                for j in range(BATCH_TILES):
                    last = pe.transpose(ps_yT[:, j * P:(j + 1) * P], y[:, j, :], ident[:, :])
                last.then_inc(y_transposed, 1)

            def project_out(it, k):
                pe.wait_ge(yT_ready, seq(it, k))
                for j in range(BATCH_TILES):
                    out = ps_out[:, j * C:(j + 1) * C]
                    pe.matmul(out, yT[:, j * P:(j + 1) * P], w["proj_w"][:, :], start=True, stop=False)
                    last = pe.matmul(out, w["ones_row"][:, :], w["proj_bias"][:, :], start=False, stop=True)
                last.then_inc(out_ready, 1)

            software_pipeline(pe, BATCHES // GU, U, [
                (26, per_seq(0, transpose_x)), (25, per_seq(0, project_v)), *head_groups(project_qk, (23, 21, 19, 17)),
                (11, scores), (8, transpose_z), (6, per_four(attend)), (5, per_four(transpose_heads)), (3, per_seq(HEADS - 1, transpose_y)), (2, per_seq(HEADS - 1, project_out))])


def bucket_one_hot():
    import math
    import numpy as np
    dist = T - 1 - np.arange(2 * T)
    rp = np.maximum(dist, 0)
    exact = NUM_BUCKETS // 2
    large = exact + (np.log(np.maximum(rp, 1).astype(np.float32) / np.float32(exact)) / np.float32(math.log(MAX_DISTANCE / exact))
                     * np.float32(NUM_BUCKETS - exact)).astype(np.int32)
    bucket = np.where(rp < exact, rp, np.minimum(large, NUM_BUCKETS - 1))
    hot = (np.arange(NUM_BUCKETS)[:, None] == bucket[None]) & (dist >= 0)
    return np.concatenate([hot.astype(np.float32), np.where(dist < 0, MASKED, 0.0).astype(np.float32)[None]])


def prepare_attention(nc, d, banks, used, sb, scratch):
    q_w, k_w = sb("q_w", [P, HEAD_GROUPS, P]), sb("k_w", [P, HEAD_GROUPS, P])
    v_w, proj_w = sb("v_w", [P, C]), sb("proj_w", [P, C])
    qk_bias, lo_slots = sb("qk_bias", [P, 2, HEAD_GROUPS]), sb("lo_slots", [P, 2])
    v_bias, proj_bias, ones_row = sb("v_bias", [P, C]), sb("proj_bias", [1, C]), sb("ones_row", [1, P])
    rel_bias = sb("rel_bias", [P, HEADS, WIDTH])
    with ExitStack() as c2:
        table = c2.enter_context(nc.sbuf_tensor("bias_table", [NUM_BUCKETS + 1, HEADS], F32))
        hot = c2.enter_context(nc.sbuf_tensor("bias_hot", [NUM_BUCKETS + 1, 2 * T], F32))
        flip = c2.enter_context(nc.sbuf_tensor("bias_flip", [P, P], F32))
        by_distance = c2.enter_context(nc.sbuf_tensor("bias_by_distance", [HEADS, 2 * T], F32))
        reversed_rows = c2.enter_context(nc.sbuf_tensor("bias_reversed", [P, HEADS, WIDTH], F32))
        bank = bank_taker(banks)
        ps, ps_d = bank([P, 4, 512]), bank([HEADS, 2 * T])
        loaded, ready, copied, stored, spread, flipped, done, others = (
            new_sem(nc, used, f"bias_{n}") for n in ("loaded", "ready", "copied", "stored", "spread", "flipped", "done", "others"))
        block = c2.enter_context(nc.Block())
        flat = HEADS * WIDTH
        chunks = flat // 512
        rows = reversed_rows[:, :, :].rearrange("p h w -> p (h w)")
        out = rel_bias[:, :, :].rearrange("p h w -> p (h w)")

        @block.sync
        def _(sync):
            sync.dma_start(table[:, :], d["bias_table"]).then_inc(loaded, 16)
            sync.dma_start(hot[:, :], d["bias_hot"]).then_inc(loaded, 16)
            sync.dma_start(flip[:, :], d["flip"]).then_inc(loaded, 16)
            sync.wait_ge(copied, 1)
            sync.dma_start(scratch, by_distance[:, :]).then_inc(stored, 16)
            sync.wait_ge(stored, 16)
            sync.dma_start(reversed_rows[:, :, P:WIDTH], bass.AP(scratch.tensor, scratch.offset, [[1, P], [2 * T, HEADS], [1, T]])).then_inc(spread, 16)
            sync.dma_start(reversed_rows[:, :, 0:P], bass.AP(scratch.tensor, scratch.offset + P, [[1, P], [2 * T, HEADS], [1, P]])).then_inc(spread, 16)

        @block.scalar
        def _(act):
            for dst, name in ((q_w[:, :, :].rearrange("p g m -> p (g m)"), "q_w"), (k_w[:, :, :].rearrange("p g m -> p (g m)"), "k_w"),
                              (v_w[:, :], "v_w"), (proj_w[:, :], "proj_w"), (qk_bias[:, :, :].rearrange("p i g -> p (i g)"), "qk_bias"),
                              (lo_slots[:, :], "lo_slots"), (v_bias[:, :], "v_bias"), (proj_bias[:, :], "proj_bias"), (ones_row[:, :], "ones_row")):
                act.dma_start(dst, d[name]).then_inc(others, 16)
            act.wait_ge(others, 9 * 16)
            act.mul(qk_bias[:, 0, :], qk_bias[:, 0, :], HEAD_D ** -0.5)
            act.wait_ge(ready, 1)
            act.copy(by_distance[:, :], ps_d[:, :]).then_inc(copied, 1)
            for n in range(chunks):
                act.wait_ge(flipped, n + 1)
                act.copy(out[:, n * 512:(n + 1) * 512], ps[:, n % 4, :]).then_inc(done, 1)

        @block.tensor
        def _(pe):
            pe.wait_ge(loaded, 48)
            pe.matmul(ps_d[:, :], table[:, :], hot[:, :], start=True, stop=True).then_inc(ready, 1)
            pe.wait_ge(spread, 32)
            for n in range(chunks):
                if n >= 4:
                    pe.wait_ge(done, n - 3)
                pe.matmul(ps[:, n % 4, :], flip[:, :], rows[:, n * 512:(n + 1) * 512], start=True, stop=True).then_inc(flipped, 1)
    return dict(q_w=q_w, k_w=k_w, v_w=v_w, proj_w=proj_w, q_bias=qk_bias[:, 0, :], k_bias=qk_bias[:, 1, :], lo_slots=lo_slots,
                v_bias=v_bias, proj_bias=proj_bias, ones_row=ones_row, rel_bias=rel_bias)


RET_H, RET_D, RET_V = 8, 64, 128
RET_PAIRS = RET_H // 2
VG_JOBS = 8


def retention_phase(nc, tag, banks, used, x_res, ident, neg_half, w):
    GU = 4
    U = GU * RET_H
    RING = 4
    with ExitStack() as ctx:
        def sb(name, shape, dt=F32):
            return ctx.enter_context(nc.sbuf_tensor(f"{tag}_{name}", shape, dt))

        bank = bank_taker(banks)

        def sem(name):
            return new_sem(nc, used, f"{tag}_{name}")

        stats = sb("stats", [P, 2, BATCH_TILES, 6])
        mv = sb("mv", [P, 2, BATCH_TILES, 2])
        var_eps = sb("var_eps", [P, 2, BATCH_TILES])
        rstd = sb("rstd", [P, 2, BATCH_TILES])
        xn = sb("xn", [P, BATCH_TILES, C])
        x_hi, x_lo = sb("x_hi", [P, 2, T], F32R), sb("x_lo", [P, 2, T], F32R)
        turned = sb("turned", [P, 2, 2, T])
        rotated = sb("rotated", [P, RING, 2, T])
        value = sb("value", [P, 2, BATCH_TILES, RET_H, RET_V])
        gate = sb("gate", [P, 2, BATCH_TILES, RET_H, RET_V])
        decayed = sb("decayed", [P, 2, WIDTH])
        head_stats = sb("head_stats", [P, RING, BATCH_TILES, 6])
        head_mv = sb("head_mv", [P, RING, BATCH_TILES, 2])
        head_var = sb("head_var", [P, RING, BATCH_TILES])
        head_rstd = sb("head_rstd", [P, RING, BATCH_TILES])
        normed = sb("normed", [P, RING, BATCH_TILES, RET_V])
        weighted = sb("weighted", [P, 2, BATCH_TILES, RET_V])
        affine = sb("affine", [P, RING, BATCH_TILES, RET_V])
        zT = sb("zT", [P, BATCH_TILES, RET_H, P])
        ps_r, ps_s, ps_o = bank([P, 2, 2, T]), bank([P, 2, 512]), bank([P, 2, 512])
        ps_g = bank([P, 512])
        ps_f = bank([P, 512])
        ps_x = ps_out = ps_f[:, 0:T]

        stats_done, aggr_done, eps_added, rstd_done, xn_ready = (sem(n) for n in ("stats_done", "aggr_done", "eps_added", "rstd_done", "xn_ready"))
        xn_transposed, x_hi_ready, x_split = sem("xn_transposed"), sem("x_hi_ready"), sem("x_split")
        rot_projected, turned_ready, rotated_ready = sem("rot_projected"), sem("turned_ready"), sem("rotated_ready")
        vg_projected, vg_ready = sem("vg_projected"), sem("vg_ready")
        scores_ready, decayed_ready, heads_ready = sem("scores_ready"), sem("decayed_ready"), sem("heads_ready")
        head_stats_done, head_aggr_done, head_eps_added, head_rstd_done = (sem(n) for n in ("head_stats_done", "head_aggr_done", "head_eps_added", "head_rstd_done"))
        normed_ready, weighted_done, affine_ready, gated_ready = (sem(n) for n in ("normed_ready", "weighted_done", "affine_ready", "gated_ready"))
        z_transposed, zT_ready, out_ready, x_updated = (sem(n) for n in ("z_transposed", "zT_ready", "out_ready", "x_updated"))

        block = ctx.enter_context(nc.Block())

        def unit(it, k, back=0):
            return it * U + (k + 1 - back)

        def seq(it, k, back=0):
            return it * GU + (k // RET_H + 1 - back)

        def wait_free(engine, semaphore, value):
            if not isinstance(value, int) or value > 0:
                engine.wait_ge(semaphore, value)

        def per_seq(at, emit):
            def stage(it, k):
                if k % RET_H == at:
                    emit(it, k)
            return stage

        def pieces(tile, emit):
            def stage(it, k):
                if k % 4 == 3:
                    emit(it, k, tile)
            return stage

        def piece(it, k, tile, back=0):
            return (it * (U // 4) + k // 4) * BATCH_TILES + (tile + 1 - back)

        def x_seq(it, k):
            return x_res[:, bass.ds((it * GU + k // RET_H) * BATCH_TILES, BATCH_TILES), :]

        @block.vector
        def _(dve):
            def layernorm(it, k):
                p = k // RET_H % 2
                xs = x_seq(it, k)
                for j in range(BATCH_TILES):
                    last = dve.bn_stats(stats[:, p, j, :], xs[:, j, :])
                last.then_inc(stats_done, 1)
                dve.wait_ge(stats_done, seq(it, k))
                dve.nop(nofuse=True)
                for j in range(BATCH_TILES):
                    last = dve.bn_aggr(mv[:, p, j, :], stats[:, p, j, :])
                last.then_inc(aggr_done, 1)

            def normalise(it, k):
                p = k // RET_H % 2
                xs = x_seq(it, k)
                dve.wait_ge(rstd_done, seq(it, k))
                wait_free(dve, xn_transposed, seq(it, k, 1))
                for j in range(BATCH_TILES):
                    last = dve.tensor_scalar(xn[:, j, :], xs[:, j, :], mv[:, p, j, 0:1], rstd[:, p, j:j + 1],
                                             ALU.subtract, ALU.mult)
                last.then_inc(xn_ready, 1)

            def split_x(it, k):
                p = k // RET_H % 2
                dve.wait_ge(x_hi_ready, seq(it, k))
                dve.tensor_tensor(x_lo[:, p, :], ps_x, x_hi[:, p, :].bitcast(F32), ALU.subtract).then_inc(x_split, 1)

            def turn(it, k):
                dve.wait_ge(rot_projected, unit(it, k))
                wait_free(dve, rotated_ready, unit(it, k, 2))
                dve.tensor_tensor(turned[:, k % 2], ps_r[:, k % 2], w["cos_sin"][:, :, :], ALU.mult).then_inc(turned_ready, 1)

            def decay(it, k):
                dve.wait_ge(scores_ready, unit(it, k))
                wait_free(dve, heads_ready, unit(it, k, 2))
                dve.tensor_tensor(decayed[:, k % 2, :], ps_s[:, k % 2, 0:WIDTH], w["decay"][:, k % RET_H, :],
                                  ALU.mult).then_inc(decayed_ready, 1)

            def head_statistics(it, k):
                r = k % RING
                dve.wait_ge(heads_ready, unit(it, k))
                for j in range(BATCH_TILES):
                    last = dve.bn_stats(head_stats[:, r, j, :], ps_o[:, k % 2, j * RET_V:(j + 1) * RET_V])
                last.then_inc(head_stats_done, 1)
                dve.wait_ge(head_stats_done, unit(it, k))
                dve.nop(nofuse=True)
                for j in range(BATCH_TILES):
                    last = dve.bn_aggr(head_mv[:, r, j, :], head_stats[:, r, j, :])
                last.then_inc(head_aggr_done, 1)

            def normalise_head(it, k):
                r = k % RING
                dve.wait_ge(head_rstd_done, unit(it, k))
                wait_free(dve, weighted_done, unit(it, k, RING))
                for j in range(BATCH_TILES):
                    last = dve.tensor_scalar(normed[:, r, j, :], ps_o[:, k % 2, j * RET_V:(j + 1) * RET_V], head_mv[:, r, j, 0:1],
                                             head_rstd[:, r, j:j + 1], ALU.subtract, ALU.mult)
                last.then_inc(normed_ready, 1)

            def gate_head(it, k):
                p, h = k // RET_H % 2, k % RET_H
                dve.wait_ge(affine_ready, unit(it, k))
                if h % 4 == 0:
                    dve.wait_ge(vg_ready, (it * GU + k // RET_H) * VG_JOBS + 6 + 2 * (h // 4))
                dve.tensor_tensor(gate[:, p, :, h, :], affine[:, k % RING], gate[:, p, :, h, :], ALU.mult).then_inc(gated_ready, 1)

            def residual(it, k):
                dve.wait_ge(out_ready, seq(it, k))
                xs = x_seq(it, k).rearrange("p j c -> p (j c)")
                dve.tensor_tensor(xs, ps_out, xs, ALU.add).then_inc(x_updated, 1)

            software_pipeline(dve, BATCHES // GU, U, [
                (22, per_seq(0, layernorm)), (18, per_seq(0, split_x)), (15, turn), (10, decay), (8, head_statistics),
                (7, normalise_head), (6, gate_head), (21, per_seq(0, normalise)), (0, per_seq(RET_H - 1, residual))])

        @block.gpsimd
        def _(pool):
            def inverse_std(it, k):
                p = k // RET_H % 2
                pool.wait_ge(aggr_done, seq(it, k))
                pool.nop(nofuse=True)
                pool.tensor_scalar(var_eps[:, p, :], mv[:, p, :, 1], LN_EPS, None, ALU.add).then_inc(eps_added, 1)
                pool.wait_ge(eps_added, seq(it, k))
                pool.tensor_tensor(rstd[:, p, :], var_eps[:, p, :], neg_half[:, 0:BATCH_TILES], ALU.pow).then_inc(rstd_done, 1)

            def rotate(it, k):
                pool.wait_ge(turned_ready, unit(it, k))
                wait_free(pool, scores_ready, unit(it, k // 2 * 2 + 1, 2 * RING))
                pool.tensor_tensor(rotated[:, k // 2 % RING, k % 2, :], turned[:, k % 2, 0, :], turned[:, k % 2, 1, :],
                                   ALU.add).then_inc(rotated_ready, 1)

            def inverse_head_std(it, k):
                r = k % RING
                pool.wait_ge(head_aggr_done, unit(it, k))
                pool.nop(nofuse=True)
                pool.tensor_scalar(head_var[:, r, :], head_mv[:, r, :, 1], LN_EPS, None, ALU.add).then_inc(head_eps_added, 1)
                pool.wait_ge(head_eps_added, unit(it, k))
                pool.tensor_tensor(head_rstd[:, r, :], head_var[:, r, :], neg_half[:, 0:BATCH_TILES], ALU.pow).then_inc(head_rstd_done, 1)

            def weigh_head(it, k):
                h = k % RET_H
                shape = [P, BATCH_TILES, RET_V]
                pool.wait_ge(normed_ready, unit(it, k))
                pool.tensor_tensor(weighted[:, k % 2], normed[:, k % RING], w["gn_weight"][:, h, :].unsqueeze(1).to_broadcast(shape),
                                   ALU.mult).then_inc(weighted_done, 1)
                pool.wait_ge(weighted_done, unit(it, k))
                wait_free(pool, gated_ready, unit(it, k, RING))
                pool.tensor_tensor(affine[:, k % RING], weighted[:, k % 2], w["gn_bias"][:, h, :].unsqueeze(1).to_broadcast(shape),
                                   ALU.add).then_inc(affine_ready, 1)

            software_pipeline(pool, BATCHES // GU, U, [
                (22, per_seq(0, inverse_std)), (15, rotate), (8, inverse_head_std), (7, weigh_head)])

        @block.scalar
        def _(act):
            def copy_x_hi(it, k):
                act.wait_ge(xn_transposed, seq(it, k))
                act.copy(x_hi[:, k // RET_H % 2, :], ps_x).then_inc(x_hi_ready, 1)

            def copy_vg(it, k):
                p, n = k // RET_H % 2, k % RET_H
                tile, half = n % 2, n // 2 % 2
                act.wait_ge(vg_projected, unit(it, k))
                if n < 4:
                    wait_free(act, heads_ready, (it * GU + k // RET_H - 1) * RET_H)
                    dst, func = value, ACT.Copy
                else:
                    wait_free(act, z_transposed, (it * GU + k // RET_H - 1) * 2 * BATCH_TILES)
                    dst, func = gate, ACT.Silu
                act.activation(dst[:, p, tile, 4 * half:4 * half + 4, :].rearrange("p h v -> p (h v)"), ps_g[:, :], func).then_inc(vg_ready, 1)

            def copy_zT(it, k, tile):
                act.wait_ge(z_transposed, piece(it, k, tile))
                half = k // 4 % 2
                if half == 0 and tile == 0:
                    wait_free(act, out_ready, seq(it, k, 1))
                act.copy(zT[:, tile, 4 * half:4 * half + 4, :].rearrange("p h t -> p (h t)"), ps_f[:, :]).then_inc(zT_ready, 1)

            software_pipeline(act, BATCHES // GU, U, [
                (18, per_seq(0, copy_x_hi)), (12, copy_vg), (3, pieces(0, copy_zT)), (2, pieces(1, copy_zT))])

        @block.tensor
        def _(pe):
            def transpose_x(it, k):
                pe.wait_ge(xn_ready, seq(it, k))
                wait_free(pe, zT_ready, (it * GU + k // RET_H - 2) * 4)
                for j in range(BATCH_TILES):
                    last = pe.transpose(ps_x[:, j * P:(j + 1) * P], xn[:, j, :], ident[:, :])
                last.then_inc(xn_transposed, 1)

            def project_rotary(it, k):
                p, n = k // RET_H % 2, k % RET_H
                if n == 0:
                    pe.wait_ge(x_split, seq(it, k))
                wait_free(pe, turned_ready, unit(it, k, 2))
                for twin in range(2):
                    column = ((n % 2) * 2 + twin) * RET_H * RET_D + n // 2 * P
                    w_hi, w_lo = (part[:, column:column + P] for part in w["projections"])
                    out = ps_r[:, k % 2, twin, :]
                    pe.matmul(out, w_hi, x_hi[:, p, :], start=True, stop=False)
                    pe.matmul(out, w_hi, x_lo[:, p, :], start=False, stop=False)
                    last = pe.matmul(out, w_lo, x_hi[:, p, :], start=False, stop=True)
                last.then_inc(rot_projected, 1)

            def project_vg(it, k):
                p, n = k // RET_H % 2, k % RET_H
                tile, half = n % 2, n // 2 % 2
                column = 4 * RET_H * RET_D + (n // 4) * RET_H * RET_V + half * 512
                w_hi, w_lo = (part[:, column:column + 512] for part in w["projections"])
                hi, lo = (part[:, p, tile * P:(tile + 1) * P] for part in (x_hi, x_lo))
                wait_free(pe, vg_ready, unit(it, k, 1))
                pe.matmul(ps_g[:, :], hi, w_hi, start=True, stop=False)
                pe.matmul(ps_g[:, :], hi, w_lo, start=False, stop=False)
                pe.matmul(ps_g[:, :], lo, w_hi, start=False, stop=True).then_inc(vg_projected, 1)

            def scores(it, k):
                r, rows = k // 2 % RING, slice(RET_D * (k % 2), RET_D * (k % 2) + RET_D)
                pe.wait_ge(rotated_ready, unit(it, k // 2 * 2 + 1))
                wait_free(pe, decayed_ready, unit(it, k, 2))
                q, kk = rotated[rows, r, 0, :], rotated[rows, r, 1, :]
                pe.matmul(ps_s[:, k % 2, 0:T], kk[:, 0:P], q, start=True, stop=True)
                pe.matmul(ps_s[:, k % 2, T:WIDTH], kk[:, P:T], q[:, P:T], start=True, stop=True).then_inc(scores_ready, 1)

            def retain(it, k):
                p, h = k // RET_H % 2, k % RET_H
                pe.wait_ge(decayed_ready, unit(it, k))
                if h % 4 == 0:
                    pe.wait_ge(vg_ready, (it * GU + k // RET_H) * VG_JOBS + 2 + 2 * (h // 4))
                wait_free(pe, normed_ready, unit(it, k, 2))
                s, out = decayed[:, k % 2, :], ps_o[:, k % 2, :]
                pe.matmul(out[:, 0:RET_V], s[:, 0:P], value[:, p, 0, h, :], start=True, stop=True)
                pe.matmul(out[:, RET_V:2 * RET_V], s[:, P:T], value[:, p, 0, h, :], start=True, stop=False)
                pe.matmul(out[:, RET_V:2 * RET_V], s[:, T:], value[:, p, 1, h, :], start=False, stop=True).then_inc(heads_ready, 1)

            def transpose_z(it, k, tile):
                pe.wait_ge(gated_ready, unit(it, k))
                first = k % RET_H == 3 and tile == 0
                if first:
                    wait_free(pe, x_updated, seq(it, k, 1))
                else:
                    pe.wait_ge(zT_ready, piece(it, k, tile, 1))
                for i in range(4):
                    last = pe.transpose(ps_f[:, i * P:(i + 1) * P], gate[:, k // RET_H % 2, tile, k % RET_H - 3 + i, :], ident[:, :])
                last.then_inc(z_transposed, 1)

            def project_out(it, k):
                pe.wait_ge(zT_ready, piece(it, k, 1))
                ahead = seq(it, k, -3)
                pe.wait_ge(x_split, min(ahead, BATCHES) if isinstance(ahead, int) else ahead)
                for j in range(BATCH_TILES):
                    for h in range(RET_H):
                        last = pe.matmul(ps_out[:, j * P:(j + 1) * P], zT[:, j, h, :], w["out_w"][:, h, :], start=(h == 0), stop=(h == RET_H - 1))
                last.then_inc(out_ready, 1)

            software_pipeline(pe, BATCHES // GU, U, [
                (18, per_seq(0, transpose_x)), (15, project_rotary), (12, project_vg), (10, scores), (8, retain),
                (3, pieces(0, transpose_z)), (2, pieces(1, transpose_z)), (0, per_seq(RET_H - 1, project_out))])


def retention_tables():
    import numpy as np
    f = np.float32
    inv_freq = f(1.0) / f(10000.0) ** (np.arange(0, RET_D, 2, dtype=f) / f(RET_D))
    freqs = np.arange(T, dtype=f)[:, None] * inv_freq[None]
    emb = np.concatenate([freqs, freqs], axis=1).T
    sign = np.where(np.arange(RET_D) < RET_D // 2, f(-1), f(1))[:, None]
    cos_sin = np.concatenate([np.tile(np.cos(emb), (2, 1)), np.tile(np.sin(emb) * sign, (2, 1))], axis=1)
    log_gamma = np.log2(f(1.0) - np.exp2(f(-5.0) - np.arange(RET_H, dtype=f)))
    n = np.arange(T, dtype=f)
    rel = n[None] - n[:, None]
    full = np.where(rel[None] >= 0, np.exp2(np.maximum(rel, 0)[None] * log_gamma[:, None, None]), f(0)) * f(RET_D ** -0.5)
    decay = np.concatenate([full[:, :P, :], full[:, P:, P:]], axis=2)
    return cos_sin.astype(f), decay.transpose(1, 0, 2).reshape(P, RET_H * WIDTH).astype(f)


def prepare_retention(nc, d, used, sb):
    columns = 4 * RET_H * RET_D + 2 * RET_H * RET_V
    hi, lo = sb("ret_hi", [P, columns], F32R), sb("ret_lo", [P, columns], F32R)
    out_w, cos_sin, decay = sb("ret_out_w", [P, RET_H, C]), sb("ret_cos_sin", [P, 2, T]), sb("ret_decay", [P, RET_H, WIDTH])
    gn_weight, gn_bias = sb("ret_gn_weight", [P, RET_H, RET_V]), sb("ret_gn_bias", [P, RET_H, RET_V])
    with ExitStack() as c2:
        parts = 4
        width = columns // parts
        stage = c2.enter_context(nc.sbuf_tensor("ret_stage", [P, columns], F32))
        loaded = [new_sem(nc, used, f"ret_loaded{i}") for i in range(parts)]
        others, hi_done = new_sem(nc, used, "ret_others"), new_sem(nc, used, "ret_hi_done")
        block = c2.enter_context(nc.Block())

        @block.sync
        def _(sync):
            for i in range(parts):
                sync.dma_start(stage[:, i * width:(i + 1) * width], d["ret_w"][:, i * width:(i + 1) * width]).then_inc(loaded[i], 16)
            for dst, name in ((out_w, "ret_out_w"), (cos_sin, "ret_cos_sin"), (decay, "ret_decay"), (gn_weight, "ret_gn_weight"), (gn_bias, "ret_gn_bias")):
                sync.dma_start(dst[:, :, :].rearrange("p a b -> p (a b)"), d[name]).then_inc(others, 16)
            sync.wait_ge(others, 5 * 16)

        @block.scalar
        def _(act):
            for i in range(parts):
                act.wait_ge(loaded[i], 16)
                act.copy(hi[:, i * width:(i + 1) * width], stage[:, i * width:(i + 1) * width]).then_inc(hi_done, 1)

        @block.vector
        def _(dve):
            for i in range(parts):
                at = slice(i * width, (i + 1) * width)
                dve.wait_ge(hi_done, i + 1)
                dve.tensor_tensor(lo[:, at], stage[:, at], hi[:, at].bitcast(F32), ALU.subtract)
    return dict(projections=(hi, lo), out_w=out_w, cos_sin=cos_sin, decay=decay, gn_weight=gn_weight, gn_bias=gn_bias)


def build(nc, d, out):
    with ExitStack() as ctx:
        def sb(name, shape, dt=F32):
            return ctx.enter_context(nc.sbuf_tensor(name, shape, dt))

        def sem(name):
            return ctx.enter_context(nc.semaphore(name))

        banks = ctx.enter_context(nc.psum_tensor("banks", [P, 8, 512], F32))
        x_res = sb("x_res", [P, TILES, C])
        ident = sb("ident", [P, P])
        neg_half = sb("neg_half", [P, 8])
        ffn_w = sb("ffn_w", [P, C + LORA_E + LORA_R])
        lora_rows = sb("lora_rows", [LORA_ROWS + 1, C])
        lora_router_b = sb("lora_router_b", [P, GROUP, LORA_E])
        x_loaded, first_loaded, out_stored, lora_scaled = sem("x_loaded"), sem("first_loaded"), sem("out_stored"), sem("lora_scaled")

        used = []
        with nc.Block() as block:
            @block.sync
            def _(sync):
                sync.dma_start(x_res[:, :, :], d["x"].rearrange("(t p) c -> p t c", p=P)).then_inc(x_loaded, 16)
                sync.wait_ge(x_loaded, 16)

            @block.gpsimd
            def _(pool):
                pool.memset(neg_half[:, :], -0.5)

            @block.scalar
            def _(act):
                act.dma_start(ident[:, :], d["ident"]).then_inc(first_loaded, 16)
                act.dma_start(ffn_w[:, :], d["ffn_w"]).then_inc(first_loaded, 16)
                act.dma_start(lora_rows[:, :], d["lora_rows"]).then_inc(first_loaded, 16)
                act.dma_start(lora_router_b[:, :, :], d["lora_router_b"].rearrange("p (t e) -> p t e", e=LORA_E)).then_inc(first_loaded, 16)
                act.wait_ge(first_loaded, 64)
                act.mul(lora_rows[0:LORA_ROWS, :], lora_rows[0:LORA_ROWS, :], LORA_SCALING)

        moe_hi, moe_lo = sb("moe_hi", [P, 3 * MOE_UNITS * MOE_F], F32R), sb("moe_lo", [P, 3 * MOE_UNITS * MOE_F], F32R)
        router_hi, router_lo = sb("router_hi", [P, MOE_E], F32R), sb("router_lo", [P, MOE_E], F32R)
        moe_bias = sb("moe_bias", [P, GROUP, MOE_E])
        before = sb("before", [P, GROUP * MOE_G, MOE_G])
        select = sb("select", [3 * MOE_E, MOE_E, P], BF16)
        ident_bf = sb("ident_bf", [P, P], BF16)

        def prepare_moe():
            with ExitStack() as c2:
                stage = c2.enter_context(nc.sbuf_tensor("moe_stage", [P, 3 * MOE_UNITS * MOE_F], F32))
                rstage = c2.enter_context(nc.sbuf_tensor("router_stage", [P, MOE_E], F32))
                sstage = c2.enter_context(nc.sbuf_tensor("select_stage", [3 * MOE_E, MOE_E * P], F32))
                parts = 3
                width = MOE_UNITS * MOE_F
                loaded = [new_sem(nc, used, f"moe_loaded{i}") for i in range(parts)]
                small = new_sem(nc, used, "moe_small")
                hi_done = new_sem(nc, used, "moe_hi_done")
                block = c2.enter_context(nc.Block())

                @block.sync
                def _(sync):
                    for i in range(parts):
                        sync.dma_start(stage[:, i * width:(i + 1) * width], d["moe_w"][:, i * width:(i + 1) * width]).then_inc(loaded[i], 16)

                @block.scalar
                def _(act):
                    act.dma_start(rstage[:, :], d["moe_router"]).then_inc(small, 16)
                    act.dma_start(sstage[:, :], d["moe_select"]).then_inc(small, 16)
                    act.dma_start(moe_bias[:, :, :], d["moe_bias"].rearrange("p (t e) -> p t e", e=MOE_E)).then_inc(small, 16)
                    act.dma_start(before[:, :, :], d["moe_before"].rearrange("p (t e) -> p t e", e=MOE_G)).then_inc(small, 16)
                    act.wait_ge(small, 64)
                    act.copy(router_hi[:, :], rstage[:, :]).then_inc(hi_done, 1)
                    act.copy(ident_bf[:, :], ident[:, :])
                    act.copy(select[:, :, :].rearrange("p e c -> p (e c)"), sstage[:, :])
                    for i in range(parts):
                        act.wait_ge(loaded[i], 16)
                        act.copy(moe_hi[:, i * width:(i + 1) * width], stage[:, i * width:(i + 1) * width]).then_inc(hi_done, 1)

                @block.vector
                def _(dve):
                    dve.wait_ge(hi_done, 1)
                    dve.tensor_tensor(router_lo[:, :], rstage[:, :], router_hi[:, :].bitcast(F32), ALU.subtract)
                    for i in range(parts):
                        dve.wait_ge(hi_done, i + 2)
                        at = slice(i * width, (i + 1) * width)
                        dve.tensor_tensor(moe_lo[:, at], stage[:, at], moe_hi[:, at].bitcast(F32), ALU.subtract)

        moe = dict(up_down=(moe_hi, moe_lo), router=(router_hi[:, :], router_lo[:, :]), bias=moe_bias, before=before, select=select)
        lora = dict(base_T=ffn_w[:, 0:C], router_a=ffn_w[:, C:], lora_rows=lora_rows[:, :], router_b=lora_router_b)
        ffn_lora_phase(nc, "ffn1", banks, used, x_res, ident, neg_half, lora)
        with ExitStack() as c2:
            attn = prepare_attention(nc, d, banks, used, lambda n, shape: c2.enter_context(nc.sbuf_tensor(n, shape, F32)), d["scratch"])
            attention_phase(nc, "attn", banks, used, x_res, ident, neg_half, attn)
        ffn_lora_phase(nc, "ffn2", banks, used, x_res, ident, neg_half, lora)
        retire(nc, used)
        prepare_moe()
        moe_phase(nc, "moe1", banks, used, x_res, ident, ident_bf, neg_half, moe)
        with ExitStack() as c2:
            ret = prepare_retention(nc, d, used, lambda n, shape, dt=F32: c2.enter_context(nc.sbuf_tensor(n, shape, dt)))
            retention_phase(nc, "ret", banks, used, x_res, ident, neg_half, ret)
        retire(nc, used)
        moe_phase(nc, "moe2", banks, used, x_res, ident, ident_bf, neg_half, moe)

        with nc.Block() as block:
            @block.sync
            def _(sync):
                sync.dma_start(out.rearrange("(t p) c -> p t c", p=P), x_res[:, :, :]).then_inc(out_stored, 16)
                sync.wait_ge(out_stored, 16)


def kernel(**inputs):
    import numpy as np
    import concourse.bacc as bacc
    from concourse.bass_utils import run_bass_kernel_spmd

    def arr(name):
        return np.asarray(inputs[name])

    host = {
        "x": arr("L0_attn_x").reshape(TILES * P, C),
        "ident": np.eye(P, dtype=np.float32),
        "ffn_w": np.concatenate([arr("L0_ffn_base_w").T, arr("L0_ffn_router_w").T, arr("L0_ffn_lora_A")], axis=1),
        "lora_rows": np.concatenate([arr("L0_ffn_lora_B").reshape(LORA_ROWS, C), arr("L0_ffn_base_b")[None]], axis=0),
        "lora_router_b": np.tile(arr("L0_ffn_router_b")[None], (P, GROUP)),
    }
    blocks = [arr("L1_ffn_gate_w").transpose(1, 0, 2).reshape(C, MOE_E * MOE_F), arr("L1_ffn_sh_gate_w"),
              arr("L1_ffn_up_w").transpose(1, 0, 2).reshape(C, MOE_E * MOE_F), arr("L1_ffn_sh_up_w"),
              arr("L1_ffn_down_w").transpose(1, 0, 2).reshape(MOE_F, MOE_E * C),
              arr("L1_ffn_sh_down_w").reshape(MOE_SHARED, MOE_F, C).transpose(1, 0, 2).reshape(MOE_F, MOE_SHARED * C)]
    host["moe_w"] = np.concatenate(blocks, axis=1)
    host["moe_router"] = arr("L1_ffn_router_w").T
    host["moe_bias"] = np.tile(arr("L1_ffn_bias")[None], (P, GROUP))
    host["moe_before"] = np.tile(np.tril(np.ones((MOE_G, MOE_G), np.float32), -1).reshape(1, -1), (P, GROUP))
    host["moe_select"] = np.tile(np.repeat(np.eye(MOE_E, dtype=np.float32), P, axis=1), (3, 1))
    wa, ba = arr("L0_attn_W_attn"), arr("L0_attn_b_attn")

    def stacked(a):
        a = a.reshape(-1, HEAD_GROUPS, 4, 1, HEAD_D)
        return np.tile(a, (1, 1, 1, SLOTS, 1)).reshape(a.shape[0], HEAD_GROUPS * P)

    host["q_w"], host["k_w"], host["v_w"] = stacked(wa[:, 0:C]), stacked(wa[:, C:2 * C]), wa[:, 2 * C:]
    host["qk_bias"] = np.concatenate([stacked(ba[None, i * C:(i + 1) * C]).reshape(HEAD_GROUPS, P).T for i in range(2)], axis=1)
    slot = np.arange(P) // HEAD_D % SLOTS
    host["lo_slots"] = np.stack([slot // 2, slot % 2], axis=1).astype(np.float32)
    host["v_bias"] = np.tile(ba[None, 2 * C:], (P, 1))
    host["proj_w"], host["proj_bias"] = arr("L0_attn_W_proj"), arr("L0_attn_b_proj")[None]
    host["ones_row"] = np.ones((1, P), np.float32)
    host["bias_table"] = np.concatenate([arr("L0_attn_bias_table"), np.ones((1, HEADS), np.float32)])
    host["bias_hot"] = bucket_one_hot()
    host["flip"] = np.eye(P, dtype=np.float32)[::-1]
    def swapped(a):
        return a.reshape(RET_H, 2, RET_D // 2, C)[:, ::-1].reshape(RET_H * RET_D, C)

    wq, wk = arr("L1_attn_Wq"), arr("L1_attn_Wk")
    host["ret_w"] = np.concatenate([wq, swapped(wq), wk, swapped(wk), arr("L1_attn_Wv"), arr("L1_attn_Wg")]).T
    host["ret_out_w"] = arr("L1_attn_Wo").reshape(C, RET_H, RET_V).transpose(2, 1, 0).reshape(RET_V, RET_H * C)
    host["ret_gn_weight"], host["ret_gn_bias"] = (np.tile(arr(n)[None], (P, 1)) for n in ("L1_attn_gn_weight", "L1_attn_gn_bias"))
    host["ret_cos_sin"], host["ret_decay"] = retention_tables()
    host = {k: np.ascontiguousarray(v) for k, v in host.items()}
    nc = bacc.Bacc("TRN2", target_bir_lowering=False, num_devices=1)
    dram = {k: nc.dram_tensor(f"in_{k}", list(v.shape), F32, kind="ExternalInput").ap() for k, v in host.items()}
    out = nc.dram_tensor("out", [TILES * P, C], F32, kind="ExternalOutput").ap()
    dram["scratch"] = nc.dram_tensor("scratch", [HEADS, 2 * T], F32).ap()
    build(nc, dram, out)
    r = run_bass_kernel_spmd(nc, [{f"in_{k}": v for k, v in host.items()}], core_ids=[0])
    return r.results[0]["out"].reshape(BATCHES, T, C)
```

```python
from contextlib import ExitStack

import concourse.bass as bass
from concourse import mybir

P = 128
F32 = mybir.dt.float32
F32R = mybir.dt.float32r
BF16 = mybir.dt.bfloat16
ALU = mybir.AluOpType
ACT = mybir.ActivationFunctionType
AX = mybir.AxisListType

BATCHES, T, C = 16, 256, 128
TILES = BATCHES * T // P
LN_EPS = 1e-5

GROUP = 4
GROUPS = TILES // GROUP
GT = GROUP * P
FIRST_GROUPS = 2

LORA_E, LORA_R = 8, 8
LORA_ROWS = LORA_E * LORA_R
LORA_SCALING = 2.0


def software_pipeline(engine, iterations, units, stages):
    most = max(lead for lead, _ in stages)
    assert most <= units
    for step in range(-most, 0):
        for lead, emit in stages:
            if step + lead >= 0:
                emit((step + lead) // units, (step + lead) % units)
    if iterations > 1:
        with engine.Fori(0, iterations - 1) as it:
            for step in range(units):
                for lead, emit in stages:
                    emit(it + (step + lead) // units, (step + lead) % units)
    for step in range(units):
        for lead, emit in stages:
            if step + lead < units:
                emit(iterations - 1, step + lead)


def new_sem(nc, used, name):
    used.append(nc.alloc_semaphore(name=name))
    return used[-1]


def retire(nc, used):
    nc.clear_and_free_semaphores(used)
    nc.all_engine_barrier()
    used.clear()


def bank_taker(banks):
    taken = [0]

    def take(shape):
        size = 1
        for n in shape[1:]:
            size *= n
        first = taken[0]
        taken[0] += -(-size // 512)
        assert taken[0] <= 8
        flat = banks[0:shape[0], first:taken[0], :].rearrange("p b c -> p (b c)")[:, 0:size]
        if len(shape) == 3:
            return flat.rearrange("p (a b) -> p a b", a=shape[1])
        if len(shape) == 4:
            return flat.rearrange("p (a b c) -> p a b c", a=shape[1], b=shape[2])
        return flat

    return take


def ffn_lora_phase(nc, tag, banks, used, x_res, ident, neg_half, w, background, x_first=None, x_rest=None, split=None):
    U = 4
    with ExitStack() as ctx:
        def sb(name, shape, dt=F32):
            return ctx.enter_context(nc.sbuf_tensor(f"{tag}_{name}", shape, dt))

        bank = bank_taker(banks)

        def sem(name):
            return new_sem(nc, used, f"{tag}_{name}")

        stats = sb("stats", [P, 2, GROUP, 6])
        mv = sb("mv", [P, 2, GROUP, 2])
        rstd = sb("rstd", [P, 2, GROUP])
        var_eps = sb("var_eps", [P, 2, GROUP])
        xn = sb("xn", [P, 2, GROUP, C])
        xnT = sb("xnT", [P, 4, GT])
        logit = sb("logit", [P, 2, GROUP, LORA_E])
        top = sb("top", [P, 2, GROUP])
        shifted = sb("shifted", [P, 2, GROUP, LORA_E])
        expd = sb("expd", [P, 2, GROUP, LORA_E])
        total = sb("total", [P, 2, GROUP])
        inv = sb("inv", [P, 2, GROUP])
        gate = sb("gate", [P, 2, GROUP, LORA_E], BF16)
        mid = sb("mid", [P, 2, GROUP, LORA_R])
        om = sb("om", [P, 2, GROUP, LORA_ROWS + 1])
        omT = sb("omT", [LORA_ROWS + 1, 2, GT])
        ps_t = bank([P, 2, GT])
        ps_small = bank([P, 512])[:, 0:GROUP * 16].rearrange("p (j e) -> p j e", e=16)
        ps_o = bank([LORA_ROWS + 1, 2, GT])
        ps_y = bank([P, 2, GT])

        stats_done, aggr_done, rstd_done, xn_ready = sem("stats_done"), sem("aggr_done"), sem("rstd_done"), sem("xn_ready")
        eps_added = sem("eps_added")
        ones_ready, xn_transposed, xnT_ready, small_ready = sem("ones_ready"), sem("xn_transposed"), sem("xnT_ready"), sem("small_ready")
        logit_done, top_done, shifted_ready, exp_ready = sem("logit_done"), sem("top_done"), sem("shifted_ready"), sem("exp_ready")
        total_done, inv_done, gate_done, om_ready = sem("total_done"), sem("inv_done"), sem("gate_done"), sem("om_ready")
        om_transposed, omT_ready, y_ready, x_updated = sem("om_transposed"), sem("omT_ready"), sem("y_ready"), sem("x_updated")

        block = ctx.enter_context(nc.Block())

        def count(it, u, back=0):
            return it * U + (u + 1 - back)

        def wait_free(engine, semaphore, value):
            if not isinstance(value, int) or value > 0:
                engine.wait_ge(semaphore, value)

        def x_group(it, u):
            return x_res[:, bass.ds((it * U + u) * GROUP, GROUP), :]

        def beside(engine, which):
            return [(1, in_last_iteration(engine, GROUPS // U, split[2], split[which]))] if split else []

        @block.sync
        def _(sync):
            background(sync, x_updated)

        @block.vector
        def _(dve):
            for p in range(2):
                dve.memset(om[:, p, :, LORA_ROWS:], 1.0).then_inc(ones_ready, 1)

            def layernorm(it, u):
                p = u % 2
                xg = x_group(it, u)
                if x_first is not None:
                    dve.wait_ge(x_first if isinstance(it, int) and it * U + u < FIRST_GROUPS else x_rest, 16)
                for j in range(GROUP):
                    last = dve.bn_stats(stats[:, p, j, :], xg[:, j, :])
                last.then_inc(stats_done, 1)
                dve.wait_ge(stats_done, count(it, u))
                dve.nop(nofuse=True)
                for j in range(GROUP):
                    last = dve.bn_aggr(mv[:, p, j, :], stats[:, p, j, :])
                last.then_inc(aggr_done, 1)

            def normalise(it, u):
                p = u % 2
                xg = x_group(it, u)
                dve.wait_ge(rstd_done, count(it, u))
                wait_free(dve, xn_transposed, count(it, u, 2))
                for j in range(GROUP):
                    last = dve.tensor_scalar(xn[:, p, j, :], xg[:, j, :], mv[:, p, j, 0:1], rstd[:, p, j:j + 1],
                                             ALU.subtract, ALU.mult)
                last.then_inc(xn_ready, 1)

            def router_shift(it, u):
                p = u % 2
                dve.wait_ge(small_ready, count(it, u))
                dve.tensor_tensor(logit[:, p], ps_small[:, :, 0:LORA_E], w["router_b"][:, :, :], ALU.add).then_inc(logit_done, 1)
                dve.tensor_copy(mid[:, p], ps_small[:, :, LORA_E:])
                dve.wait_ge(logit_done, count(it, u))
                dve.tensor_reduce(top[:, p, :], logit[:, p], AX.X, ALU.max).then_inc(top_done, 1)
                dve.wait_ge(top_done, count(it, u))
                dve.tensor_tensor(shifted[:, p], logit[:, p], top[:, p, :].unsqueeze(2).to_broadcast([P, GROUP, LORA_E]),
                                  ALU.subtract).then_inc(shifted_ready, 1)

            def gates(it, u):
                p = u % 2
                dve.wait_ge(exp_ready, count(it, u))
                dve.tensor_reduce(total[:, p, :], expd[:, p], AX.X, ALU.add).then_inc(total_done, 1)
                dve.wait_ge(total_done, count(it, u))
                dve.reciprocal(inv[:, p, :], total[:, p, :]).then_inc(inv_done, 1)
                dve.wait_ge(inv_done, count(it, u))
                dve.tensor_tensor(gate[:, p], expd[:, p], inv[:, p, :].unsqueeze(2).to_broadcast([P, GROUP, LORA_E]),
                                  ALU.mult).then_inc(gate_done, 1)
                dve.wait_ge(gate_done, count(it, u))
                for j in range(GROUP):
                    last = dve.tensor_tensor(
                        om[:, p, j, 0:LORA_ROWS].rearrange("p (e r) -> p e r", e=LORA_E),
                        gate[:, p, j, :].unsqueeze(2).to_broadcast([P, LORA_E, LORA_R]),
                        mid[:, p, j, :].unsqueeze(1).to_broadcast([P, LORA_E, LORA_R]), ALU.mult)
                last.then_inc(om_ready, 1)

            def residual(it, u):
                dve.wait_ge(y_ready, count(it, u))
                xg = x_group(it, u).rearrange("p j c -> p (j c)")
                dve.scalar_tensor_tensor(xg, ps_y[:, u % 2, :], 0.5, xg, ALU.mult, ALU.add).then_inc(x_updated, 1)

            software_pipeline(dve, GROUPS // U, U, [
                (3, normalise), (2, router_shift), (4, layernorm), (2, gates), (0, residual)])

        @block.gpsimd
        def _(pool):
            def inverse_std(it, u):
                pool.wait_ge(aggr_done, count(it, u))
                pool.nop(nofuse=True)
                pool.tensor_scalar(var_eps[:, u % 2, :], mv[:, u % 2, :, 1], LN_EPS, None, ALU.add).then_inc(eps_added, 1)
                pool.wait_ge(eps_added, count(it, u))
                pool.tensor_tensor(rstd[:, u % 2, :], var_eps[:, u % 2, :], neg_half[:, 0:GROUP], ALU.pow).then_inc(rstd_done, 1)

            software_pipeline(pool, GROUPS // U, U, [
                (4, inverse_std)] + beside(pool, 1))

        @block.tensor
        def _(pe):
            def transpose_x(it, u):
                pe.wait_ge(xn_ready, count(it, u))
                wait_free(pe, xnT_ready, count(it, u, 2))
                for j in range(GROUP):
                    last = pe.transpose(ps_t[:, u % 2, j * P:(j + 1) * P], xn[:, u % 2, j, :], ident[:, :])
                last.then_inc(xn_transposed, 1)

            def router_and_mid(it, u):
                pe.wait_ge(xnT_ready, count(it, u))
                wait_free(pe, shifted_ready, count(it, u, 1))
                for j in range(GROUP):
                    last = pe.matmul(ps_small[:, j, :], xnT[:, u % 4, j * P:(j + 1) * P], w["router_a"], start=True, stop=True)
                last.then_inc(small_ready, 1)

            def transpose_om(it, u):
                pe.wait_ge(om_ready, count(it, u))
                wait_free(pe, omT_ready, count(it, u, 2))
                for j in range(GROUP):
                    last = pe.transpose(ps_o[:, u % 2, j * P:(j + 1) * P], om[:, u % 2, j, :], ident[:, :])
                last.then_inc(om_transposed, 1)

            def project(it, u):
                pe.wait_ge(omT_ready, count(it, u))
                wait_free(pe, x_updated, count(it, u, 2))
                for j in range(GROUP):
                    y = ps_y[:, u % 2, j * P:(j + 1) * P]
                    pe.matmul(y, xnT[:, u % 4, j * P:(j + 1) * P], w["base_T"], start=True, stop=False)
                    last = pe.matmul(y, omT[:, u % 2, j * P:(j + 1) * P], w["lora_rows"], start=False, stop=True)
                last.then_inc(y_ready, 1)

            pe.wait_ge(ones_ready, 2)
            software_pipeline(pe, GROUPS // U, U, [
                (3, transpose_x), (1, transpose_om), (3, router_and_mid), (1, project)])

        @block.scalar
        def _(act):
            def copy_xT(it, u):
                act.wait_ge(xn_transposed, count(it, u))
                wait_free(act, y_ready, count(it, u, 4))
                act.copy(xnT[:, u % 4, :], ps_t[:, u % 2, :]).then_inc(xnT_ready, 1)

            def exponent(it, u):
                act.wait_ge(shifted_ready, count(it, u))
                act.activation(expd[:, u % 2], shifted[:, u % 2], ACT.Exp).then_inc(exp_ready, 1)

            def copy_omT(it, u):
                act.wait_ge(om_transposed, count(it, u))
                wait_free(act, y_ready, count(it, u, 2))
                act.copy(omT[:, u % 2, :], ps_o[:, u % 2, :]).then_inc(omT_ready, 1)

            software_pipeline(act, GROUPS // U, U, [
                (2, exponent), (3, copy_xT), (1, copy_omT)] + beside(act, 0))


MOE_E, MOE_G, MOE_K = 16, 4, 4
MOE_EPG = MOE_E // MOE_G
MOE_F = 128
MOE_SHARED = 2
MOE_UNITS = MOE_E + MOE_SHARED
MOE_SCALE = 2.5
PAD, PICKED, PICKED_BELOW = -3.0e38, -3.3e38, -3.2e38


def moe_phase(nc, tag, banks, used, x_res, ident, ident_bf, neg_half, w, background, split=None):
    GU = 2
    U = GU * MOE_UNITS
    RING = 3
    with ExitStack() as ctx:
        def sb(name, shape, dt=F32):
            return ctx.enter_context(nc.sbuf_tensor(f"{tag}_{name}", shape, dt))

        bank = bank_taker(banks)

        def sem(name):
            return new_sem(nc, used, f"{tag}_{name}")

        stats = sb("stats", [P, GU, GROUP, 6])
        mv = sb("mv", [P, GU, GROUP, 2])
        var_eps = sb("var_eps", [P, GU, GROUP])
        rstd = sb("rstd", [P, GU, GROUP])
        xn = sb("xn", [P, GROUP, C])
        x_hi = sb("x_hi", [P, GU, GT], F32R)
        x_lo = sb("x_lo", [P, GU, GT], F32R)
        silu_l = sb("silu_l", [P, GROUP, MOE_E])
        tanh_l = sb("tanh_l", [P, GROUP, MOE_E])
        inv_l = sb("inv_l", [P, GROUP, MOE_E])
        not_low = sb("not_low", [P, GROUP, MOE_E])
        upper = sb("upper", [P, GROUP, MOE_E])
        score = sb("score", [P, GROUP, MOE_E])
        biased = sb("biased", [P, GROUP, MOE_E])
        pair_max = sb("pair_max", [P, GROUP * MOE_G, 2])
        pair_min = sb("pair_min", [P, GROUP * MOE_G, 2])
        first = sb("first", [P, GROUP * MOE_G])
        low_max = sb("low_max", [P, GROUP * MOE_G])
        high_min = sb("high_min", [P, GROUP * MOE_G])
        second = sb("second", [P, GROUP * MOE_G])
        group_score = sb("group_score", [P, GROUP, MOE_G])
        above = sb("above", [P, GROUP * MOE_G, MOE_G])
        tied = sb("tied", [P, GROUP * MOE_G, MOE_G])
        tied_before = sb("tied_before", [P, GROUP * MOE_G, MOE_G])
        beaten = sb("beaten", [P, GROUP * MOE_G, MOE_G])
        rank = sb("rank", [P, GROUP * MOE_G])
        kept = sb("kept", [P, GROUP * MOE_G])
        kept_minus = sb("kept_minus", [P, GROUP * MOE_G])
        kept_score = sb("kept_score", [P, GROUP, MOE_E])
        masked = sb("masked", [P, GROUP, MOE_E + MOE_K])
        top8 = sb("top8", [P, GROUP, 8])
        wanted = sb("wanted", [P, GROUP, 8])
        replaced = sb("replaced", [P, GROUP, MOE_E + MOE_K])
        picked = sb("picked", [P, GROUP, MOE_E])
        picked_score = sb("picked_score", [P, GROUP, MOE_E])
        total = sb("total", [P, GROUP])
        total_eps = sb("total_eps", [P, GROUP])
        inv = sb("inv", [P, GROUP])
        inv_scaled = sb("inv_scaled", [P, GROUP])
        combine = sb("combine", [P, GROUP, MOE_E])
        rest = sb("rest", [P, GROUP, MOE_E])
        rest2 = sb("rest2", [P, GROUP, MOE_E])
        combine3 = sb("combine3", [P, GROUP, 3, MOE_E], BF16)
        combine3T = sb("combine3T", [3 * MOE_E, GU, GT], BF16)
        gated = sb("gated", [P, RING, GT])
        product = sb("product", [P, 2, GT])
        act_f = sb("act_f", [P, RING, GT])
        act_hi = sb("act_hi", [P, RING, GT], F32R)
        act_lo = sb("act_lo", [P, RING, GT], F32R)
        yT = sb("yT", [P, GT])
        ps_h, ps_u, ps_c = bank([P, GT]), bank([P, 2, GT]), bank([P, 2, GT])
        ps_y, ps_t = bank([P, GT]), bank([P, GT])
        ps_m = bank([P, GT])
        ps_logit = ps_m[:, 0:GROUP * MOE_E].rearrange("p (j e) -> p j e", e=MOE_E)
        ps_cT = ps_m[0:3 * MOE_E, 256:512].bitcast(BF16)

        pads_set = sem("pads_set")
        stats_done, aggr_done, eps_added, rstd_done, xn_ready = (sem(n) for n in ("stats_done", "aggr_done", "eps_added", "rstd_done", "xn_ready"))
        xn_transposed, x_hi_ready, x_split = sem("xn_transposed"), sem("x_hi_ready"), sem("x_split")
        logits_ready, score_ready, topk_step, combine_split = sem("logits_ready"), sem("score_ready"), sem("topk_step"), sem("combine_split")
        combine_step, combine_transposed, combineT_ready = sem("combine_step"), sem("combine_transposed"), sem("combineT_ready")
        h_ready, u_ready, c_ready, gated_ready, product_done = (sem(n) for n in ("h_ready", "u_ready", "c_ready", "gated_ready", "product_done"))
        act_ready, act_hi_ready, act_lo_ready, down_done = sem("act_ready"), sem("act_hi_ready"), sem("act_lo_ready"), sem("down_done")
        yT_ready, y_transposed, x_updated = sem("yT_ready"), sem("y_transposed"), sem("x_updated")

        block = ctx.enter_context(nc.Block())

        def unit(it, k, back=0):
            return it * U + (k + 1 - back)

        def routed(it, k):
            return it * GU * MOE_E + (k // MOE_UNITS * MOE_E + k % MOE_UNITS - MOE_SHARED + 1)

        def group(it, k, back=0):
            return it * GU + (k // MOE_UNITS + 1 - back)

        def wait_free(engine, semaphore, value):
            if not isinstance(value, int) or value > 0:
                engine.wait_ge(semaphore, value)

        def per_group(at, emit):
            def stage(it, k):
                if k % MOE_UNITS == at:
                    emit(it, k)
            return stage

        def x_group(it, k):
            return x_res[:, bass.ds((it * GU + k // MOE_UNITS) * GROUP, GROUP), :]

        TOPK_STEPS = 33

        def beside(engine, which):
            return [(0, in_last_iteration(engine, GROUPS // GU, split[2], split[which]))] if split else []

        @block.sync
        def _(sync):
            background(sync, x_updated)

        @block.vector
        def _(dve):
            dve.nop(nofuse=True).then_inc(x_updated, 1)
            dve.memset(masked[:, :, MOE_E:], PAD).then_inc(pads_set, 1)
            dve.memset(wanted[:, :, MOE_K:], PAD).then_inc(pads_set, 1)
            dve.wait_ge(pads_set, 2)

            def layernorm(it, k):
                p = k // MOE_UNITS % GU
                xg = x_group(it, k)
                for j in range(GROUP):
                    last = dve.bn_stats(stats[:, p, j, :], xg[:, j, :])
                last.then_inc(stats_done, 1)
                dve.wait_ge(stats_done, group(it, k))
                dve.nop(nofuse=True)
                for j in range(GROUP):
                    last = dve.bn_aggr(mv[:, p, j, :], stats[:, p, j, :])
                last.then_inc(aggr_done, 1)

            def normalise(it, k):
                p = k // MOE_UNITS % GU
                xg = x_group(it, k)
                dve.wait_ge(rstd_done, group(it, k))
                wait_free(dve, xn_transposed, group(it, k, 1))
                for j in range(GROUP):
                    last = dve.tensor_scalar(xn[:, j, :], xg[:, j, :], mv[:, p, j, 0:1], rstd[:, p, j:j + 1],
                                             ALU.subtract, ALU.mult)
                last.then_inc(xn_ready, 1)

            def split_x(it, k):
                p = k // MOE_UNITS % GU
                dve.wait_ge(x_hi_ready, group(it, k))
                dve.tensor_tensor(x_lo[:, p, :], ps_t[:, :], x_hi[:, p, :].bitcast(F32), ALU.subtract).then_inc(x_split, 1)

            def topk_ops(it, k):
                per_token = [P, GROUP * MOE_G, MOE_G]
                s4 = biased[:, :, :].rearrange("p j (g e) -> p (j g) e", e=MOE_EPG)
                gs = group_score[:, :, :]
                gs_of = group_score[:, :, :].rearrange("p j g -> p (j g)").unsqueeze(2).to_broadcast(per_token)

                def others(dst):
                    return dst[:, :, :].rearrange("p (j g) h -> p j g h", g=MOE_G)

                def compare(dst, op):
                    shape = [P, GROUP, MOE_G, MOE_G]
                    return dve.tensor_tensor(others(dst), gs.unsqueeze(2).to_broadcast(shape),
                                             gs.unsqueeze(3).to_broadcast(shape), op)

                k4 = kept_score[:, :, :].rearrange("p j (g e) -> p (j g) e", e=MOE_EPG)
                m4 = masked[:, :, 0:MOE_E].rearrange("p j (g e) -> p j g e", e=MOE_EPG)
                j4 = [P, GROUP, MOE_G, MOE_EPG]
                return [
                    lambda: dve.tensor_scalar(not_low[:, :, :], ps_logit, -1.0, None, ALU.is_ge),
                    lambda: dve.reciprocal(inv_l[:, :, :], ps_logit),
                    lambda: dve.tensor_tensor(score[:, :, :], silu_l[:, :, :], inv_l[:, :, :], ALU.mult),
                    lambda: dve.tensor_scalar(upper[:, :, :], tanh_l[:, :, :], 0.5, 0.5, ALU.mult, ALU.add),
                    lambda: [dve.nop(nofuse=True), dve.copy_predicated(score[:, :, :], not_low[:, :, :].bitcast(mybir.dt.int32), upper[:, :, :])],
                    lambda: dve.tensor_tensor(biased[:, :, :], score[:, :, :], w["bias"][:, :, :], ALU.add),
                    lambda: dve.tensor_tensor(pair_max[:, :, :], s4[:, :, 0:4:2], s4[:, :, 1:4:2], ALU.max),
                    lambda: dve.tensor_tensor(pair_min[:, :, :], s4[:, :, 0:4:2], s4[:, :, 1:4:2], ALU.min),
                    lambda: dve.tensor_tensor(first[:, :], pair_max[:, :, 0], pair_max[:, :, 1], ALU.max),
                    lambda: dve.tensor_tensor(high_min[:, :], pair_max[:, :, 0], pair_max[:, :, 1], ALU.min),
                    lambda: dve.tensor_tensor(low_max[:, :], pair_min[:, :, 0], pair_min[:, :, 1], ALU.max),
                    lambda: dve.tensor_tensor(second[:, :], high_min[:, :], low_max[:, :], ALU.max),
                    lambda: dve.tensor_tensor(gs.rearrange("p j g -> p (j g)"), first[:, :], second[:, :], ALU.add),
                    lambda: compare(above, ALU.is_gt),
                    lambda: compare(tied, ALU.is_equal),
                    lambda: dve.tensor_tensor(tied_before[:, :, :], tied[:, :, :], w["before"][:, :, :], ALU.mult),
                    lambda: dve.tensor_tensor(beaten[:, :, :], above[:, :, :], tied_before[:, :, :], ALU.add),
                    lambda: dve.tensor_reduce(rank[:, :], beaten[:, :, :], AX.X, ALU.add),
                    lambda: dve.tensor_scalar(kept[:, :], rank[:, :], 2.0, None, ALU.is_lt),
                    lambda: dve.tensor_scalar(kept_minus[:, :], kept[:, :], 1.0, None, ALU.subtract),
                    lambda: dve.tensor_tensor(k4, s4, kept[:, :].unsqueeze(2).to_broadcast(per_token), ALU.mult),
                    lambda: dve.tensor_tensor(
                        m4, kept_score[:, :, :].rearrange("p j (g e) -> p j g e", e=MOE_EPG),
                        kept_minus[:, :].rearrange("p (j g) -> p j g", g=MOE_G).unsqueeze(3).to_broadcast(j4), ALU.add),
                    lambda: [dve.nop(nofuse=True)] + [dve.max(top8[:, j, :], masked[:, j, :]) for j in range(GROUP)],
                    lambda: dve.tensor_copy(wanted[:, :, 0:MOE_K], top8[:, :, 0:MOE_K]),
                    lambda: [dve.nop(nofuse=True)] + [dve.match_replace(replaced[:, j, :], wanted[:, j, :], masked[:, j, :], PICKED)
                                                      for j in range(GROUP)],
                    lambda: dve.tensor_scalar(picked[:, :, :], replaced[:, :, 0:MOE_E], PICKED_BELOW, None, ALU.is_lt),
                    lambda: dve.tensor_tensor(picked_score[:, :, :], picked[:, :, :], score[:, :, :], ALU.mult),
                    lambda: dve.tensor_reduce(total[:, :], picked_score[:, :, :], AX.X, ALU.add),
                    lambda: dve.tensor_scalar(total_eps[:, :], total[:, :], 1e-20, None, ALU.add),
                    lambda: dve.reciprocal(inv[:, :], total_eps[:, :]),
                    lambda: dve.tensor_scalar(inv_scaled[:, :], inv[:, :], MOE_SCALE, None, ALU.mult),
                    lambda: dve.tensor_tensor(combine[:, :, :], picked_score[:, :, :],
                                              inv_scaled[:, :].unsqueeze(2).to_broadcast([P, GROUP, MOE_E]), ALU.mult),
                ]

            def topk(lo, hi):
                def stage(it, k):
                    ops = topk_ops(it, k)
                    assert len(ops) == TOPK_STEPS - 1
                    g0 = it * GU + k // MOE_UNITS
                    if lo == 0:
                        dve.wait_ge(score_ready, group(it, k))
                    for i in range(lo, min(hi, len(ops))):
                        if i > 0:
                            dve.wait_ge(topk_step, g0 * (TOPK_STEPS - 1) + i)
                        if i == len(ops) - 1:
                            wait_free(dve, combine_split, group(it, k, 1))
                        last = ops[i]()
                        if isinstance(last, list):
                            last = last[-1]
                        last.then_inc(topk_step, 1)
                return stage

            def multiply(it, k):
                e = k % MOE_UNITS
                dve.wait_ge(gated_ready, unit(it, k))
                dve.wait_ge(u_ready, unit(it, k))
                if e >= MOE_SHARED:
                    dve.tensor_tensor(product[:, k % 2, :], ps_u[:, k % 2, :], gated[:, k % RING, :], ALU.mult).then_inc(product_done, 1)
                    dve.wait_ge(product_done, routed(it, k))
                    dve.wait_ge(c_ready, routed(it, k))
                    wait_free(dve, act_lo_ready, unit(it, k, RING))
                    dve.tensor_tensor(act_f[:, k % RING, :], ps_c[:, k % 2, :], product[:, k % 2, :], ALU.mult).then_inc(act_ready, 1)
                else:
                    wait_free(dve, act_lo_ready, unit(it, k, RING))
                    dve.tensor_tensor(act_f[:, k % RING, :], ps_u[:, k % 2, :], gated[:, k % RING, :], ALU.mult).then_inc(act_ready, 1)

            def residual(it, k):
                dve.wait_ge(y_transposed, group(it, k, -1))
                xg = x_group(it, k).rearrange("p j c -> p (j c)")
                dve.scalar_tensor_tensor(xg, ps_t[:, :], 0.5, xg, ALU.mult, ALU.add).then_inc(x_updated, 1)

            software_pipeline(dve, GROUPS // GU, U, [
                (19, per_group(0, layernorm)), (16, per_group(0, split_x)), (14, per_group(0, topk(0, 5))),
                (13, per_group(0, topk(5, 10))), (12, per_group(0, topk(10, 14))), (11, per_group(0, topk(14, 18))),
                (10, per_group(0, topk(18, 22))), (9, per_group(0, topk(22, 25))), (8, per_group(0, topk(25, 29))),
                (7, per_group(0, topk(29, 33))), (4, multiply), (18, per_group(0, normalise)),
                (0, per_group(MOE_UNITS - 1, residual))])

        @block.gpsimd
        def _(pool):
            def inverse_std(it, k):
                p = k // MOE_UNITS % GU
                pool.wait_ge(aggr_done, group(it, k))
                pool.nop(nofuse=True)
                pool.tensor_scalar(var_eps[:, p, :], mv[:, p, :, 1], LN_EPS, None, ALU.add).then_inc(eps_added, 1)
                pool.wait_ge(eps_added, group(it, k))
                pool.tensor_tensor(rstd[:, p, :], var_eps[:, p, :], neg_half[:, 0:GROUP], ALU.pow).then_inc(rstd_done, 1)

            def split_combine(it, k):
                steps = 4 * (it * GU + k // MOE_UNITS)
                part = [combine3[:, :, i, :] for i in range(3)]
                pool.wait_ge(topk_step, (it * GU + k // MOE_UNITS + 1) * (TOPK_STEPS - 1))
                wait_free(pool, combine_transposed, group(it, k, 1))
                pool.nop(nofuse=True)
                pool.tensor_copy(part[0], combine[:, :, :]).then_inc(combine_step, 1)
                pool.wait_ge(combine_step, steps + 1)
                pool.tensor_tensor(rest[:, :, :], combine[:, :, :], part[0], ALU.subtract).then_inc(combine_step, 1)
                pool.wait_ge(combine_step, steps + 2)
                pool.nop(nofuse=True)
                pool.tensor_copy(part[1], rest[:, :, :]).then_inc(combine_step, 1)
                pool.wait_ge(combine_step, steps + 3)
                pool.tensor_tensor(rest2[:, :, :], rest[:, :, :], part[1], ALU.subtract).then_inc(combine_step, 1)
                pool.wait_ge(combine_step, steps + 4)
                pool.nop(nofuse=True)
                pool.tensor_copy(part[2], rest2[:, :, :]).then_inc(combine_split, 1)

            def split_lo(it, k):
                pool.wait_ge(act_hi_ready, unit(it, k))
                wait_free(pool, down_done, unit(it, k, RING))
                pool.tensor_tensor(act_lo[:, k % RING, :], act_f[:, k % RING, :], act_hi[:, k % RING, :].bitcast(F32),
                                   ALU.subtract).then_inc(act_lo_ready, 1)

            software_pipeline(pool, GROUPS // GU, U, [
                (19, per_group(0, inverse_std)), (7, per_group(0, split_combine)), (4, split_lo)] + beside(pool, 1))

        @block.scalar
        def _(act):
            def copy_x_hi(it, k):
                act.wait_ge(xn_transposed, group(it, k))
                act.copy(x_hi[:, k // MOE_UNITS % GU, :], ps_t[:, :]).then_inc(x_hi_ready, 1)

            def sigmoid(it, k):
                act.wait_ge(logits_ready, group(it, k))
                wait_free(act, topk_step, (it * GU + k // MOE_UNITS) * (TOPK_STEPS - 1))
                act.activation(silu_l[:, :, :], ps_logit, ACT.Silu)
                act.activation(tanh_l[:, :, :], ps_logit, ACT.Tanh, scale=0.5).then_inc(score_ready, 1)

            def copy_combineT(it, k):
                act.wait_ge(combine_transposed, group(it, k))
                act.copy(combine3T[:, k // MOE_UNITS % GU, :], ps_cT).then_inc(combineT_ready, 1)

            def silu(it, k):
                act.wait_ge(h_ready, unit(it, k))
                wait_free(act, act_ready, unit(it, k, RING))
                act.activation(gated[:, k % RING, :], ps_h[:, :], ACT.Silu).then_inc(gated_ready, 1)

            def split_hi(it, k):
                act.wait_ge(act_ready, unit(it, k))
                wait_free(act, down_done, unit(it, k, RING))
                act.copy(act_hi[:, k % RING, :], act_f[:, k % RING, :]).then_inc(act_hi_ready, 1)

            def copy_yT(it, k):
                act.wait_ge(down_done, unit(it, k))
                act.wait_ge(y_transposed, group(it, k, 0))
                act.copy(yT[:, :], ps_y[:, :]).then_inc(yT_ready, 1)

            software_pipeline(act, GROUPS // GU, U, [
                (16, per_group(0, copy_x_hi)), (14, per_group(0, sigmoid)), (4, silu), (3, per_group(0, copy_combineT)),
                (3, split_hi), (1, per_group(MOE_UNITS - 1, copy_yT))] + beside(act, 0))

        @block.tensor
        def _(pe):
            pe.nop(nofuse=True).then_inc(y_transposed, 1)

            def three_pass(out, weights, column, hi, lo, start=True, stop=True):
                w_hi, w_lo = (part[:, column:column + MOE_F] for part in weights)
                pe.matmul(out, w_hi, hi, start=start, stop=False)
                pe.matmul(out, w_hi, lo, start=False, stop=False)
                return pe.matmul(out, w_lo, hi, start=False, stop=stop)

            def transpose_x(it, k):
                pe.wait_ge(xn_ready, group(it, k))
                wait_free(pe, x_updated, group(it, k, 1))
                for j in range(GROUP):
                    last = pe.transpose(ps_t[:, j * P:(j + 1) * P], xn[:, j, :], ident[:, :])
                last.then_inc(xn_transposed, 1)

            def router(it, k):
                p = k // MOE_UNITS % GU
                pe.wait_ge(x_split, group(it, k))
                wait_free(pe, topk_step, (it * GU + k // MOE_UNITS) * (TOPK_STEPS - 1))
                for j in range(GROUP):
                    hi, lo = x_hi[:, p, j * P:(j + 1) * P], x_lo[:, p, j * P:(j + 1) * P]
                    r_hi, r_lo = w["router"]
                    pe.matmul(ps_logit[:, j, :], hi, r_hi, start=True, stop=False)
                    pe.matmul(ps_logit[:, j, :], lo, r_hi, start=False, stop=False)
                    last = pe.matmul(ps_logit[:, j, :], hi, r_lo, start=False, stop=True)
                last.then_inc(logits_ready, 1)

            def transpose_combine(it, k):
                pe.wait_ge(combine_split, group(it, k))
                wait_free(pe, combineT_ready, group(it, k, 1))
                pe.nop(nofuse=True)
                for j in range(GROUP):
                    last = pe.transpose(ps_cT[:, j * P:(j + 1) * P], combine3[:, j, :, :].rearrange("p i e -> p (i e)"), ident_bf[:, :])
                last.then_inc(combine_transposed, 1)

            def up(it, k):
                p, e = k // MOE_UNITS % GU, k % MOE_UNITS
                if e == 0:
                    pe.wait_ge(x_split, group(it, k))
                wait_free(pe, gated_ready, unit(it, k, 1))
                three_pass(ps_h[:, :], w["up_down"], e * MOE_F, x_hi[:, p, :], x_lo[:, p, :]).then_inc(h_ready, 1)
                if (k - 2) % MOE_UNITS >= MOE_SHARED:
                    wait_free(pe, product_done, routed(it, k - 2))
                else:
                    wait_free(pe, act_ready, unit(it, k - 2))
                three_pass(ps_u[:, k % 2, :], w["up_down"], (MOE_UNITS + e) * MOE_F, x_hi[:, p, :], x_lo[:, p, :]).then_inc(u_ready, 1)

            def weights_of(it, k):
                p, e = k // MOE_UNITS % GU, k % MOE_UNITS
                if e < MOE_SHARED:
                    return
                if e == MOE_SHARED:
                    pe.wait_ge(combineT_ready, group(it, k))
                wait_free(pe, act_ready, unit(it, k, 2))
                pe.matmul(ps_c[:, k % 2, :], w["select"][:, e - MOE_SHARED, :], combine3T[:, p, :], start=True, stop=True).then_inc(c_ready, 1)

            def down(it, k):
                e = k % MOE_UNITS
                d_hi, d_lo = (part[:, (2 * MOE_UNITS + e) * MOE_F:(2 * MOE_UNITS + e + 1) * MOE_F] for part in w["up_down"])
                pe.wait_ge(act_hi_ready, unit(it, k))
                if e == 0:
                    wait_free(pe, yT_ready, group(it, k, 1))
                pe.matmul(ps_y[:, :], d_hi, act_hi[:, k % RING, :], start=(e == 0), stop=False)
                pe.matmul(ps_y[:, :], d_lo, act_hi[:, k % RING, :], start=False, stop=False)
                pe.wait_ge(act_lo_ready, unit(it, k))
                pe.matmul(ps_y[:, :], d_hi, act_lo[:, k % RING, :], start=False, stop=(e == MOE_UNITS - 1)).then_inc(down_done, 1)

            def transpose_y(it, k):
                pe.wait_ge(yT_ready, group(it, k))
                seen = group(it, k, -1)
                pe.wait_ge(x_split, min(seen, GROUPS) if isinstance(seen, int) else seen)
                for j in range(GROUP):
                    last = pe.transpose(ps_t[:, j * P:(j + 1) * P], yT[:, j * P:(j + 1) * P], ident[:, :])
                last.then_inc(y_transposed, 1)

            software_pipeline(pe, GROUPS // GU, U, [
                (16, per_group(0, transpose_x)), (14, per_group(0, router)), (4, up),
                (3, per_group(0, transpose_combine)), (4, weights_of), (1, down),
                (0, per_group(MOE_UNITS - 1, transpose_y))])


HEADS = 16
HEAD_D = C // HEADS
BATCH_TILES = T // P
HEAD_GROUPS = HEADS // 4
SLOTS = 4
WIDTH = 3 * P
NUM_BUCKETS, MAX_DISTANCE = 32, 128
MASKED = -1.0e30


def attention_phase(nc, tag, banks, used, x_res, ident, neg_half, w):
    GU = 2
    U = GU * HEADS
    Z, PR = 4, 8
    SCALE = HEAD_D ** -0.5
    with ExitStack() as ctx:
        def sb(name, shape, dt=F32):
            return ctx.enter_context(nc.sbuf_tensor(f"{tag}_{name}", shape, dt))

        bank = bank_taker(banks)

        def sem(name):
            return new_sem(nc, used, f"{tag}_{name}")

        stats = sb("stats", [P, GU, BATCH_TILES, 6])
        mv = sb("mv", [P, GU, BATCH_TILES, 2])
        var_eps = sb("var_eps", [P, GU, BATCH_TILES])
        rstd = sb("rstd", [P, GU, BATCH_TILES])
        xn = sb("xn", [P, BATCH_TILES, C])
        xnT = sb("xnT", [P, GU, T])
        x_hi, x_lo = sb("x_hi", [P, GU, T], F32R), sb("x_lo", [P, GU, T], F32R)
        v_aug = sb("v_aug", [P, GU, BATCH_TILES, HEADS, 32])
        qk_f = sb("qk_f", [P, 2, 2, T])
        qk_hi = sb("qk_hi", [P, 2, 2, T])
        stack = sb("stack", [P, GU, HEAD_GROUPS, 2, T], F32R)
        z = sb("z", [P, Z, WIDTH])
        top = sb("top", [P, Z, BATCH_TILES])
        prob = sb("prob", [P, PR, WIDTH])
        avT = sb("avT", [P, 2, T])
        inv = sb("inv", [P, 2, BATCH_TILES, 4])
        y = sb("y", [P, BATCH_TILES, C])
        yT = sb("yT", [P, T])
        ps_s, ps_p = bank([P, 2, 512]), bank([P, 2, 512])
        ps_qk, ps_av, ps_heads = bank([P, 2, T]), bank([P, 512])[:, 0:T], bank([P, 512])
        ps_heads = ps_heads[:, 0:T].rearrange("p (j i d) -> p j i d", j=BATCH_TILES, d=32)
        ps_f = bank([P, 512])
        ps_x = ps_v = ps_yT = ps_out = ps_f[:, 0:T]

        ones_set = sem("ones_set")
        stats_done, aggr_done, eps_added, rstd_done, xn_ready = (sem(n) for n in ("stats_done", "aggr_done", "eps_added", "rstd_done", "xn_ready"))
        xn_transposed, xnT_ready, v_projected, v_ready = (sem(n) for n in ("xn_transposed", "xnT_ready", "v_projected", "v_ready"))
        qk_projected, qk_copied, qk_hi_done, stack_ready = (sem(n) for n in ("qk_projected", "qk_copied", "qk_hi_done", "stack_ready"))
        scores_ready, biased_done, shifted0, shifted1 = (sem(n) for n in ("scores_ready", "biased_done", "shifted0", "shifted1"))
        z_transposed, prob_ready, av_done, avT_ready, inv_done, y_ready = (sem(n) for n in ("z_transposed", "prob_ready", "av_done", "avT_ready", "inv_done", "y_ready"))
        heads_transposed = sem("heads_transposed")
        x_hi_ready, x_split, x_biased = sem("x_hi_ready"), sem("x_split"), sem("x_biased")
        y_transposed, yT_ready, out_ready, x_updated = (sem(n) for n in ("y_transposed", "yT_ready", "out_ready", "x_updated"))

        block = ctx.enter_context(nc.Block())

        def unit(it, k, back=0):
            return it * U + (k + 1 - back)

        def seq(it, k, back=0):
            return it * GU + (k // HEADS + 1 - back)

        def wait_free(engine, semaphore, value):
            if not isinstance(value, int) or value > 0:
                engine.wait_ge(semaphore, value)

        def per_seq(at, emit):
            def stage(it, k):
                if k % HEADS == at:
                    emit(it, k)
            return stage

        def x_seq(it, k):
            return x_res[:, bass.ds((it * GU + k // HEADS) * BATCH_TILES, BATCH_TILES), :]

        def of_group(hg, emit):
            return per_seq(0, lambda it, k: emit(it, k, hg))

        def per_four(emit):
            def stage(it, k):
                if k % 4 == 3:
                    emit(it, k)
            return stage

        def fours(it, k, back=0):
            return it * (U // 4) + (k // 4 + 1 - back)

        def hg_count(it, k, hg, back=0):
            return (it * GU + k // HEADS) * HEAD_GROUPS + (hg + 1 - back)

        @block.vector
        def _(dve):
            dve.memset(v_aug[:, :, :, :, HEAD_D:HEAD_D + 1], 1.0)
            dve.memset(v_aug[:, :, :, :, HEAD_D + 1:], 0.0)

            def layernorm(it, k):
                p = k // HEADS % GU
                xs = x_seq(it, k)
                for j in range(BATCH_TILES):
                    last = dve.bn_stats(stats[:, p, j, :], xs[:, j, :])
                last.then_inc(stats_done, 1)
                dve.wait_ge(stats_done, seq(it, k))
                dve.nop(nofuse=True)
                for j in range(BATCH_TILES):
                    last = dve.bn_aggr(mv[:, p, j, :], stats[:, p, j, :])
                last.then_inc(aggr_done, 1)

            def normalise(it, k):
                p = k // HEADS % GU
                xs = x_seq(it, k)
                dve.wait_ge(rstd_done, seq(it, k))
                wait_free(dve, xn_transposed, seq(it, k, 1))
                for j in range(BATCH_TILES):
                    last = dve.tensor_scalar(xn[:, j, :], xs[:, j, :], mv[:, p, j, 0:1], rstd[:, p, j:j + 1],
                                             ALU.subtract, ALU.mult)
                last.then_inc(xn_ready, 1)

            def split_x(it, k):
                p = k // HEADS % GU
                xs = x_seq(it, k)
                dve.wait_ge(xn_ready, seq(it, k))
                dve.tensor_tensor(xs, xs, w["proj_bias"][:, :].unsqueeze(1).to_broadcast([P, BATCH_TILES, C]), ALU.add).then_inc(x_biased, 1)
                dve.wait_ge(xnT_ready, seq(it, k))
                wait_free(dve, qk_projected, (it * GU + k // HEADS - 1) * HEAD_GROUPS)
                dve.tensor_copy(x_hi[:, p, :], xnT[:, p, :]).then_inc(x_hi_ready, 1)
                dve.wait_ge(x_hi_ready, seq(it, k))
                dve.tensor_tensor(x_lo[:, p, :], xnT[:, p, :], x_hi[:, p, :].bitcast(F32), ALU.subtract).then_inc(x_split, 1)

            def add_v_bias(it, k):
                p = k // HEADS % GU
                dve.wait_ge(v_projected, seq(it, k))
                wait_free(dve, av_done, (it * GU + k // HEADS - 1) * HEAD_GROUPS)
                for j in range(BATCH_TILES):
                    last = dve.tensor_tensor(v_aug[:, p, j, :, 0:HEAD_D],
                                             ps_v[:, j * C:(j + 1) * C].rearrange("p (h d) -> p h d", d=HEAD_D),
                                             w["v_bias"][:, :].rearrange("p (h d) -> p h d", d=HEAD_D), ALU.add)
                last.then_inc(v_ready, 1)

            def mask_hi(it, k, hg):
                r = hg % 2
                dve.wait_ge(qk_copied, hg_count(it, k, hg))
                wait_free(dve, stack_ready, hg_count(it, k, hg, 2))
                for i in range(2):
                    last = dve.tensor_scalar(qk_hi[:, r, i, :].bitcast(F32R), qk_f[:, r, i, :], w["lo_slots"][:, i:i + 1], None, ALU.mult)
                last.then_inc(qk_hi_done, 1)

            def bias_and_max(it, k):
                h = k % HEADS
                dve.wait_ge(scores_ready, unit(it, k))
                wait_free(dve, z_transposed, unit(it, k, Z))
                dve.nop(nofuse=True)
                for j, cols in enumerate((slice(0, P), slice(P, WIDTH))):
                    bias = w["rel_bias"][:, h, P:T] if j == 0 else w["rel_bias"][:, h, :]
                    last = dve.tensor_tensor_reduce(out=z[:, k % Z, cols], in0=ps_s[:, k % 2, cols], in1=bias,
                                                    scale=1.0, scalar=-3.0e38, op0=ALU.add, op1=ALU.max,
                                                    accum_out=top[:, k % Z, j:j + 1])
                last.then_inc(biased_done, 1)

            def divide(it, k):
                r, hg = k // 4 % 2, k % HEADS // 4
                dve.wait_ge(heads_transposed, fours(it, k))
                dve.reciprocal(inv[:, r], ps_heads[:, :, :, HEAD_D]).then_inc(inv_done, 1)
                dve.wait_ge(inv_done, fours(it, k))
                if hg == 0:
                    wait_free(dve, y_transposed, seq(it, k, 1))
                dve.tensor_tensor(y[:, :, 4 * hg * HEAD_D:4 * (hg + 1) * HEAD_D].rearrange("p j (i d) -> p j i d", d=HEAD_D),
                                  ps_heads[:, :, :, 0:HEAD_D],
                                  inv[:, r].unsqueeze(3).to_broadcast([P, BATCH_TILES, 4, HEAD_D]), ALU.mult).then_inc(y_ready, 1)

            def residual(it, k):
                dve.wait_ge(out_ready, seq(it, k))
                dve.wait_ge(x_biased, seq(it, k))
                xs = x_seq(it, k).rearrange("p j c -> p (j c)")
                dve.tensor_tensor(xs, ps_out, xs, ALU.add).then_inc(x_updated, 1)

            software_pipeline(dve, BATCHES // GU, U, [
                (28, per_seq(0, layernorm)), (27, per_seq(0, normalise)), (5, per_four(divide)),
                (25, per_seq(0, split_x)), (24, per_seq(0, add_v_bias)), (20, of_group(1, mask_hi)),
                (15, of_group(3, mask_hi)), (12, bias_and_max), (18, of_group(2, mask_hi)),
                (1, per_seq(HEADS - 1, residual)), (22, of_group(0, mask_hi))])

        @block.gpsimd
        def _(pool):
            def inverse_std(it, k):
                p = k // HEADS % GU
                pool.wait_ge(aggr_done, seq(it, k))
                pool.nop(nofuse=True)
                pool.tensor_scalar(var_eps[:, p, :], mv[:, p, :, 1], LN_EPS, None, ALU.add).then_inc(eps_added, 1)
                pool.wait_ge(eps_added, seq(it, k))
                pool.tensor_tensor(rstd[:, p, :], var_eps[:, p, :], neg_half[:, 0:BATCH_TILES], ALU.pow).then_inc(rstd_done, 1)

            def fill_stack(it, k, hg):
                p = k // HEADS % GU
                pool.wait_ge(qk_hi_done, hg_count(it, k, hg))
                wait_free(pool, scores_ready, (it * GU + k // HEADS - 1) * HEADS + 1)
                pool.tensor_tensor(stack[:, p, hg], qk_f[:, hg % 2], qk_hi[:, hg % 2], ALU.subtract).then_inc(stack_ready, 1)

            def shift_tile1(it, k):
                pool.wait_ge(biased_done, unit(it, k))
                pool.tensor_tensor(z[:, k % Z, P:WIDTH], top[:, k % Z, 1:2].to_broadcast([P, WIDTH - P]),
                                   z[:, k % Z, P:WIDTH], ALU.subtract).then_inc(shifted1, 1)

            software_pipeline(pool, BATCHES // GU, U, [
                (29, per_seq(0, inverse_std)), (21, of_group(0, fill_stack)), (17, of_group(2, fill_stack)),
                (16, of_group(3, fill_stack)), (20, of_group(1, fill_stack)), (12, shift_tile1)])

        @block.scalar
        def _(act):
            def copy_xT(it, k):
                act.wait_ge(xn_transposed, seq(it, k))
                act.copy(xnT[:, k // HEADS % GU, :], ps_x).then_inc(xnT_ready, 1)

            def copy_qk(it, k, hg):
                r = hg % 2
                act.wait_ge(qk_projected, hg_count(it, k, hg))
                wait_free(act, stack_ready, hg_count(it, k, hg, 2))
                act.activation(qk_f[:, r, 0, :], ps_qk[:, 0, :], ACT.Identity, bias=w["q_bias"][:, hg:hg + 1], scale=SCALE)
                act.activation(qk_f[:, r, 1, :], ps_qk[:, 1, :], ACT.Identity, bias=w["k_bias"][:, hg:hg + 1]).then_inc(qk_copied, 1)

            def shift_tile0(it, k):
                act.wait_ge(biased_done, unit(it, k))
                act.activation(z[:, k % Z, 0:P], z[:, k % Z, 0:P], ACT.Identity, bias=top[:, k % Z, 0:1], scale=-1.0).then_inc(shifted0, 1)

            def exponent(it, k):
                act.wait_ge(z_transposed, unit(it, k))
                wait_free(act, av_done, fours(it, k - PR))
                act.activation(prob[:, k % PR, :], ps_p[:, k % 2, 0:WIDTH], ACT.Exp, scale=-1.0).then_inc(prob_ready, 1)

            def copy_avT(it, k):
                act.wait_ge(av_done, fours(it, k))
                wait_free(act, heads_transposed, fours(it, k, 2))
                act.copy(avT[:, k // 4 % 2, :], ps_av).then_inc(avT_ready, 1)

            def copy_yT(it, k):
                act.wait_ge(y_transposed, seq(it, k))
                wait_free(act, out_ready, seq(it, k, 1))
                act.copy(yT[:, :], ps_yT).then_inc(yT_ready, 1)

            software_pipeline(act, BATCHES // GU, U, [
                (26, per_seq(0, copy_xT)), (21, of_group(1, copy_qk)), (23, of_group(0, copy_qk)),
                (4, per_seq(HEADS - 1, copy_yT)), (19, of_group(2, copy_qk)), (17, of_group(3, copy_qk)), (9, exponent),
                (11, shift_tile0), (8, per_four(copy_avT))])

        @block.tensor
        def _(pe):
            def transpose_x(it, k):
                pe.wait_ge(xn_ready, seq(it, k))
                wait_free(pe, x_updated, seq(it, k, 3))
                for j in range(BATCH_TILES):
                    last = pe.transpose(ps_x[:, j * P:(j + 1) * P], xn[:, j, :], ident[:, :])
                last.then_inc(xn_transposed, 1)

            def project_v(it, k):
                p = k // HEADS % GU
                pe.wait_ge(xnT_ready, seq(it, k))
                for j in range(BATCH_TILES):
                    last = pe.matmul(ps_v[:, j * C:(j + 1) * C], xnT[:, p, j * P:(j + 1) * P], w["v_w"][:, :], start=True, stop=True)
                last.then_inc(v_projected, 1)

            def project_qk(it, k, hg):
                p = k // HEADS % GU
                if hg == 0:
                    pe.wait_ge(x_split, seq(it, k))
                wait_free(pe, qk_copied, hg_count(it, k, hg, 1))
                for i in range(2):
                    w_hi, w_lo = w["qk_hi"][:, i, hg, :], w["qk_lo"][:, i, hg, :]
                    pe.matmul(ps_qk[:, i, :], w_hi, x_hi[:, p, :], start=True, stop=False)
                    pe.matmul(ps_qk[:, i, :], w_hi, x_lo[:, p, :], start=False, stop=False)
                    last = pe.matmul(ps_qk[:, i, :], w_lo, x_hi[:, p, :], start=False, stop=True)
                last.then_inc(qk_projected, 1)

            def scores(it, k):
                p, h = k // HEADS % GU, k % HEADS
                hg, rows = h // 4, slice(32 * (h % 4), 32 * (h % 4) + 32)
                if h % 4 == 0:
                    pe.wait_ge(stack_ready, hg_count(it, k, hg))
                wait_free(pe, biased_done, unit(it, k, 2))
                q, kk = stack[rows, p, hg, 0, :], stack[rows, p, hg, 1, :]
                pe.matmul(ps_s[:, k % 2, 0:P], q[:, 0:P], kk[:, 0:P], start=True, stop=True)
                pe.matmul(ps_s[:, k % 2, P:WIDTH], q[:, P:T], kk[:, :], start=True, stop=True).then_inc(scores_ready, 1)

            def transpose_z(it, k):
                pe.wait_ge(shifted0, unit(it, k))
                pe.wait_ge(shifted1, unit(it, k))
                wait_free(pe, prob_ready, unit(it, k, 2))
                for j in range(3):
                    last = pe.transpose(ps_p[:, k % 2, j * P:(j + 1) * P], z[:, k % Z, j * P:(j + 1) * P], ident[:, :])
                last.then_inc(z_transposed, 1)

            def attend(it, k):
                p, hg = k // HEADS % GU, k % HEADS // 4
                pe.wait_ge(prob_ready, unit(it, k))
                if hg == 0:
                    pe.wait_ge(v_ready, seq(it, k))
                wait_free(pe, avT_ready, fours(it, k, 1))
                for i in range(4):
                    pr, rows = prob[:, (k - 3 + i) % PR, :], slice(32 * i, 32 * i + 32)
                    pe.matmul(ps_av[rows, :], v_aug[:, p, 0, 4 * hg + i, :], pr[:, 0:T], start=True, stop=False, skip_group_check=True)
                for i in range(4):
                    pr, rows = prob[:, (k - 3 + i) % PR, :], slice(32 * i, 32 * i + 32)
                    last = pe.matmul(ps_av[rows, P:T], v_aug[:, p, 1, 4 * hg + i, :], pr[:, T:], start=False, stop=True, skip_group_check=True)
                last.then_inc(av_done, 1)

            def transpose_heads(it, k):
                pe.wait_ge(avT_ready, fours(it, k))
                wait_free(pe, y_ready, fours(it, k, 1))
                for j in range(BATCH_TILES):
                    last = pe.transpose(ps_heads[:, j].rearrange("p i d -> p (i d)"), avT[:, k // 4 % 2, j * P:(j + 1) * P], ident[:, :])
                last.then_inc(heads_transposed, 1)

            def transpose_y(it, k):
                pe.wait_ge(y_ready, fours(it, k))
                ahead = seq(it, k, -2)
                pe.wait_ge(v_ready, min(ahead, BATCHES) if isinstance(ahead, int) else ahead)
                for j in range(BATCH_TILES):
                    last = pe.transpose(ps_yT[:, j * P:(j + 1) * P], y[:, j, :], ident[:, :])
                last.then_inc(y_transposed, 1)

            def project_out(it, k):
                pe.wait_ge(yT_ready, seq(it, k))
                for j in range(BATCH_TILES):
                    last = pe.matmul(ps_out[:, j * C:(j + 1) * C], yT[:, j * P:(j + 1) * P], w["proj_w"][:, :], start=True, stop=True)
                last.then_inc(out_ready, 1)

            software_pipeline(pe, BATCHES // GU, U, [
                (24, per_seq(0, project_v)), (23, of_group(0, project_qk)), (21, of_group(1, project_qk)),
                (19, of_group(2, project_qk)), (12, scores), (17, of_group(3, project_qk)),
                (1, per_seq(HEADS - 1, project_out)), (26, per_seq(0, transpose_x)), (7, per_four(attend)),
                (9, transpose_z), (6, per_four(transpose_heads)), (4, per_seq(HEADS - 1, transpose_y))])


def bucket_one_hot():
    import math
    import numpy as np
    dist = T - 1 - np.arange(2 * T)
    rp = np.maximum(dist, 0)
    exact = NUM_BUCKETS // 2
    large = exact + (np.log(np.maximum(rp, 1).astype(np.float32) / np.float32(exact)) / np.float32(math.log(MAX_DISTANCE / exact))
                     * np.float32(NUM_BUCKETS - exact)).astype(np.int32)
    bucket = np.where(rp < exact, rp, np.minimum(large, NUM_BUCKETS - 1))
    hot = (np.arange(NUM_BUCKETS)[:, None] == bucket[None]) & (dist >= 0)
    return np.concatenate([hot.astype(np.float32), np.where(dist < 0, MASKED, 0.0).astype(np.float32)[None]])


def attention_weights(nc, ctx):
    def sb(name, shape, dt=F32):
        return ctx.enter_context(nc.sbuf_tensor(name, shape, dt))

    qk_shape = [P, 2, HEAD_GROUPS, P]
    w = dict(qk_w=sb("qk_w", qk_shape), qk_hi=sb("qk_w_hi", qk_shape, F32R), qk_lo=sb("qk_w_lo", qk_shape, F32R), v_w=sb("v_w", [P, C]), proj_w=sb("proj_w", [P, C]),
             qk_bias=sb("qk_bias", [P, 2, HEAD_GROUPS]), lo_slots=sb("lo_slots", [P, 2]), v_bias=sb("v_bias", [P, C]),
             proj_bias=sb("proj_bias", [P, C]), rel_bias=sb("rel_bias", [P, HEADS, T]),
             table=sb("bias_table", [NUM_BUCKETS + 1, HEADS]), hot=sb("bias_hot", [NUM_BUCKETS + 1, 2 * T]), flip=sb("bias_flip", [P, P]),
             by_distance=sb("bias_by_distance", [HEADS, 2 * T]), reversed_rows=sb("bias_reversed", [P, HEADS, T]))
    w["q_bias"], w["k_bias"] = w["qk_bias"][:, 0, :], w["qk_bias"][:, 1, :]
    return w


ATTENTION_LOADS = ("qk_w", "v_w", "proj_w", "qk_bias", "lo_slots", "v_bias", "proj_bias", "flip")


def flat(tensor):
    if len(tensor.shape) == 4:
        return tensor[:, :, :, :].rearrange("p a b c -> p (a b c)")
    if len(tensor.shape) == 3:
        return tensor[:, :, :].rearrange("p a b -> p (a b)")
    return tensor[:, :]


def flip_bias(nc, banks, used, w, weights_loaded, spread):
    hi_done = new_sem(nc, used, "bias_hi_done")
    ps = bank_taker(banks)([P, 8, 512])
    flipped, done, done_v = (new_sem(nc, used, f"bias_{n}") for n in ("flipped", "done", "done_v"))
    chunks = HEADS * T // 512
    rows, out = flat(w["reversed_rows"]), flat(w["rel_bias"])
    with nc.Block() as block:
        @block.scalar
        def _(act):
            act.wait_ge(weights_loaded, len(ATTENTION_LOADS) * 16)
            act.mul(w["q_bias"], w["q_bias"], HEAD_D ** -0.5)
            act.copy(flat(w["qk_hi"]), flat(w["qk_w"])).then_inc(hi_done, 1)
            for n in range(0, chunks, 2):
                act.wait_ge(flipped, n + 1)
                act.copy(out[:, n * 512:(n + 1) * 512], ps[:, n, :]).then_inc(done, 1)

        @block.vector
        def _(dve):
            for n in range(1, chunks, 2):
                dve.wait_ge(flipped, n + 1)
                dve.tensor_copy(out[:, n * 512:(n + 1) * 512], ps[:, n, :]).then_inc(done_v, 1)

        @block.gpsimd
        def _(pool):
            pool.wait_ge(hi_done, 1)
            pool.tensor_tensor(flat(w["qk_lo"]), flat(w["qk_w"]), flat(w["qk_hi"]).bitcast(F32), ALU.subtract)

        @block.tensor
        def _(pe):
            pe.wait_ge(weights_loaded, len(ATTENTION_LOADS) * 16)
            pe.wait_ge(spread, 16)
            for n in range(chunks):
                pe.matmul(ps[:, n, :], w["flip"][:, :], rows[:, n * 512:(n + 1) * 512], start=True, stop=True).then_inc(flipped, 1)


RET_H, RET_D, RET_V = 8, 64, 128
RET_COLUMNS = 2 * RET_H * RET_D + 2 * RET_H * RET_V
VG_JOBS = 8


def retention_phase(nc, tag, banks, used, x_res, ident, neg_half, w):
    GU = 4
    U = GU * RET_H
    RING = 4
    TWINS, PAIRS = 4, 2
    with ExitStack() as ctx:
        def sb(name, shape, dt=F32):
            return ctx.enter_context(nc.sbuf_tensor(f"{tag}_{name}", shape, dt))

        bank = bank_taker(banks)

        def sem(name):
            return new_sem(nc, used, f"{tag}_{name}")

        stats = sb("stats", [P, 2, BATCH_TILES, 6])
        mv = sb("mv", [P, 2, BATCH_TILES, 2])
        var_eps = sb("var_eps", [P, 2, BATCH_TILES])
        rstd = sb("rstd", [P, 2, BATCH_TILES])
        xn = sb("xn", [P, BATCH_TILES, C])
        x_hi, x_lo = sb("x_hi", [P, 2, T], F32R), sb("x_lo", [P, 2, T], F32R)
        twins = sb("twins", [P, TWINS, 2, 2, T])
        turned = sb("turned", [P, 2, 2, T])
        rotated = sb("rotated", [P, PAIRS, 2, T])
        value = sb("value", [P, 2, BATCH_TILES, RET_H, RET_V])
        gate = sb("gate", [P, 2, BATCH_TILES, RET_H, RET_V])
        decayed = sb("decayed", [P, 2, WIDTH])
        head_stats = sb("head_stats", [P, RING, BATCH_TILES, 6])
        head_mv = sb("head_mv", [P, RING, BATCH_TILES, 2])
        head_var = sb("head_var", [P, RING, BATCH_TILES])
        head_rstd = sb("head_rstd", [P, RING, BATCH_TILES])
        normed = sb("normed", [P, 2, BATCH_TILES, RET_V])
        head_shift = sb("head_shift", [P, RING, BATCH_TILES])
        weighted = sb("weighted", [P, RING, BATCH_TILES, RET_V])
        affine = sb("affine", [P, 2, BATCH_TILES, RET_V])
        zT = sb("zT", [P, BATCH_TILES, RET_H, P])
        ps_r, ps_s, ps_o = bank([P, 2, 512]), bank([P, 2, 512]), bank([P, 2, 512])
        ps_g = bank([P, 512])
        ps_f = bank([P, 512])
        ps_x = ps_out = ps_f[:, 0:T]

        stats_done, aggr_done, eps_added, rstd_done, xn_ready = (sem(n) for n in ("stats_done", "aggr_done", "eps_added", "rstd_done", "xn_ready"))
        xn_transposed, x_hi_ready, x_split = sem("xn_transposed"), sem("x_hi_ready"), sem("x_split")
        plain_ready, swapped_even, swapped_odd = sem("plain_ready"), sem("swapped_even"), sem("swapped_odd")
        swapped = (swapped_even, swapped_odd)
        rot_projected, turned_ready, rotated_ready = sem("rot_projected"), sem("turned_ready"), sem("rotated_ready")
        vg_projected, vg_ready = sem("vg_projected"), sem("vg_ready")
        scores_ready, decayed_ready, heads_ready = sem("scores_ready"), sem("decayed_ready"), sem("heads_ready")
        head_stats_done, head_aggr_done, head_eps_added, head_rstd_done = (sem(n) for n in ("head_stats_done", "head_aggr_done", "head_eps_added", "head_rstd_done"))
        head_shift_done = sem("head_shift_done")
        normed_ready, weighted_done, affine_ready, gated_ready = (sem(n) for n in ("normed_ready", "weighted_done", "affine_ready", "gated_ready"))
        z_transposed, zT_ready, out_ready, x_updated = (sem(n) for n in ("z_transposed", "zT_ready", "out_ready", "x_updated"))

        block = ctx.enter_context(nc.Block())

        def unit(it, k, back=0):
            return it * U + (k + 1 - back)

        def seq(it, k, back=0):
            return it * GU + (k // RET_H + 1 - back)

        def wait_free(engine, semaphore, value):
            if not isinstance(value, int) or value > 0:
                engine.wait_ge(semaphore, value)

        def per_seq(at, emit):
            def stage(it, k):
                if k % RET_H == at:
                    emit(it, k)
            return stage

        def pieces(tile, emit):
            def stage(it, k):
                if k % 4 == 3:
                    emit(it, k, tile)
            return stage

        def piece(it, k, tile, back=0):
            return (it * (U // 4) + k // 4) * BATCH_TILES + (tile + 1 - back)

        def x_seq(it, k):
            return x_res[:, bass.ds((it * GU + k // RET_H) * BATCH_TILES, BATCH_TILES), :]

        def swaps(it, k, back=0):
            return (it * (U // 4) + k // 4 + 1 - back) * 4 * 16

        @block.sync
        def _(sync):
            def swap_halves(it, k):
                r, half = k // 2 % TWINS, RET_D // 2
                sync.wait_ge(plain_ready, unit(it, k))
                wait_free(sync, swapped[k // 2 % 2], swaps(it, k, 1))
                for to, at in ((0, half), (half, 0)):
                    for head in range(2):
                        src = slice(head * RET_D + at, head * RET_D + at + half)
                        dst = slice(head * RET_D + to, head * RET_D + to + half)
                        sync.dma_start(twins[dst, r, 1], twins[src, r, 0]).then_inc(swapped[k // 2 % 2], 16)

            def per_pair(emit):
                def stage(it, k):
                    if k % 2 == 1:
                        emit(it, k)
                return stage

            software_pipeline(sync, BATCHES // GU, U, [
                (16, per_pair(swap_halves))])

        @block.vector
        def _(dve):
            dve.nop(nofuse=True).then_inc(x_updated, 1)

            def layernorm(it, k):
                p = k // RET_H % 2
                xs = x_seq(it, k)
                for j in range(BATCH_TILES):
                    last = dve.bn_stats(stats[:, p, j, :], xs[:, j, :])
                last.then_inc(stats_done, 1)
                dve.wait_ge(stats_done, seq(it, k))
                dve.nop(nofuse=True)
                for j in range(BATCH_TILES):
                    last = dve.bn_aggr(mv[:, p, j, :], stats[:, p, j, :])
                last.then_inc(aggr_done, 1)

            def normalise(it, k):
                p = k // RET_H % 2
                xs = x_seq(it, k)
                dve.wait_ge(rstd_done, seq(it, k))
                wait_free(dve, xn_transposed, seq(it, k, 1))
                for j in range(BATCH_TILES):
                    last = dve.tensor_scalar(xn[:, j, :], xs[:, j, :], mv[:, p, j, 0:1], rstd[:, p, j:j + 1],
                                             ALU.subtract, ALU.mult)
                last.then_inc(xn_ready, 1)

            def split_x(it, k):
                p = k // RET_H % 2
                dve.wait_ge(x_hi_ready, seq(it, k))
                dve.tensor_tensor(x_lo[:, p, :], ps_x, x_hi[:, p, :].bitcast(F32), ALU.subtract).then_inc(x_split, 1)

            def turn(it, k):
                dve.wait_ge(swapped[k // 2 % 2], swaps(it, k))
                wait_free(dve, rotated_ready, unit(it, k, 2))
                dve.tensor_tensor(turned[:, k % 2], twins[:, k // 2 % TWINS, :, k % 2, :], w["cos_sin"][:, :, :], ALU.mult).then_inc(turned_ready, 1)

            def decay(it, k):
                dve.wait_ge(scores_ready, unit(it, k))
                wait_free(dve, heads_ready, unit(it, k, 2))
                dve.tensor_tensor(decayed[:, k % 2, :], ps_s[:, k % 2, 0:WIDTH], w["decay"][:, k % RET_H, :],
                                  ALU.mult).then_inc(decayed_ready, 1)

            def head_statistics(it, k):
                r = k % RING
                dve.wait_ge(heads_ready, unit(it, k))
                for j in range(BATCH_TILES):
                    last = dve.bn_stats(head_stats[:, r, j, :], ps_o[:, k % 2, j * RET_V:(j + 1) * RET_V])
                last.then_inc(head_stats_done, 1)
                dve.wait_ge(head_stats_done, unit(it, k))
                dve.nop(nofuse=True)
                for j in range(BATCH_TILES):
                    last = dve.bn_aggr(head_mv[:, r, j, :], head_stats[:, r, j, :])
                last.then_inc(head_aggr_done, 1)

            def shift_of_head(it, k):
                r = k % RING
                dve.wait_ge(head_rstd_done, unit(it, k))
                dve.scalar_tensor_tensor(head_shift[:, r, :], head_mv[:, r, :, 0], -1.0, head_rstd[:, r, :], ALU.mult, ALU.mult).then_inc(head_shift_done, 1)

            def gate_head(it, k):
                p, h = k // RET_H % 2, k % RET_H
                dve.wait_ge(weighted_done, unit(it, k))
                dve.tensor_tensor(affine[:, k % 2], weighted[:, k % RING], w["gn_bias"][:, h, :].unsqueeze(1).to_broadcast([P, BATCH_TILES, RET_V]),
                                  ALU.add).then_inc(affine_ready, 1)
                dve.wait_ge(affine_ready, unit(it, k))
                if h % 4 == 0:
                    dve.wait_ge(vg_ready, (it * GU + k // RET_H) * VG_JOBS + 6 + 2 * (h // 4))
                dve.tensor_tensor(gate[:, p, :, h, :], affine[:, k % 2], gate[:, p, :, h, :], ALU.mult).then_inc(gated_ready, 1)

            def residual(it, k):
                dve.wait_ge(out_ready, seq(it, k, -1))
                xs = x_seq(it, k).rearrange("p j c -> p (j c)")
                dve.tensor_tensor(xs, ps_out, xs, ALU.add).then_inc(x_updated, 1)

            software_pipeline(dve, BATCHES // GU, U, [
                (12, turn), (19, per_seq(0, normalise)), (10, decay), (18, per_seq(0, split_x)),
                (25, per_seq(0, layernorm)), (0, per_seq(RET_H - 1, residual)), (8, shift_of_head), (9, head_statistics),
                (6, gate_head)])

        @block.gpsimd
        def _(pool):
            def inverse_std(it, k):
                p = k // RET_H % 2
                pool.wait_ge(aggr_done, seq(it, k))
                pool.nop(nofuse=True)
                pool.tensor_scalar(var_eps[:, p, :], mv[:, p, :, 1], LN_EPS, None, ALU.add).then_inc(eps_added, 1)
                pool.wait_ge(eps_added, seq(it, k))
                pool.tensor_tensor(rstd[:, p, :], var_eps[:, p, :], neg_half[:, 0:BATCH_TILES], ALU.pow).then_inc(rstd_done, 1)

            def rotate(it, k):
                pool.wait_ge(turned_ready, unit(it, k))
                wait_free(pool, scores_ready, unit(it, k // 2 * 2 + 1, 2 * PAIRS))
                pool.tensor_tensor(rotated[:, k // 2 % PAIRS, k % 2, :], turned[:, k % 2, 0, :], turned[:, k % 2, 1, :],
                                   ALU.add).then_inc(rotated_ready, 1)

            def inverse_head_std(it, k):
                r = k % RING
                pool.wait_ge(head_aggr_done, unit(it, k))
                pool.nop(nofuse=True)
                pool.tensor_scalar(head_var[:, r, :], head_mv[:, r, :, 1], LN_EPS, None, ALU.add).then_inc(head_eps_added, 1)
                pool.wait_ge(head_eps_added, unit(it, k))
                pool.tensor_tensor(head_rstd[:, r, :], head_var[:, r, :], neg_half[:, 0:BATCH_TILES], ALU.pow).then_inc(head_rstd_done, 1)

            def weigh_head(it, k):
                h = k % RET_H
                pool.wait_ge(normed_ready, unit(it, k))
                wait_free(pool, gated_ready, unit(it, k, RING))
                pool.tensor_tensor(weighted[:, k % RING], normed[:, k % 2], w["gn_weight"][:, h, :].unsqueeze(1).to_broadcast([P, BATCH_TILES, RET_V]),
                                   ALU.mult).then_inc(weighted_done, 1)

            software_pipeline(pool, BATCHES // GU, U, [
                (9, inverse_head_std), (25, per_seq(0, inverse_std)), (13, rotate), (8, weigh_head)])

        @block.scalar
        def _(act):
            def copy_x_hi(it, k):
                act.wait_ge(xn_transposed, seq(it, k))
                wait_free(act, vg_projected, (it * GU + k // RET_H - 1) * VG_JOBS)
                act.copy(x_hi[:, k // RET_H % 2, :], ps_x).then_inc(x_hi_ready, 1)

            def copy_plain(it, k):
                act.wait_ge(rot_projected, unit(it, k))
                wait_free(act, turned_ready, unit(it, k // 2 * 2 + 1, 2 * TWINS))
                act.copy(twins[:, k // 2 % TWINS, 0, k % 2, :], ps_r[:, k % 2, 0:T]).then_inc(plain_ready, 1)

            def copy_vg(it, k):
                p, n = k // RET_H % 2, k % RET_H
                tile, half = n % 2, n // 2 % 2
                act.wait_ge(vg_projected, unit(it, k))
                if n < 4:
                    wait_free(act, heads_ready, (it * GU + k // RET_H - 1) * RET_H)
                    dst, func = value, ACT.Copy
                else:
                    wait_free(act, z_transposed, (it * GU + k // RET_H - 1) * 2 * BATCH_TILES + 1)
                    dst, func = gate, ACT.Silu
                act.activation(dst[:, p, tile, 4 * half:4 * half + 4, :].rearrange("p h v -> p (h v)"), ps_g[:, :], func).then_inc(vg_ready, 1)

            def normalise_head(it, k):
                r = k % RING
                act.wait_ge(head_shift_done, unit(it, k))
                wait_free(act, weighted_done, unit(it, k, 2))
                for j in range(BATCH_TILES):
                    last = act.activation(normed[:, k % 2, j, :], ps_o[:, k % 2, j * RET_V:(j + 1) * RET_V], ACT.Identity,
                                          bias=head_shift[:, r, j:j + 1], scale=head_rstd[:, r, j:j + 1])
                last.then_inc(normed_ready, 1)

            def copy_zT(it, k, tile):
                act.wait_ge(z_transposed, piece(it, k, tile, -1))
                half = k // 4 % 2
                if half == 0 and tile == 0:
                    act.wait_ge(out_ready, seq(it, k))
                act.copy(zT[:, tile, 4 * half:4 * half + 4, :].rearrange("p h t -> p (h t)"), ps_f[:, :]).then_inc(zT_ready, 1)

            software_pipeline(act, BATCHES // GU, U, [
                (18, per_seq(0, copy_x_hi)), (16, copy_plain), (8, normalise_head), (12, copy_vg),
                (4, pieces(0, copy_zT)), (3, pieces(1, copy_zT))])

        @block.tensor
        def _(pe):
            pe.nop(nofuse=True).then_inc(z_transposed, 1)
            pe.nop(nofuse=True).then_inc(out_ready, 1)

            def transpose_x(it, k):
                pe.wait_ge(xn_ready, seq(it, k))
                wait_free(pe, zT_ready, (it * GU + k // RET_H - 2) * 4)
                for j in range(BATCH_TILES):
                    last = pe.transpose(ps_x[:, j * P:(j + 1) * P], xn[:, j, :], ident[:, :])
                last.then_inc(xn_transposed, 1)

            def project_rotary(it, k):
                p, n = k // RET_H % 2, k % RET_H
                if n == 0:
                    pe.wait_ge(x_split, seq(it, k))
                wait_free(pe, plain_ready, unit(it, k, 2))
                column = (n % 2) * RET_H * RET_D + n // 2 * P
                w_hi, w_lo = (part[:, column:column + P] for part in w["projections"])
                out = ps_r[:, k % 2, 0:T]
                pe.matmul(out, w_hi, x_hi[:, p, :], start=True, stop=False)
                pe.matmul(out, w_hi, x_lo[:, p, :], start=False, stop=False)
                pe.matmul(out, w_lo, x_hi[:, p, :], start=False, stop=True).then_inc(rot_projected, 1)

            def project_vg(it, k):
                p, n = k // RET_H % 2, k % RET_H
                tile, half = n % 2, n // 2 % 2
                column = 2 * RET_H * RET_D + (n // 4) * RET_H * RET_V + half * 512
                w_hi, w_lo = (part[:, column:column + 512] for part in w["projections"])
                hi, lo = (part[:, p, tile * P:(tile + 1) * P] for part in (x_hi, x_lo))
                wait_free(pe, vg_ready, unit(it, k, 1))
                pe.matmul(ps_g[:, :], hi, w_hi, start=True, stop=False)
                pe.matmul(ps_g[:, :], hi, w_lo, start=False, stop=False)
                pe.matmul(ps_g[:, :], lo, w_hi, start=False, stop=True).then_inc(vg_projected, 1)

            def scores(it, k):
                r, rows = k // 2 % PAIRS, slice(RET_D * (k % 2), RET_D * (k % 2) + RET_D)
                pe.wait_ge(rotated_ready, unit(it, k // 2 * 2 + 1))
                wait_free(pe, decayed_ready, unit(it, k, 2))
                q, kk = rotated[rows, r, 0, :], rotated[rows, r, 1, :]
                pe.matmul(ps_s[:, k % 2, 0:T], kk[:, 0:P], q, start=True, stop=True)
                pe.matmul(ps_s[:, k % 2, T:WIDTH], kk[:, P:T], q[:, P:T], start=True, stop=True).then_inc(scores_ready, 1)

            def retain(it, k):
                p, h = k // RET_H % 2, k % RET_H
                pe.wait_ge(decayed_ready, unit(it, k))
                if h % 4 == 0:
                    pe.wait_ge(vg_ready, (it * GU + k // RET_H) * VG_JOBS + 2 + 2 * (h // 4))
                wait_free(pe, normed_ready, unit(it, k, 2))
                s, out = decayed[:, k % 2, :], ps_o[:, k % 2, :]
                pe.matmul(out[:, 0:RET_V], s[:, 0:P], value[:, p, 0, h, :], start=True, stop=True)
                pe.matmul(out[:, RET_V:2 * RET_V], s[:, P:T], value[:, p, 0, h, :], start=True, stop=False)
                pe.matmul(out[:, RET_V:2 * RET_V], s[:, T:], value[:, p, 1, h, :], start=False, stop=True).then_inc(heads_ready, 1)

            def transpose_z(it, k, tile):
                pe.wait_ge(gated_ready, unit(it, k))
                first = k % RET_H == 3 and tile == 0
                if first:
                    pe.wait_ge(x_updated, seq(it, k))
                else:
                    pe.wait_ge(zT_ready, piece(it, k, tile, 1))
                for i in range(4):
                    last = pe.transpose(ps_f[:, i * P:(i + 1) * P], gate[:, k // RET_H % 2, tile, k % RET_H - 3 + i, :], ident[:, :])
                last.then_inc(z_transposed, 1)

            def project_out(it, k):
                pe.wait_ge(zT_ready, piece(it, k, 1))
                ahead = seq(it, k, -3)
                pe.wait_ge(x_split, min(ahead, BATCHES) if isinstance(ahead, int) else ahead)
                for j in range(BATCH_TILES):
                    for h in range(RET_H):
                        last = pe.matmul(ps_out[:, j * P:(j + 1) * P], zT[:, j, h, :], w["out_w"][:, h, :], start=(h == 0), stop=(h == RET_H - 1))
                last.then_inc(out_ready, 1)

            software_pipeline(pe, BATCHES // GU, U, [
                (10, scores), (18, per_seq(0, transpose_x)), (2, pieces(1, transpose_z)), (17, project_rotary),
                (0, per_seq(RET_H - 1, project_out)), (9, retain), (3, pieces(0, transpose_z)), (12, project_vg)])


def retention_tables():
    import numpy as np
    f = np.float32
    inv_freq = f(1.0) / f(10000.0) ** (np.arange(0, RET_D, 2, dtype=f) / f(RET_D))
    freqs = np.arange(T, dtype=f)[:, None] * inv_freq[None]
    emb = np.concatenate([freqs, freqs], axis=1).T
    sign = np.where(np.arange(RET_D) < RET_D // 2, f(-1), f(1))[:, None]
    cos_sin = np.concatenate([np.tile(np.cos(emb), (2, 1)), np.tile(np.sin(emb) * sign, (2, 1))], axis=1)
    log_gamma = np.log2(f(1.0) - np.exp2(f(-5.0) - np.arange(RET_H, dtype=f)))
    n = np.arange(T, dtype=f)
    rel = n[None] - n[:, None]
    full = np.where(rel[None] >= 0, np.exp2(np.maximum(rel, 0)[None] * log_gamma[:, None, None]), f(0)) * f(RET_D ** -0.5)
    decay = np.concatenate([full[:, :P, :], full[:, P:, P:]], axis=2)
    return cos_sin.astype(f), decay.transpose(1, 0, 2).reshape(P, RET_H * WIDTH).astype(f)


def retention_weights(nc, ctx):
    def sb(name, shape, dt=F32):
        return ctx.enter_context(nc.sbuf_tensor(name, shape, dt))

    return dict(projections=(sb("ret_hi", [P, RET_COLUMNS], F32R), sb("ret_lo", [P, RET_COLUMNS], F32R)), out_w=sb("ret_out_w", [P, RET_H, C]),
                cos_sin=sb("ret_cos_sin", [P, 2, T]), decay=sb("ret_decay", [P, RET_H, WIDTH]),
                gn_weight=sb("ret_gn_weight", [P, RET_H, RET_V]), gn_bias=sb("ret_gn_bias", [P, RET_H, RET_V]))


RETENTION_LOADS = ("out_w", "cos_sin", "decay", "gn_weight", "gn_bias")


def weight_split(nc, used, tag, stage, hi, lo, loaded, parts):
    hi_done = new_sem(nc, used, f"{tag}_hi_done")
    width = stage.shape[1] // parts

    def on_scalar(act, i):
        at = slice(i * width, (i + 1) * width)
        act.wait_ge(loaded[i], 16)
        act.copy(hi[:, at], stage[:, at]).then_inc(hi_done, 1)

    def on_pool(pool, i):
        at = slice(i * width, (i + 1) * width)
        pool.wait_ge(hi_done, i + 1)
        pool.tensor_tensor(lo[:, at], stage[:, at], hi[:, at].bitcast(F32), ALU.subtract)

    return on_scalar, on_pool


def in_last_iteration(engine, iterations, parts, emit):
    def stage(it, k):
        if isinstance(it, int) and it == iterations - 1 and k < parts:
            emit(engine, k)
    return stage


MOE_COLUMNS = 3 * MOE_UNITS * MOE_F
MOE_PARTS, RET_PARTS = 4, 16


def build(nc, d, out):
    with ExitStack() as ctx:
        def sb(name, shape, dt=F32):
            return ctx.enter_context(nc.sbuf_tensor(name, shape, dt))

        def sem(name):
            return ctx.enter_context(nc.semaphore(name))

        banks = ctx.enter_context(nc.psum_tensor("banks", [P, 8, 512], F32))
        x_res = sb("x_res", [P, TILES, C])
        ident, ident_bf = sb("ident", [P, P]), sb("ident_bf", [P, P], BF16)
        neg_half = sb("neg_half", [P, 8])
        ffn_w = sb("ffn_w", [P, C + LORA_E + LORA_R])
        lora_rows = sb("lora_rows", [LORA_ROWS + 1, C])
        lora_router_b = sb("lora_router_b", [P, GROUP, LORA_E])
        moe_hi, moe_lo = sb("moe_hi", [P, MOE_COLUMNS], F32R), sb("moe_lo", [P, MOE_COLUMNS], F32R)
        router, router_hi, router_lo = sb("router", [P, MOE_E]), sb("router_hi", [P, MOE_E], F32R), sb("router_lo", [P, MOE_E], F32R)
        moe_bias = sb("moe_bias", [P, GROUP, MOE_E])
        before = sb("before", [P, GROUP * MOE_G, MOE_G])
        select = sb("select", [3 * MOE_E, MOE_E, P], BF16)

        x_first, x_rest, first_loaded, out_stored = sem("x_first"), sem("x_rest"), sem("first_loaded"), sem("out_stored")
        table_loaded, distances_ready, distances_copied = sem("table_loaded"), sem("distances_ready"), sem("distances_copied")
        distances_stored, bias_spread, attn_loaded = sem("distances_stored"), sem("bias_spread"), sem("attn_loaded")
        moe_loaded, ret_loaded, router_split = sem("moe_loaded"), sem("ret_loaded"), sem("router_split")
        moe_part_loaded = [sem(f"moe_part_loaded{i}") for i in range(MOE_PARTS)]
        ret_part_loaded = [sem(f"ret_part_loaded{i}") for i in range(RET_PARTS)]
        used = []
        x_rows = d["x"].rearrange("(t p) c -> p t c", p=P)
        out_rows = out.rearrange("(t p) c -> p t c", p=P)
        lora = dict(base_T=ffn_w[:, 0:C], router_a=ffn_w[:, C:], lora_rows=lora_rows[:, :], router_b=lora_router_b)
        moe = dict(up_down=(moe_hi, moe_lo), router=(router_hi[:, :], router_lo[:, :]), bias=moe_bias, before=before, select=select)

        with ExitStack() as attn_ctx:
            attn = attention_weights(nc, attn_ctx)

            with nc.Block() as block:
                @block.sync
                def _(sync):
                    first = FIRST_GROUPS * GROUP
                    sync.dma_start(x_res[:, 0:first, :], x_rows[:, 0:first, :]).then_inc(x_first, 16)

                @block.gpsimd
                def _(pool):
                    pool.memset(neg_half[:, :], -0.5)

                @block.scalar
                def _(act):
                    act.dma_start(attn["table"][:, :], d["bias_table"]).then_inc(table_loaded, 16)
                    act.dma_start(attn["hot"][:, :], d["bias_hot"]).then_inc(table_loaded, 16)
                    act.dma_start(ident[:, :], d["ident"]).then_inc(first_loaded, 16)
                    act.dma_start(lora_rows[:, :], d["lora_rows"]).then_inc(first_loaded, 16)
                    act.dma_start(ffn_w[:, :], d["ffn_w"]).then_inc(first_loaded, 16)
                    act.dma_start(flat(lora_router_b), d["lora_router_b"]).then_inc(first_loaded, 16)
                    first = FIRST_GROUPS * GROUP
                    act.dma_start(x_res[:, first:, :], x_rows[:, first:, :]).then_inc(x_rest, 16)
                    act.wait_ge(distances_ready, 1)
                    act.copy(attn["by_distance"][:, :], banks[0:HEADS, 0, :]).then_inc(distances_copied, 1)
                    act.wait_ge(first_loaded, 64)
                    act.mul(lora_rows[0:LORA_ROWS, :], lora_rows[0:LORA_ROWS, :], LORA_SCALING)

                @block.tensor
                def _(pe):
                    pe.wait_ge(table_loaded, 32)
                    pe.matmul(banks[0:HEADS, 0, :], attn["table"][:, :], attn["hot"][:, :], start=True, stop=True).then_inc(distances_ready, 1)

            def load_attention(sync, x_updated):
                scratch = d["scratch"]
                sync.wait_ge(distances_copied, 1)
                sync.dma_start(scratch, attn["by_distance"][:, :]).then_inc(distances_stored, 16)
                for name in ATTENTION_LOADS:
                    sync.dma_start(flat(attn[name]), d[name]).then_inc(attn_loaded, 16)
                sync.wait_ge(distances_stored, 16)
                sync.dma_start(attn["reversed_rows"][:, :, :],
                               bass.AP(scratch.tensor, scratch.offset, [[1, P], [2 * T, HEADS], [1, T]])).then_inc(bias_spread, 16)

            ffn_lora_phase(nc, "ffn1", banks, used, x_res, ident, neg_half, lora, load_attention, x_first, x_rest)

            flip_bias(nc, banks, used, attn, attn_loaded, bias_spread)
            attention_phase(nc, "attn", banks, used, x_res, ident, neg_half, attn)

        with ExitStack() as stage_ctx:
            stage = stage_ctx.enter_context(nc.sbuf_tensor("moe_stage", [P, MOE_COLUMNS], F32))
            select_stage = stage_ctx.enter_context(nc.sbuf_tensor("select_stage", [3 * MOE_E, MOE_E * P], F32))

            def load_moe(sync, x_updated):
                for dst, name in ((router[:, :], "moe_router"), (select_stage[:, :], "moe_select"), (flat(moe_bias), "moe_bias"),
                                  (flat(before), "moe_before")):
                    sync.dma_start(dst, d[name]).then_inc(moe_loaded, 16)
                for i in range(MOE_PARTS):
                    at = slice(i * MOE_COLUMNS // MOE_PARTS, (i + 1) * MOE_COLUMNS // MOE_PARTS)
                    sync.dma_start(stage[:, at], d["moe_w"][:, at]).then_inc(moe_part_loaded[i], 16)

            split_hi, split_lo = weight_split(nc, used, "moe", stage, moe_hi, moe_lo, moe_part_loaded, MOE_PARTS)

            def split_on_scalar(act, i):
                if i == 0:
                    act.wait_ge(moe_loaded, 4 * 16)
                    act.copy(router_hi[:, :], router[:, :]).then_inc(router_split, 1)
                    act.copy(ident_bf[:, :], ident[:, :])
                    act.copy(flat(select), select_stage[:, :])
                split_hi(act, i)

            def split_on_pool(pool, i):
                if i == 0:
                    pool.wait_ge(router_split, 1)
                    pool.tensor_tensor(router_lo[:, :], router[:, :], router_hi[:, :].bitcast(F32), ALU.subtract)
                split_lo(pool, i)

            ffn_lora_phase(nc, "ffn2", banks, used, x_res, ident, neg_half, lora, load_moe, split=(split_on_scalar, split_on_pool, MOE_PARTS))

        retire(nc, used)

        with ExitStack() as ret_ctx:
            ret = retention_weights(nc, ret_ctx)
            with ExitStack() as stage_ctx:
                stage = stage_ctx.enter_context(nc.sbuf_tensor("ret_stage", [P, RET_COLUMNS], F32))

                def load_retention(sync, x_updated):
                    for i in range(RET_PARTS):
                        at = slice(i * RET_COLUMNS // RET_PARTS, (i + 1) * RET_COLUMNS // RET_PARTS)
                        sync.dma_start(stage[:, at], d["ret_w"][:, at]).then_inc(ret_part_loaded[i], 16)
                    for name in RETENTION_LOADS:
                        sync.dma_start(flat(ret[name]), d["ret_" + name]).then_inc(ret_loaded, 16)
                    sync.wait_ge(ret_loaded, len(RETENTION_LOADS) * 16)

                split_hi, split_lo = weight_split(nc, used, "ret", stage, *ret["projections"], ret_part_loaded, RET_PARTS)
                moe_phase(nc, "moe1", banks, used, x_res, ident, ident_bf, neg_half, moe, load_retention, (split_hi, split_lo, RET_PARTS))

            retention_phase(nc, "ret", banks, used, x_res, ident, neg_half, ret)

        def store_x(sync, x_updated):
            for g in range(GROUPS):
                sync.wait_ge(x_updated, g + 2)
                rows = slice(g * GROUP, (g + 1) * GROUP)
                sync.dma_start(out_rows[:, rows, :], x_res[:, rows, :]).then_inc(out_stored, 16)
            sync.wait_ge(out_stored, GROUPS * 16)

        moe_phase(nc, "moe2", banks, used, x_res, ident, ident_bf, neg_half, moe, store_x)

def kernel(**inputs):
    import numpy as np
    import concourse.bacc as bacc
    from concourse.bass_utils import run_bass_kernel_spmd

    def arr(name):
        return np.asarray(inputs[name])

    host = {
        "x": arr("L0_attn_x").reshape(TILES * P, C),
        "ident": np.eye(P, dtype=np.float32),
        "ffn_w": np.concatenate([arr("L0_ffn_base_w").T, arr("L0_ffn_router_w").T, arr("L0_ffn_lora_A")], axis=1),
        "lora_rows": np.concatenate([arr("L0_ffn_lora_B").reshape(LORA_ROWS, C), arr("L0_ffn_base_b")[None]], axis=0),
        "lora_router_b": np.tile(arr("L0_ffn_router_b")[None], (P, GROUP)),
    }
    blocks = [arr("L1_ffn_sh_gate_w"), arr("L1_ffn_gate_w").transpose(1, 0, 2).reshape(C, MOE_E * MOE_F),
              arr("L1_ffn_sh_up_w"), arr("L1_ffn_up_w").transpose(1, 0, 2).reshape(C, MOE_E * MOE_F),
              arr("L1_ffn_sh_down_w").reshape(MOE_SHARED, MOE_F, C).transpose(1, 0, 2).reshape(MOE_F, MOE_SHARED * C),
              arr("L1_ffn_down_w").transpose(1, 0, 2).reshape(MOE_F, MOE_E * C)]
    host["moe_w"] = np.concatenate(blocks, axis=1)
    host["moe_router"] = arr("L1_ffn_router_w").T
    host["moe_bias"] = np.tile(arr("L1_ffn_bias")[None], (P, GROUP))
    host["moe_before"] = np.tile(np.tril(np.ones((MOE_G, MOE_G), np.float32), -1).reshape(1, -1), (P, GROUP))
    host["moe_select"] = np.tile(np.repeat(np.eye(MOE_E, dtype=np.float32), P, axis=1), (3, 1))
    wa, ba = arr("L0_attn_W_attn"), arr("L0_attn_b_attn")

    def stacked(a):
        a = a.reshape(-1, HEAD_GROUPS, 4, 1, HEAD_D)
        return np.tile(a, (1, 1, 1, SLOTS, 1)).reshape(a.shape[0], HEAD_GROUPS * P)

    host["qk_w"] = np.concatenate([stacked(wa[:, 0:C]), stacked(wa[:, C:2 * C])], axis=1)
    host["v_w"] = wa[:, 2 * C:]
    host["qk_bias"] = np.concatenate([stacked(ba[None, i * C:(i + 1) * C]).reshape(HEAD_GROUPS, P).T for i in range(2)], axis=1)
    slot = np.arange(P) // HEAD_D % SLOTS
    host["lo_slots"] = np.stack([slot // 2, slot % 2], axis=1).astype(np.float32)
    host["v_bias"] = np.tile(ba[None, 2 * C:], (P, 1))
    host["proj_w"], host["proj_bias"] = arr("L0_attn_W_proj"), np.tile(arr("L0_attn_b_proj")[None], (P, 1))
    host["bias_table"] = np.concatenate([arr("L0_attn_bias_table"), np.ones((1, HEADS), np.float32)])
    host["bias_hot"] = bucket_one_hot()
    host["flip"] = np.eye(P, dtype=np.float32)[::-1]
    host["ret_w"] = np.concatenate([arr("L1_attn_Wq"), arr("L1_attn_Wk"), arr("L1_attn_Wv"), arr("L1_attn_Wg")]).T
    host["ret_out_w"] = arr("L1_attn_Wo").reshape(C, RET_H, RET_V).transpose(2, 1, 0).reshape(RET_V, RET_H * C)
    host["ret_gn_weight"], host["ret_gn_bias"] = (np.tile(arr(n)[None], (P, 1)) for n in ("L1_attn_gn_weight", "L1_attn_gn_bias"))
    host["ret_cos_sin"], host["ret_decay"] = retention_tables()
    host = {k: np.ascontiguousarray(v) for k, v in host.items()}
    nc = bacc.Bacc("TRN2", target_bir_lowering=False, num_devices=1)
    dram = {k: nc.dram_tensor(f"in_{k}", list(v.shape), F32, kind="ExternalInput").ap() for k, v in host.items()}
    out = nc.dram_tensor("out", [TILES * P, C], F32, kind="ExternalOutput").ap()
    dram["scratch"] = nc.dram_tensor("scratch", [HEADS, 2 * T], F32).ap()
    build(nc, dram, out)
    r = run_bass_kernel_spmd(nc, [{f"in_{k}": v for k, v in host.items()}], core_ids=[0])
    return r.results[0]["out"].reshape(BATCHES, T, C)
```
